# Optimizing a Trainium2 kernel written in Bass

```python
import numpy as np
import jax
import jax.numpy as jnp

def _softmax(x, axis=-1):
    return jax.nn.softmax(x, axis=axis)

def _gelu(x):
    return jax.nn.gelu(x, approximate=True)

def _silu(x):
    return jax.nn.silu(x)

def _sigmoid(x):
    return jax.nn.sigmoid(x)

def _layernorm(x, axis=-1, eps=1e-05):
    m = jnp.mean(x, axis=axis, keepdims=True)
    v = jnp.var(x, axis=axis, keepdims=True)
    return (x - m) / jnp.sqrt(v + eps)

def _scatter_add(tgt, idx, src, axis=0):
    return tgt.at[idx].add(src)

def _segment_sum(src, seg, n):
    return jax.ops.segment_sum(src, seg, n)
kernel_name = 'mk_prb_d2_jaxref_r8_3f9177'

def setup_inputs(seed: int=0):
    np.random.seed(seed)
    _w = jnp.asarray

    def _L0_attn_setup():
        import jax, jax.numpy as jnp
        import numpy as np
        import math
        N_HEAD = 16
        HEAD_DIM = 64
        N_EMBD = 128
        MIN_CTX = 32
        FULL_CTX = 128

        def _pruning_ratio(T):
            if T < MIN_CTX:
                return 1.0
            if T >= FULL_CTX:
                return 0.2
            progress = (T - MIN_CTX) / (FULL_CTX - MIN_CTX)
            return 0.5 - 0.3 * progress
        key = jax.random.key(seed)
        k1, k2, k3, k4, k5 = jax.random.split(key, 5)
        B, T = (1, 256)
        x = jax.random.normal(k1, (B, T, N_EMBD), dtype=jnp.float32)
        W_attn = jax.random.normal(k2, (3 * N_HEAD * HEAD_DIM, N_EMBD), dtype=jnp.float32) * 0.02
        b_attn = jnp.zeros((3 * N_HEAD * HEAD_DIM,), dtype=jnp.float32)
        W_proj = jax.random.normal(k3, (N_EMBD, N_HEAD * HEAD_DIM), dtype=jnp.float32) * 0.02
        b_proj = jnp.zeros((N_EMBD,), dtype=jnp.float32)
        return {'x': x, 'W_attn': W_attn, 'b_attn': b_attn, 'W_proj': W_proj, 'b_proj': b_proj}
    _L0_attn_in = _L0_attn_setup()

    def _L0_ffn_setup():
        import jax, jax.numpy as jnp
        import numpy as np
        key = jax.random.key(seed)
        kx, kw = jax.random.split(key)
        x = jax.random.normal(kx, (32, 512, 128), dtype=jnp.float32)
        weight = jax.random.normal(kw, (128, 128), dtype=jnp.float32) * 0.01
        return {'x': x, 'weight': weight}
    _L0_ffn_in = _L0_ffn_setup()

    def _L1_attn_setup():
        import jax, jax.numpy as jnp
        import numpy as np
        EPS = 1e-05
        H, N, F = (128, 16, 512)

        def layernorm(x, g, b):
            mu = jnp.mean(x, axis=-1, keepdims=True)
            var = jnp.mean(jnp.square(x - mu), axis=-1, keepdims=True)
            return (x - mu) * jax.lax.rsqrt(var + EPS) * g + b

        def _selective_ssm(xn, delta, Bm, Cm, A, D):
            Bsz = xn.shape[0]
            xs = (jnp.moveaxis(delta, 1, 0), jnp.moveaxis(Bm, 1, 0), jnp.moveaxis(Cm, 1, 0), jnp.moveaxis(xn, 1, 0))

            def step(h, t):
                d_t, b_t, c_t, x_t = t
                dA = jnp.exp(d_t[:, :, None] * A)
                dBx = d_t[:, :, None] * b_t[:, None, :] * x_t[:, :, None]
                h = dA * h + dBx
                y = jnp.einsum('bhn,bn->bh', h, c_t)
                return (h, y)
            h0 = jnp.zeros((Bsz, H, N), xn.dtype)
            _, ys = jax.lax.scan(step, h0, xs)
            y = jnp.moveaxis(ys, 0, 1)
            return y + D * xn
        key = jax.random.key(seed)
        ks = jax.random.split(key, 12)
        B, L = (2, 256)
        s = lambda fan_in: 1.0 / np.sqrt(fan_in)
        inp = {'x': jax.random.normal(ks[0], (B, L, H), jnp.float32), 'ln1_g': jnp.ones((H,), jnp.float32), 'ln1_b': jnp.zeros((H,), jnp.float32), 'Wd': jax.random.uniform(ks[1], (H, H), jnp.float32, -s(H), s(H)), 'bd': jnp.zeros((H,), jnp.float32), 'Wbc': jax.random.uniform(ks[2], (2 * N, H), jnp.float32, -s(H), s(H)), 'bbc': jnp.zeros((2 * N,), jnp.float32), 'A_log': jnp.log(jnp.tile(jnp.arange(1, N + 1, dtype=jnp.float32), (H, 1))), 'D': jnp.ones((H,), jnp.float32), 'ln2_g': jnp.ones((H,), jnp.float32), 'ln2_b': jnp.zeros((H,), jnp.float32), 'W1': jax.random.uniform(ks[3], (F, H), jnp.float32, -s(H), s(H)), 'b1': jnp.zeros((F,), jnp.float32), 'W2': jax.random.uniform(ks[4], (H, F), jnp.float32, -s(F), s(F)), 'b2': jnp.zeros((H,), jnp.float32)}
        return inp
    _L1_attn_in = _L1_attn_setup()

    def _L1_ffn_setup():
        import jax, jax.numpy as jnp
        import numpy as np
        B, S, D, F, E, NS, K = (2, 128, 128, 512, 8, 8, 2)
        FS = F // NS
        key = jax.random.key(seed)
        ks = jax.random.split(key, 8)
        scale = 0.02
        return {'hidden_states': jax.random.normal(ks[0], (B, S, D), jnp.float32), 'gate_W': jax.random.normal(ks[1], (E, D), jnp.float32) * scale, 'w1_e': jax.random.normal(ks[2], (E, D, F), jnp.float32) * scale, 'w3_e': jax.random.normal(ks[3], (E, D, F), jnp.float32) * scale, 'w2_e': jax.random.normal(ks[4], (E, F, D), jnp.float32) * scale, 'w1_s': jax.random.normal(ks[5], (NS, D, FS), jnp.float32) * scale, 'w3_s': jax.random.normal(ks[6], (NS, D, FS), jnp.float32) * scale, 'w2_s': jax.random.normal(ks[7], (NS, FS, D), jnp.float32) * scale}
    _L1_ffn_in = _L1_ffn_setup()
    _d = {'L0_attn_x': _L0_attn_in['x'], 'L0_attn_W_attn': _L0_attn_in['W_attn'], 'L0_attn_b_attn': _L0_attn_in['b_attn'], 'L0_attn_W_proj': _L0_attn_in['W_proj'], 'L0_attn_b_proj': _L0_attn_in['b_proj'], 'L0_ffn_weight': _L0_ffn_in['weight'], 'L1_attn_ln1_g': _L1_attn_in['ln1_g'], 'L1_attn_ln1_b': _L1_attn_in['ln1_b'], 'L1_attn_Wd': _L1_attn_in['Wd'], 'L1_attn_bd': _L1_attn_in['bd'], 'L1_attn_Wbc': _L1_attn_in['Wbc'], 'L1_attn_bbc': _L1_attn_in['bbc'], 'L1_attn_A_log': _L1_attn_in['A_log'], 'L1_attn_D': _L1_attn_in['D'], 'L1_attn_ln2_g': _L1_attn_in['ln2_g'], 'L1_attn_ln2_b': _L1_attn_in['ln2_b'], 'L1_attn_W1': _L1_attn_in['W1'], 'L1_attn_b1': _L1_attn_in['b1'], 'L1_attn_W2': _L1_attn_in['W2'], 'L1_attn_b2': _L1_attn_in['b2'], 'L1_ffn_gate_W': _L1_ffn_in['gate_W'], 'L1_ffn_w1_e': _L1_ffn_in['w1_e'], 'L1_ffn_w3_e': _L1_ffn_in['w3_e'], 'L1_ffn_w2_e': _L1_ffn_in['w2_e'], 'L1_ffn_w1_s': _L1_ffn_in['w1_s'], 'L1_ffn_w3_s': _L1_ffn_in['w3_s'], 'L1_ffn_w2_s': _L1_ffn_in['w2_s']}
    _x0 = _d['L0_attn_x']
    _d['L0_attn_x'] = jax.random.normal(jax.random.fold_in(jax.random.key(seed), 1), (1, 2048, 128), dtype=_x0.dtype)
    del _x0
    return _d

def reference(L0_attn_x, L0_attn_W_attn, L0_attn_b_attn, L0_attn_W_proj, L0_attn_b_proj, L0_ffn_weight, L1_attn_ln1_g, L1_attn_ln1_b, L1_attn_Wd, L1_attn_bd, L1_attn_Wbc, L1_attn_bbc, L1_attn_A_log, L1_attn_D, L1_attn_ln2_g, L1_attn_ln2_b, L1_attn_W1, L1_attn_b1, L1_attn_W2, L1_attn_b2, L1_ffn_gate_W, L1_ffn_w1_e, L1_ffn_w3_e, L1_ffn_w2_e, L1_ffn_w1_s, L1_ffn_w3_s, L1_ffn_w2_s):

    def _L0_attn_ref(x, W_attn, b_attn, W_proj, b_proj):
        import jax, jax.numpy as jnp
        import numpy as np
        import math
        N_HEAD = 16
        HEAD_DIM = 64
        N_EMBD = 128
        MIN_CTX = 32
        FULL_CTX = 128

        def _pruning_ratio(T):
            if T < MIN_CTX:
                return 1.0
            if T >= FULL_CTX:
                return 0.2
            progress = (T - MIN_CTX) / (FULL_CTX - MIN_CTX)
            return 0.5 - 0.3 * progress
        B, T, C = x.shape
        H, hd = (N_HEAD, HEAD_DIM)
        qkv = x @ W_attn.T + b_attn
        q, k, v = jnp.split(qkv, 3, axis=-1)
        q = q.reshape(B, T, H, hd).transpose(0, 2, 1, 3)
        k = k.reshape(B, T, H, hd).transpose(0, 2, 1, 3)
        v = v.reshape(B, T, H, hd).transpose(0, 2, 1, 3)
        att = jnp.einsum('bhqd,bhkd->bhqk', q, k) * (1.0 / math.sqrt(hd))
        i = jnp.arange(T)
        causal = i[None, :] <= i[:, None]
        neg_inf = jnp.float32(-jnp.inf)
        att = jnp.where(causal[None, None], att, neg_inf)
        S = jnp.maximum(att[:, 0], 0.0)
        keepS = (i[None, :] != 0) & (i[:, None] != i[None, :])
        S = jnp.where(keepS[None], S, 0.0)
        S_shifted = jnp.roll(S, 1, axis=-2).at[:, 0, :].set(0.0)
        FF = jnp.cumsum(S_shifted, axis=-2)
        att = att - FF[:, None]
        ratio = _pruning_ratio(T)
        memory_budget = max(1, int(T * ratio))
        if ratio < 1.0:
            FF_mod = jnp.where(causal[None], FF, jnp.inf)
            sorted_idx = jnp.argsort(FF_mod, axis=-1)
            eff_k = jnp.minimum(memory_budget - 1, i + 1)
            sel = i[None, :] < eff_k[:, None]
            keep = jnp.zeros((B, T, T), dtype=bool)
            keep = keep.at[jnp.arange(B)[:, None, None], i[None, :, None], sorted_idx].set(jnp.broadcast_to(sel[None], (B, T, T)))
            keep = keep | jnp.eye(T, dtype=bool)[None]
            att = jnp.where(keep[:, None], att, neg_inf)
        y = jax.nn.softmax(att, axis=-1) @ v
        y = y.transpose(0, 2, 1, 3).reshape(B, T, H * hd)
        y = y @ W_proj.T + b_proj
        return y

    def _L0_ffn_ref(x, weight):
        import jax, jax.numpy as jnp
        import numpy as np
        b_weight = jnp.sign(weight)
        return jnp.einsum('bsi,oi->bso', x, b_weight)

    def _L1_attn_ref(x, ln1_g, ln1_b, Wd, bd, Wbc, bbc, A_log, D, ln2_g, ln2_b, W1, b1, W2, b2):
        import jax, jax.numpy as jnp
        import numpy as np
        EPS = 1e-05
        H, N, F = (128, 16, 512)

        def layernorm(x, g, b):
            mu = jnp.mean(x, axis=-1, keepdims=True)
            var = jnp.mean(jnp.square(x - mu), axis=-1, keepdims=True)
            return (x - mu) * jax.lax.rsqrt(var + EPS) * g + b

        def _selective_ssm(xn, delta, Bm, Cm, A, D):
            Bsz = xn.shape[0]
            xs = (jnp.moveaxis(delta, 1, 0), jnp.moveaxis(Bm, 1, 0), jnp.moveaxis(Cm, 1, 0), jnp.moveaxis(xn, 1, 0))

            def step(h, t):
                d_t, b_t, c_t, x_t = t
                dA = jnp.exp(d_t[:, :, None] * A)
                dBx = d_t[:, :, None] * b_t[:, None, :] * x_t[:, :, None]
                h = dA * h + dBx
                y = jnp.einsum('bhn,bn->bh', h, c_t)
                return (h, y)
            h0 = jnp.zeros((Bsz, H, N), xn.dtype)
            _, ys = jax.lax.scan(step, h0, xs)
            y = jnp.moveaxis(ys, 0, 1)
            return y + D * xn
        xn = layernorm(x, ln1_g, ln1_b)
        delta = jax.nn.softplus(xn @ Wd.T + bd)
        bc = xn @ Wbc.T + bbc
        Bm, Cm = (bc[..., :N], bc[..., N:])
        A = -jnp.exp(A_log)
        ssm_out = x + _selective_ssm(xn, delta, Bm, Cm, A, D)
        normed = layernorm(ssm_out, ln2_g, ln2_b)
        hff = jax.nn.gelu(normed @ W1.T + b1, approximate=False)
        ffn_out = hff @ W2.T + b2
        return ffn_out + ssm_out

    def _L1_ffn_ref(hidden_states, gate_W, w1_e, w3_e, w2_e, w1_s, w3_s, w2_s):
        import jax, jax.numpy as jnp
        import numpy as np
        B, S, D, F, E, NS, K = (2, 128, 128, 512, 8, 8, 2)
        FS = F // NS
        b, s, d = hidden_states.shape
        e = gate_W.shape[0]
        flat = hidden_states.reshape(-1, d)
        T = flat.shape[0]
        logits = (flat @ gate_W.T).astype(jnp.float32)
        probs = jax.nn.softmax(logits, axis=-1)
        top_v, top_i = jax.lax.top_k(probs, K)
        gates = jnp.zeros((T, e), probs.dtype).at[jnp.arange(T)[:, None], top_i].set(top_v)
        g = jax.nn.silu(jnp.einsum('td,edf->etf', flat, w1_e))
        u = jnp.einsum('td,edf->etf', flat, w3_e)
        out_e = jnp.einsum('etf,efd->etd', g * u, w2_e)
        routed = jnp.einsum('te,etd->td', gates, out_e).reshape(b, s, d)
        gs = jax.nn.silu(jnp.einsum('bsd,ndf->nbsf', hidden_states, w1_s))
        us = jnp.einsum('bsd,ndf->nbsf', hidden_states, w3_s)
        shared = jnp.einsum('nbsf,nfd->bsd', gs * us, w2_s) / w1_s.shape[0]
        alpha = 0.5
        return alpha * shared + (1.0 - alpha) * routed
    x = L0_attn_x
    xn = _layernorm(x, axis=-1)
    x = x + _L0_attn_ref(xn, L0_attn_W_attn, L0_attn_b_attn, L0_attn_W_proj, L0_attn_b_proj) + _L0_ffn_ref(xn, L0_ffn_weight)
    xn = _layernorm(x, axis=-1)
    x = x + _L1_attn_ref(xn, L1_attn_ln1_g, L1_attn_ln1_b, L1_attn_Wd, L1_attn_bd, L1_attn_Wbc, L1_attn_bbc, L1_attn_A_log, L1_attn_D, L1_attn_ln2_g, L1_attn_ln2_b, L1_attn_W1, L1_attn_b1, L1_attn_W2, L1_attn_b2) + _L1_ffn_ref(xn, L1_ffn_gate_W, L1_ffn_w1_e, L1_ffn_w3_e, L1_ffn_w2_e, L1_ffn_w1_s, L1_ffn_w3_s, L1_ffn_w2_s)
    return x

_drawn_inputs = setup_inputs


def setup_inputs(seed=0):
    import zlib

    import numpy as np

    out = dict(_drawn_inputs(seed))
    spreads = {'L0_attn_b_attn': (0.0, 0.8),
     'L0_attn_b_proj': (0.0, 0.8),
     'L1_attn_ln1_g': (1.0, 0.2),
     'L1_attn_ln1_b': (0.0, 0.453),
     'L1_attn_bd': (0.0, 0.8),
     'L1_attn_bbc': (0.0, 0.384),
     'L1_attn_D': (1.0, 0.6),
     'L1_attn_ln2_g': (1.0, 0.6),
     'L1_attn_ln2_b': (0.0, 0.8),
     'L1_attn_b1': (0.0, 0.8),
     'L1_attn_b2': (0.0, 0.8)}
    factors = {'L0_attn_W_attn': 8.0,
     'L0_attn_W_proj': 8.0,
     'L1_attn_A_log': 3.133,
     'L1_attn_W1': 3.994,
     'L1_attn_W2': 3.717,
     'L1_ffn_gate_W': 8.0,
     'L1_ffn_w1_e': 8.0,
     'L1_ffn_w3_e': 8.0,
     'L1_ffn_w2_e': 8.0,
     'L1_ffn_w1_s': 8.0,
     'L1_ffn_w3_s': 8.0,
     'L1_ffn_w2_s': 8.0}
    for name, (base, spread) in spreads.items():
        noise = np.random.default_rng([zlib.crc32(name.encode()), seed]).standard_normal(out[name].shape)
        drawn = base * np.exp(spread * noise) if base else spread * noise
        out[name] = jnp.asarray(drawn.astype(out[name].dtype))
    for name, factor in factors.items():
        out[name] = (out[name] * factor).astype(out[name].dtype)
    return out
```

```python
from contextlib import ExitStack

import numpy as np

import concourse.bass as bass
from concourse import mybir

F32 = mybir.dt.float32
BF16 = mybir.dt.bfloat16
F16 = mybir.dt.float16
I32 = mybir.dt.int32
ALU = mybir.AluOpType
ACT = mybir.ActivationFunctionType
AX_X = mybir.AxisListType.X
ds = bass.ds

P = 128
T = 2048
C = 128
H = 16
HD = 64
NP = H // 2
NT = T // P
CH = 512
NC4 = T // CH
BUDGET = int(T * 0.2) - 1
BIG = 1e30
EPS = 1e-5
BITS = 32
STEPS = BITS // H
NS = 16
NE = 8
F = 512


def chunks(t):
    n = P * (t + 1)
    return [(c, min(c + CH, n)) for c in range(0, n, CH)]


def units(t):
    n = P * (t + 1)
    return [(c, min(c + 2 * CH, n)) for c in range(0, n, 2 * CH)]


def first_unit(t):
    return sum(H * len(units(u)) for u in range(t))


def first_chunk(t):
    return sum(H * len(chunks(u)) for u in range(t))


def first_mask_chunk(t):
    return sum(len(chunks(u)) for u in range(t))


def searched(t):
    return P * (t + 1) > BUDGET


def all_pairs(eng, t, body):
    if t == 0:
        body(0)
    with eng.Fori(1 if t == 0 else 0, NP - 1) as p:
        body(p)


def build(nc, A, out):
    with ExitStack() as ctx:
        def sb(name, shape, dt=F32):
            return ctx.enter_context(nc.sbuf_tensor(name, shape, dt))

        def sem(name):
            return ctx.enter_context(nc.semaphore(name))

        wide = ctx.enter_context(nc.psum_tensor("wide", [P, 8 * CH], F32))
        banks = [wide[:, i * CH:(i + 1) * CH] for i in range(8)]

        q_dram = nc.dram_tensor("q_dram", [NP, P, T], F32).ap()
        q0_dram = nc.dram_tensor("q0_dram", [HD, T + 1], F32).ap()
        bc_dram = nc.dram_tensor("bc_dram", [2 * NS, T], F32).ap()
        row_dram = nc.dram_tensor("row_dram", [NT, T], F32).ap()

        keysT = sb("keysT", [P, NP, T])
        values = sb("values", [P, NT, H * HD])
        resT = sb("resT", [P, T])
        wpT = sb("wpT", [P, NP, C])
        ident = sb("ident", [P, P])
        until = sb("until", [P, P])
        ones = sb("ones", [P, P])
        bits = sb("bits", [P, BITS], I32)
        keep3 = sb("keep3", [P, 2])
        small = sb("small", [P, 256])
        region = sb("region", [P, 14848])

        def part(at, n):
            return region[:, at:at + n]

        waT = part(0, 3 * H * HD)
        xn = part(3072, T).rearrange("p (t c) -> p t c", t=NT)
        xnT = part(5120, T)
        q_stage = [part(7168 + CH * i, CH) for i in range(2)]
        bv_all = part(8192, H * HD)
        wsT = part(9216, C)
        wneg = part(9344, C)
        logit = [part(T * i, T) for i in range(2)]
        probsT = part(2 * T, T)
        penalty = [part(3 * T + T * i, T) for i in range(2)]
        equal = part(5 * T, T // 2).bitcast(BF16)
        rank = part(5 * T + T // 2, T // 2).bitcast(F16)
        carry = part(5 * T, T)
        zq = [part(6 * T + P * i, P) for i in range(2)]
        zf = part(6 * T + 2 * P, P)
        y = part(6 * T + 3 * P, H * HD)
        yT = part(6 * T + 3 * P + H * HD, H * HD)

        stats = small[:, 0:96].rearrange("p (t s) -> p t s", t=NT)
        mv = small[:, 96:128].rearrange("p (t s) -> p t s", t=NT)
        rstd = small[:, 128:144]
        bqk = small[:, 144:160]
        bqn = small[:, 160:168]
        bp = small[:, 168:169]
        mins = small[:, 170:178]
        bias = small[:, 178:180]
        sums = small[:, 180:182]
        rsum = small[:, 182:184]
        low = small[:, 184:185]
        cand = small[:, 185:186]
        count = small[:, 186:187]
        taken = small[:, 187:188]
        need = small[:, 188:189]
        sd = small[:, 192:208]
        zero = small[:, 208:209]

        L = sem
        s_cst, s_x, s_wa, s_b, s_wp = L("s_cst"), L("s_x"), L("s_wa"), L("s_b"), L("s_wp")
        s_zero, s_mv, s_sd, s_rs, s_xn, s_xt = L("s_zero"), L("s_mv"), L("s_sd"), L("s_rs"), L("s_xn"), L("s_xt")
        s_xnT, s_bq, s_ws, s_proj, s_pa, s_pv_ev = L("s_xnT"), L("s_bq"), L("s_ws"), L("s_proj"), L("s_pa"), L("s_pv_ev")
        s_qd = [L("s_qd0"), L("s_qd1")]
        s_q0 = [L("s_q00"), L("s_q01")]
        s_q0z = L("s_q0z")
        s_stageA = L("s_stageA")

        block = ctx.enter_context(nc.Block())

        prods = ([("q", 0, c) for c in range(NC4)] + [("k", 0, c) for c in range(NC4)]
                 + [("q", p, c) for p in range(1, NP) for c in range(NC4)]
                 + [("k", p, c) for p in range(1, NP) for c in range(NC4)]
                 + [("v", t, c) for t in range(NT) for c in range(2)]
                 + [("s", 0, c) for c in range(NC4)])
        by_act = [n for n, x in enumerate(prods) if x[0] in "qk"]
        by_dve = [n for n, x in enumerate(prods) if x[0] in "vs"]

        def evacuated(eng, n):
            if n in by_act:
                eng.wait_ge(s_pa, by_act.index(n) + 1)
            else:
                eng.wait_ge(s_pv_ev, by_dve.index(n) + 1)

        s_zq = [L("s_zq0"), L("s_zq1")]
        s_zpad = L("s_zpad")
        s_qk = L("s_qk")
        s_ttr = L("s_ttr")
        s_mb = L("s_mb")
        s_exp = L("s_exp")
        s_tr = L("s_tr")
        s_cp = L("s_cp")
        s_pvc = L("s_pvc")
        s_rec = L("s_rec")
        s_y = L("s_y")
        s_zf = L("s_zf")
        s_fqk = L("s_fqk")
        s_relu = L("s_relu")
        s_msk = L("s_msk")
        s_fmm = L("s_fmm")
        s_fcp = L("s_fcp")
        s_big = L("s_big")
        s_row = L("s_row")
        s_carry = L("s_carry")
        s_srch = L("s_srch")
        s_fin = L("s_fin")
        s_dg = L("s_dg")
        s_yt = L("s_yt")
        s_yc = L("s_yc")
        s_pr = L("s_pr")
        s_res = L("s_res")

        kv = keysT[:, :, :].rearrange("p a n -> p (a n)")
        vv = values[:, :, :].rearrange("p a n -> p (a n)")

        def tiles(x):
            return x.rearrange("p (t c) -> p t c", t=NT)

        x1n, x1T = tiles(kv[:, 0:T]), kv[:, T:2 * T]
        xsT = kv[:, 2 * T:3 * T]
        delta, dxT = kv[:, 3 * T:4 * T], kv[:, 4 * T:5 * T]
        decay = [kv[:, (5 + i) * T:(6 + i) * T] for i in range(2)]
        acc = tiles(kv[:, 7 * T:8 * T])
        rowB = [vv[:, i * T:(i + 1) * T] for i in range(2)]
        rowC = [vv[:, (2 + i) * T:(3 + i) * T] for i in range(2)]
        state = [vv[:, (4 + i) * T:(5 + i) * T] for i in range(2)]
        ssmT = vv[:, 6 * T:7 * T]
        bcT = vv[:, 7 * T:8 * T]
        xaT = vv[:, 0:T]
        absz = vv[:, 2 * T:3 * T]
        hidT = vv[:, 0:4 * T].rearrange("p (f n) -> p f n", f=4)
        guT = [part(4 * CH * i, 4 * CH).rearrange("p (f n) -> p f n", f=4) for i in range(2)]
        w1b = [part(4096 + 1536 * i, F) for i in range(2)]
        w3b = [part(4608 + 1536 * i, F) for i in range(2)]
        w2b = [part(5120 + 1536 * i, F).rearrange("p (f c) -> p f c", f=4) for i in range(2)]
        silu = [part(7168 + CH * i, CH) for i in range(2)]
        w1m = part(8192, F)
        w2m = part(8704, F).rearrange("p (f c) -> p f c", f=4)
        wd, wbc, wg = part(9216, C), part(9344, 2 * NS), part(9376, NE)
        b2all = part(9384, C)
        x1 = tiles(part(9512, T))
        scr = part(11560, 8 * P)
        prob, keptw, cmp = (scr[:, P * i:P * (i + 1)].rearrange("p (t e) -> p t e", t=NT) for i in range(3))
        gate = scr[:, 3 * P:3 * P + NT * (NE + 1)].rearrange("p (t e) -> p t e", t=NT)
        top = scr[:, 640:640 + NT].rearrange("p (t o) -> p t o", o=1)
        rnk = scr[:, 656:656 + P].rearrange("p (t e) -> p t e", t=NT)
        vecs = part(12600, 64)
        ln1g, ln1b, bd, dskip, ln2g, ln2b, b1 = (vecs[:, a:b] for a, b in
                                                 ((0, 1), (1, 2), (2, 3), (3, 4), (4, 5), (5, 6), (6, 10)))
        bbc = vecs[:, 10:11]
        rate = vecs[:, 16:32]
        st2 = part(12700, 96).rearrange("p (t s) -> p t s", t=NT)
        mv2 = part(12800, 32).rearrange("p (t s) -> p t s", t=NT)
        sd2, rs2 = part(12832, NT), part(12848, NT)

        s_cw = L("s_cw")
        s_stat = L("s_stat")
        s_sq = L("s_sq")
        s_ln = L("s_ln")
        s_tp = L("s_tp")
        s_te = L("s_te")
        s_lg = L("s_lg")
        s_gt = L("s_gt")
        s_ge = L("s_ge")
        s_dl = L("s_dl")
        s_z = L("s_z")
        s_sp = L("s_sp")
        s_dx = L("s_dx")
        s_bcd = L("s_bcd")
        s_w = [L("s_w0"), L("s_w1")]
        s_bb = [L("s_bb0"), L("s_bb1")]
        s_cb = [L("s_cb0"), L("s_cb1")]
        s_an = L("s_an")
        s_bx = L("s_bx")
        s_sc = L("s_sc")
        s_hc = L("s_hc")
        s_ya = L("s_ya")
        s_h = L("s_h")
        s_si = L("s_si")
        s_gu = L("s_gu")
        s_eo = L("s_eo")
        s_ac = L("s_ac")
        s_ml = L("s_ml")
        s_ga = L("s_ga")
        s_m2 = L("s_m2")
        s_o = L("s_o")
        s_out = L("s_out")

        s_ac0 = L("s_ac0")
        s_gm = L("s_gm")
        s_yi = L("s_yi")
        STAT = 2 * NT + 2
        NW = 15

        @block.sync
        def _(sp):
            for dst, src in ((ident[:, :], A["c_ident"]), (until[:, :], A["c_until"]),
                             (ones[:, :], A["c_ones"]),
                             (bits[:, :], A["c_bits"]), (keep3[:, :], A["c_keep"])):
                sp.dma_start(dst, src).then_inc(s_cst, 16)
            sp.dma_start(xn, A["x"].rearrange("(t p) c -> p t c", p=P)).then_inc(s_x, 16)
            sp.dma_start(waT, A["W_attnT"]).then_inc(s_wa, 16)
            sp.dma_start(bqk, A["b_qkT"]).then_inc(s_b, 16)
            sp.dma_start(bp, A["b_proj"]).then_inc(s_b, 16)
            sp.dma_start(bv_all, A["b_v"].to_broadcast([P, H * HD])).then_inc(s_b, 16)
            sp.dma_start(wsT, A["W_signT"]).then_inc(s_wp, 16)
            sp.dma_start(resT[:, :], A["xT"]).then_inc(s_wp, 16)
            sp.dma_start(wpT[:, :, :], A["W_projT"].rearrange("(k p) c -> p k c", p=P)).then_inc(s_wp, 16)
            sp.wait_ge(s_zero, 1)
            with nc.allow_non_contiguous_dma(reason="one column"):
                sp.dma_start(q0_dram[:, 0:1], zero[0:HD, :]).then_inc(s_q0z, 16)
            for i in range(NP * NC4):
                p, c = divmod(i, NC4)
                n = prods.index(("q", p, c))
                evacuated(sp, n)
                sp.dma_start(q_dram[p, :, c * CH:(c + 1) * CH], q_stage[i % 2]).then_inc(s_qd[i % 2], 16)
                if p == 0:
                    sp.dma_start(q0_dram[:, 1 + c * CH:1 + (c + 1) * CH], q_stage[i % 2][0:HD, :]).then_inc(s_q0[i % 2], 16)

            def load_zf(t):
                if t > 0:
                    sp.wait_ge(s_fqk, first_mask_chunk(t))
                sp.dma_start(zf[0:HD, :], q0_dram[:, t * P:(t + 1) * P]).then_inc(s_zf, 16)

            def load_zq(t, h, par):
                if not (t == 0 and isinstance(h, int) and h < 2):
                    prev = first_unit(t) + len(units(t)) * (h - 1)
                    if isinstance(h, int) and h < 2:
                        prev = first_unit(t) - len(units(t - 1)) * (1 - h)
                    sp.wait_ge(s_qk, prev)
                pair = h // 2 if isinstance(h, int) else (h - par) // 2
                dst = zq[par][HD * par:HD * par + HD, :]
                src = q_dram[ds(pair, 1), HD * par:HD * par + HD, t * P:(t + 1) * P]
                sp.dma_start(dst, src.rearrange("a p n -> (a p) n")).then_inc(s_zq[par], 16)

            sp.wait_ge(s_q0z, 16)
            for i in range(2):
                sp.wait_ge(s_q0[i], 16 * (NC4 // 2))
                sp.wait_ge(s_qd[i], 16 * (NP * NC4 // 2))
            sp.wait_ge(s_stageA, 2)
            load_zf(0)
            for t in range(NT):
                if t + 1 < NT:
                    load_zf(t + 1)
                load_zq(t, 0, 0)
                load_zq(t, 1, 1)
                if t + 1 < NT:
                    sp.wait_ge(s_big, t + 1)
                    n = P * (t + 1)
                    sp.dma_start(row_dram[t:t + 1, 0:n], penalty[t % 2][P - 1:P, 0:n]).then_inc(s_row, 16)
                    sp.wait_ge(s_row, 16 * (t + 1))
                    if searched(t):
                        sp.wait_ge(s_fin, t)
                    if t > 0:
                        sp.wait_ge(s_fmm, first_mask_chunk(t + 1))
                    sp.dma_start(carry[0:1, 0:n], row_dram[t:t + 1, 0:n]).then_inc(s_carry, 16)
                with sp.Fori(1, NP) as p:
                    load_zq(t, 2 * p, 0)
                    load_zq(t, 2 * p + 1, 1)
            sp.wait_ge(s_res, NT)
            sp.wait_ge(s_pvc, first_chunk(NT))
            for dst, src in ((w1m, A["W1T"]), (w2m, A["W2T"].rearrange("(f p) c -> p f c", p=P)), (wd, A["WdT"]),
                             (wbc, A["WbcT"]), (wg, A["gate_WT"]), (b2all, A["b2"].to_broadcast([P, C])),
                             (ln1g, A["ln1_g"]), (ln1b, A["ln1_b"]), (bd, A["bd"]), (dskip, A["D"]),
                             (ln2g, A["ln2_g"]), (ln2b, A["ln2_b"]), (b1, A["b1T"]),
                             (bbc[0:2 * NS, :], A["bbc"]), (rate, A["A_log"])):
                sp.dma_start(dst, src).then_inc(s_cw, 16)

            def weights(e, par):
                if not (isinstance(e, int) and e < 2):
                    sp.wait_ge(s_eo, NC4 * (e - 1))
                for dst, name in ((w1b[par], "w1"), (w3b[par], "w3")):
                    sp.dma_start(dst, A[name][ds(e, 1), :, :].rearrange("a p f -> (a p) f")).then_inc(s_w[par], 16)
                sp.dma_start(w2b[par], A["w2"][ds(e, 1), :, :].rearrange("a (f p) c -> (a p) f c", p=P)).then_inc(s_w[par], 16)

            def rows(n, j):
                if not (isinstance(n, int) and n < 2):
                    sp.wait_ge(s_bx, n - 1)
                sp.dma_start(rowB[j], bc_dram[ds(n, 1), :].to_broadcast([P, T])).then_inc(s_bb[j], 16)
                if not (isinstance(n, int) and n < 2):
                    sp.wait_ge(s_hc, n - 1)
                sp.dma_start(rowC[j], bc_dram[ds(NS + n, 1), :].to_broadcast([P, T])).then_inc(s_cb[j], 16)

            weights(0, 0)
            weights(1, 1)
            sp.wait_ge(s_z, 2 * NC4)
            sp.dma_start(bc_dram, bcT[0:2 * NS, :]).then_inc(s_bcd, 16)
            sp.wait_ge(s_bcd, 16)
            sp.wait_ge(s_dx, 1)
            for j in range(2):
                rows(j, j)
            rows(2, 0)
            rows(3, 1)
            with sp.Fori(1, NE // 2) as p:
                rows(4 * p, 0)
                rows(4 * p + 1, 1)
                weights(2 * p, 0)
                rows(4 * p + 2, 0)
                rows(4 * p + 3, 1)
                weights(2 * p + 1, 1)
            weights(NE, 0)
            for c in range(NC4):
                sp.wait_ge(s_o, c + 1)
                sp.dma_start(out[0].rearrange("(t p) c -> p t c", p=P)[:, 4 * c:4 * c + 4, :],
                             acc[:, 4 * c:4 * c + 4, :]).then_inc(s_out, 16)
            sp.wait_ge(s_out, 16 * NC4)

        @block.gpsimd
        def _(pool):
            nc.gpsimd.memset(zero, 0.0).then_inc(s_zero, 1)
            pool.wait_ge(s_stageA, 2)
            nc.gpsimd.memset(zq[0], 0.0).then_inc(s_zpad, 1)
            nc.gpsimd.memset(zq[1], 0.0).then_inc(s_zpad, 1)
            for t in range(NT):
                pen = penalty[t % 2]
                pool.wait_ge(s_relu, first_mask_chunk(t + 1))
                nc.gpsimd.memset(pen[:, 0:1], 0.0).then_inc(s_msk, 1)
                pool.wait_ge(s_msk, 2 * t + 1)
                lo = max(0, P * (t - 1))
                w = P * (t + 1) - lo
                nc.gpsimd.affine_select(out=pen[:, lo:lo + w], in_=pen[:, lo:lo + w], compare_op=ALU.is_ge, fill=0.0,
                                        base=P * t - 2 - lo, pattern=[[-1, w]], channel_multiplier=1).then_inc(s_msk, 1)
                pool.wait_ge(s_fcp, first_mask_chunk(t + 1))
                dg = pen[:, P * t:P * (t + 1)]
                nc.gpsimd.affine_select(out=dg, in_=dg, compare_op=ALU.is_ge, fill=BIG,
                                        base=0, pattern=[[-1, P]], channel_multiplier=1).then_inc(s_big, 1)
                if searched(t):
                    pool.wait_ge(s_fin, t)
                    nc.gpsimd.affine_select(out=dg, in_=dg, compare_op=ALU.not_equal, fill=0.0,
                                            base=0, pattern=[[-1, P]], channel_multiplier=1).then_inc(s_dg, 1)

            def inputs(n, j):
                pool.wait_ge(s_bb[j], 16 * (n // 2 + 1) if isinstance(n, int) else 8 * (n - j) + 16)
                if not (isinstance(n, int) and n < 2):
                    pool.wait_ge(s_ya, n - 1)
                nc.gpsimd.tensor_tensor(state[j], dxT, rowB[j], ALU.mult).then_inc(s_bx, 1)

            pool.wait_ge(s_dx, 2)
            for n in range(4):
                inputs(n, n % 2)
            with pool.Fori(1, NE // 2) as p:
                for n in range(4):
                    inputs(4 * p + n, n % 2)

        @block.scalar
        def _(act):
            act.wait_ge(s_mv, NT + 1)
            nc.scalar.activation(sd, sd, ACT.Sqrt).then_inc(s_sd, 1)
            for b in range(4):
                act.wait_ge(s_xt, b + 1)
                nc.scalar.activation(xnT[:, b * CH:(b + 1) * CH], banks[b][:, :], ACT.Copy).then_inc(s_xnT, 1)
            act.wait_ge(s_bq, 1)
            nq = 0
            for n in by_act:
                kind, p, c = prods[n]
                act.wait_ge(s_proj, n + 1)
                if kind == "q":
                    if nq >= 2:
                        act.wait_ge(s_qd[nq % 2], 16 * (nq // 2))
                        if nq < NC4 + 2:
                            act.wait_ge(s_q0[nq % 2], 16 * (nq // 2))
                    nc.scalar.activation(q_stage[nq % 2], banks[n % 8][:, :], ACT.Identity,
                                         bias=bqn[:, p:p + 1], scale=-0.125).then_inc(s_pa, 1)
                    nq += 1
                else:
                    nc.scalar.activation(keysT[:, p, c * CH:(c + 1) * CH], banks[n % 8][:, :], ACT.Identity,
                                         bias=bqk[:, NP + p:NP + p + 1]).then_inc(s_pa, 1)

            def exps(t, h, par):
                n = P * (t + 1)
                act.wait_ge(s_mb, H * t + h + 1)
                if t > 0 or not isinstance(h, int) or h >= 2:
                    act.wait_ge(s_rec, H * t + h - 1)
                x = logit[par][:, 0:n]
                nc.scalar.activation(x, x, ACT.Exp, bias=bias[:, par:par + 1], scale=-1.0,
                                     accum_out=sums[:, par:par + 1]).then_inc(s_exp, 1)

            def copies(t, h):
                k = len(chunks(t))
                for c, (a, b) in enumerate(chunks(t)):
                    i = first_chunk(t) + k * h + c
                    act.wait_ge(s_tr, i + 1)
                    if t > 0 and c == 0:
                        act.wait_ge(s_pvc, first_chunk(t))
                    if not (t == 0 and isinstance(h, int) and h == 0):
                        act.wait_ge(s_pvc, i - k + 1)
                    nc.scalar.activation(probsT[:, a:b], banks[4 + c % 2][:, 0:b - a], ACT.Copy).then_inc(s_cp, 1)

            def outs(t, h, par):
                act.wait_ge(s_pvc, first_chunk(t) + len(chunks(t)) * (h + 1))
                act.wait_ge(s_rec, H * t + h + 1)
                if t > 0:
                    act.wait_ge(s_yt, 2 * t)
                nc.scalar.activation(y[:, ds(h * HD, HD)], banks[6 + par][:, 0:HD], ACT.Copy,
                                     scale=rsum[:, par:par + 1]).then_inc(s_y, 1)

            for t in range(NT):
                exps(t, 0, 0)

                def two_heads(p, t=t):
                    copies(t, 2 * p)
                    exps(t, 2 * p + 1, 1)
                    outs(t, 2 * p, 0)
                    copies(t, 2 * p + 1)
                    exps(t, 2 * p + 2, 0)
                    outs(t, 2 * p + 1, 1)

                all_pairs(act, t, two_heads)
                copies(t, H - 2)
                exps(t, H - 1, 1)
                outs(t, H - 2, 0)
                copies(t, H - 1)
                outs(t, H - 1, 1)
                for b in range(2):
                    act.wait_ge(s_yt, 2 * t + b + 1)
                    if t > 0:
                        act.wait_ge(s_pr, t)
                    nc.scalar.activation(yT[:, b * CH:(b + 1) * CH], banks[4 + b][:, :], ACT.Copy).then_inc(s_yc, 1)

            def from_banks(done, dst, first_bank, **affine):
                for b in range(NC4):
                    act.wait_ge(s_tp, done + b + 1)
                    nc.scalar.activation(dst[:, b * CH:(b + 1) * CH], banks[first_bank + b][:, :],
                                         ACT.Identity if affine else ACT.Copy, **affine).then_inc(s_te, 1)

            def root(n):
                act.wait_ge(s_stat, STAT * n + 2 * NT + 1)
                nc.scalar.activation(sd2, sd2, ACT.Sqrt).then_inc(s_sq, 1)

            act.wait_ge(s_cw, 16 * NW)
            from_banks(0, x1.rearrange("p t c -> p (t c)"), 0)
            root(0)
            root(1)
            from_banks(4, x1T, 4)
            from_banks(8, xsT, 0, bias=ln1b, scale=ln1g)
            act.wait_ge(s_gt, 2)
            nc.scalar.activation(prob, prob, ACT.Exp).then_inc(s_ge, 1)
            nc.scalar.activation(rate, rate, ACT.Exp).then_inc(s_sp, 1)
            for c in range(NC4):
                cols = slice(c * CH, (c + 1) * CH)
                act.wait_ge(s_dl, c + 1)
                nc.scalar.activation(delta[:, cols], banks[c][:, :], ACT.Identity, bias=bd).then_inc(s_z, 1)
            for c in range(NC4):
                cols = slice(c * CH, (c + 1) * CH)
                act.wait_ge(s_dl, NC4 + c + 1)
                nc.scalar.activation(bcT[0:2 * NS, cols], banks[4 + c][0:2 * NS, :], ACT.Identity,
                                     bias=bbc[0:2 * NS, :]).then_inc(s_z, 1)
            act.wait_ge(s_z, NC4)
            nc.scalar.activation(absz, delta, ACT.Abs).then_inc(s_sp, 1)
            act.wait_ge(s_sp, 2)
            nc.scalar.activation(absz, absz, ACT.Exp, scale=-1.0).then_inc(s_sp, 1)
            act.wait_ge(s_sp, 3)
            nc.scalar.activation(absz, absz, ACT.Ln, bias=ones[:, 0:1]).then_inc(s_sp, 1)

            def decays(n, j):
                if not (isinstance(n, int) and n < 2):
                    act.wait_ge(s_sc, n - 1)
                nc.scalar.activation(decay[j], delta, ACT.Exp, scale=rate[:, ds(n, 1)]).then_inc(s_an, 1)

            def silus(e):
                for m in range(4 * NC4):
                    i = 4 * NC4 * e + m
                    act.wait_ge(s_h, i + 1)
                    if not (isinstance(e, int) and e == 0 and m < 2):
                        act.wait_ge(s_gu, i - 1)
                    nc.scalar.activation(silu[m % 2], banks[2 * (m % 2)][:, :], ACT.Silu).then_inc(s_si, 1)

            act.wait_ge(s_dx, 3)
            for e in range(2):
                for j in range(2):
                    decays(2 * e + j, j)
                silus(e)
            with act.Fori(1, NE // 2) as p:
                for par in range(2):
                    for j in range(2):
                        decays(4 * p + 2 * par + j, j)
                    silus(2 * p + par)
            silus(NE)

            from_banks(12, x1n.rearrange("p t c -> p (t c)"), 0)
            root(2)
            from_banks(16, xsT, 4, bias=ln2b, scale=ln2g)
            for i in range(4 * NC4):
                f, c = divmod(i, NC4)
                act.wait_ge(s_ml, i + 1)
                nc.scalar.activation(hidT[:, f, c * CH:(c + 1) * CH], banks[i % 4][:, :], ACT.Gelu,
                                     bias=b1[:, f:f + 1]).then_inc(s_ga, 1)

        @block.tensor
        def _(pe):
            pe.wait_ge(s_cst, 16 * 5)
            for b in range(4):
                for i in range(4):
                    t = 4 * b + i
                    pe.wait_ge(s_xn, t + 1)
                    last = nc.tensor.transpose(banks[b][:, i * P:(i + 1) * P], xn[:, t, :], ident[:, :])
                last.then_inc(s_xt, 1)
            pe.wait_ge(s_wa, 16)
            pe.wait_ge(s_xnT, 4)
            pe.wait_ge(s_ws, 1)
            for n, (kind, p, c) in enumerate(prods):
                if n >= 8:
                    evacuated(pe, n - 8)
                cols = slice(c * CH, (c + 1) * CH)
                if kind == "q":
                    w, x = waT[:, p * P:(p + 1) * P], xnT[:, cols]
                elif kind == "k":
                    w, x = waT[:, (NP + p) * P:(NP + p + 1) * P], xnT[:, cols]
                elif kind == "v":
                    w, x = xnT[:, p * P:(p + 1) * P], waT[:, 2 * H * HD + c * CH:2 * H * HD + (c + 1) * CH]
                else:
                    w, x = wsT, xnT[:, cols]
                nc.tensor.matmul(banks[n % 8][:, :], w, x, start=True, stop=True).then_inc(s_proj, 1)

            pe.wait_ge(s_stageA, 2)
            pe.wait_ge(s_zpad, 2)

            def mask_scores(t):
                pe.wait_ge(s_zf, 16 * (t + 1))
                if t > 1:
                    pe.wait_ge(s_ttr, first_unit(t - 1))
                    pe.wait_ge(s_res, t - 1)
                elif t == 1:
                    pe.wait_ge(s_relu, 1)
                for c, (a, b) in enumerate(chunks(t)):
                    nc.tensor.matmul(banks[c][:, 0:b - a], zf[0:HD, :], keysT[0:HD, 0, a:b],
                                     start=True, stop=True).then_inc(s_fqk, 1)

            def mask_sums(t):
                pe.wait_ge(s_msk, 2 * t + 2)
                if t > 0:
                    pe.wait_ge(s_carry, 16 * t)
                    pe.wait_ge(s_cp, first_chunk(t - 1))
                    if t > 1:
                        pe.wait_ge(s_yc, 2 * (t - 1))
                base = first_mask_chunk(t)
                for c, (a, b) in enumerate(chunks(t)):
                    pe.wait_ge(s_fcp, base + c - 1) if base + c > 1 else None
                    carried = min(b, P * t)
                    last = nc.tensor.matmul(banks[4 + c % 2][:, 0:b - a], until[:, :], penalty[t % 2][:, a:b],
                                            start=True, stop=carried <= a)
                    if carried > a:
                        last = nc.tensor.matmul(banks[4 + c % 2][:, 0:carried - a], ones[0:1, :], carry[0:1, a:carried],
                                                start=False, stop=True)
                    last.then_inc(s_fmm, 1)

            def scores(t, h, par):
                k = len(units(t))
                pair = h // 2 if isinstance(h, int) else (h - par) // 2
                pe.wait_ge(s_zq[par], 16 * (NP * t + pair + 1))
                for c, (a, b) in enumerate(chunks(t)):
                    if isinstance(h, int) and h == 0:
                        if c == 0:
                            if t > 0:
                                pe.wait_ge(s_ttr, first_unit(t))
                                pe.wait_ge(s_res, t)
                            pe.wait_ge(s_relu, first_mask_chunk(min(t + 2, NT)))
                    elif c % 2 == 0:
                        pe.wait_ge(s_ttr, first_unit(t) + k * (h - 1) + c // 2 + 1)
                    last = nc.tensor.matmul(banks[c][:, 0:b - a], zq[par], keysT[:, ds(pair, 1), a:b].rearrange("p a n -> p (a n)"),
                                            start=True, stop=True)
                    if c % 2 or c == len(chunks(t)) - 1:
                        last.then_inc(s_qk, 1)

            def weigh(t, h, par):
                k = len(chunks(t))
                base = first_chunk(t) + k * h
                pe.wait_ge(s_exp, H * t + h + 1)

                def turn(c):
                    a, b = chunks(t)[c]
                    if c == 0:
                        pe.wait_ge(s_fcp, first_mask_chunk(min(t + 2, NT)))
                        if t > 0:
                            pe.wait_ge(s_yc, 2 * t)
                    pe.wait_ge(s_cp, base + c if c == 0 and k % 2 else base + c - 1) if k > 1 or t > 0 or not isinstance(h, int) or h > 0 else None
                    for i in range((b - a) // P):
                        last = nc.tensor.transpose(banks[4 + c % 2][:, i * P:(i + 1) * P],
                                                   logit[par][:, a + i * P:a + (i + 1) * P], ident[:, :])
                    last.then_inc(s_tr, 1)

                def sum_values(c):
                    a, b = chunks(t)[c]
                    pe.wait_ge(s_cp, base + c + 1)
                    if c == 0 and not (t == 0 and isinstance(h, int) and h < 2):
                        pe.wait_ge(s_y, H * t + h - 1)
                    for i in range((b - a) // P):
                        j = a // P + i
                        last = nc.tensor.matmul(banks[6 + par][:, 0:HD], probsT[:, j * P:(j + 1) * P],
                                                values[:, j, ds(h * HD, HD)], start=(j == 0), stop=(j == t))
                    last.then_inc(s_pvc, 1)

                turn(0)
                for c in range(1, k):
                    turn(c)
                    sum_values(c - 1)
                sum_values(k - 1)

            mask_scores(0)
            mask_sums(0)
            for t in range(NT):
                if t + 1 < NT:
                    mask_scores(t + 1)
                scores(t, 0, 0)
                if t + 1 < NT:
                    mask_sums(t + 1)

                def two_heads(p, t=t):
                    scores(t, 2 * p + 1, 1)
                    weigh(t, 2 * p, 0)
                    scores(t, 2 * p + 2, 0)
                    weigh(t, 2 * p + 1, 1)

                all_pairs(pe, t, two_heads)
                scores(t, H - 1, 1)
                weigh(t, H - 2, 0)
                weigh(t, H - 1, 1)
                pe.wait_ge(s_y, H * (t + 1))
                pe.wait_ge(s_cp, first_chunk(t + 1))
                for b in range(2):
                    for i in range(4):
                        k = 4 * b + i
                        last = nc.tensor.transpose(banks[4 + b][:, i * P:(i + 1) * P], y[:, k * P:(k + 1) * P], ident[:, :])
                    last.then_inc(s_yt, 1)
                pe.wait_ge(s_ttr, first_unit(t + 1))
                pe.wait_ge(s_yc, 2 * (t + 1))
                for k in range(NP):
                    last = nc.tensor.matmul(banks[0][:, 0:P], wpT[:, k, :], yT[:, k * P:(k + 1) * P],
                                            start=(k == 0), stop=(k == NP - 1))
                last.then_inc(s_pr, 1)

            def turn_tiles(src, first_bank):
                for b in range(NC4):
                    for i in range(4):
                        last = nc.tensor.transpose(banks[first_bank + b][:, i * P:(i + 1) * P], src(4 * b + i), ident[:, :])
                    last.then_inc(s_tp, 1)

            pe.wait_ge(s_res, NT)
            turn_tiles(lambda t: resT[:, t * P:(t + 1) * P], 0)
            pe.wait_ge(s_ln, NT)
            turn_tiles(lambda t: x1n[:, t, :], 4)
            pe.wait_ge(s_ln, 2 * NT)
            pe.wait_ge(s_te, 4)
            turn_tiles(lambda t: xaT[:, t * P:(t + 1) * P], 0)
            pe.wait_ge(s_cw, 16 * NW)
            pe.wait_ge(s_te, 8)
            for t in range(NT):
                last = nc.tensor.matmul(banks[4][:, t * NE:(t + 1) * NE], x1T[:, t * P:(t + 1) * P], wg, start=True, stop=True)
            last.then_inc(s_lg, 1)
            pe.wait_ge(s_te, 12)
            for c in range(NC4):
                nc.tensor.matmul(banks[c][:, :], wd, xsT[:, c * CH:(c + 1) * CH], start=True, stop=True).then_inc(s_dl, 1)
            pe.wait_ge(s_gt, 1)
            for c in range(NC4):
                nc.tensor.matmul(banks[4 + c][0:2 * NS, :], wbc, xsT[:, c * CH:(c + 1) * CH],
                                 start=True, stop=True).then_inc(s_dl, 1)

            pe.wait_ge(s_z, 2 * NC4)

            def hidden(e, par, c):
                x = x1T[:, c * CH:(c + 1) * CH]
                for f in range(4):
                    m = 4 * c + f
                    if not (isinstance(e, int) and e == 0 and m < 2):
                        pe.wait_ge(s_gu, 4 * NC4 * e + m - 1)
                    cols = slice(f * P, (f + 1) * P)
                    nc.tensor.matmul(banks[2 * (m % 2)][:, :], w1b[par][:, cols], x, start=True, stop=True)
                    nc.tensor.matmul(banks[2 * (m % 2) + 1][:, :], w3b[par][:, cols], x, start=True, stop=True).then_inc(s_h, 1)

            def outputs(e, par, c):
                pe.wait_ge(s_gu, 4 * NC4 * e + 4 * (c + 1))
                if not (isinstance(e, int) and e == 0 and c < 2):
                    pe.wait_ge(s_ac, NC4 * e + c - 1)
                for i in range(4):
                    for f in range(4):
                        last = nc.tensor.matmul(banks[4 + c % 2][:, i * P:(i + 1) * P], guT[c % 2][:, f, i * P:(i + 1) * P],
                                                w2b[par][:, f, :], start=(f == 0), stop=(f == 3))
                last.then_inc(s_eo, 1)

            def expert(e, par):
                pe.wait_ge(s_w[par], 48 * (e // 2 + 1) if isinstance(e, int) else 24 * (e - par) + 48)
                for c in range(NC4):
                    hidden(e, par, c)
                    if c > 0:
                        outputs(e, par, c - 1)
                outputs(e, par, NC4 - 1)

            expert(0, 0)
            expert(1, 1)
            with pe.Fori(1, NE // 2) as p:
                expert(2 * p, 0)
                expert(2 * p + 1, 1)
            expert(NE, 0)

            pe.wait_ge(s_dx, 4)
            pe.wait_ge(s_gu, 4 * NC4 * (NE + 1))
            turn_tiles(lambda t: ssmT[:, t * P:(t + 1) * P], 0)
            pe.wait_ge(s_ln, 3 * NT)
            pe.wait_ge(s_ac, NC4 * (NE + 1))
            turn_tiles(lambda t: dxT[:, t * P:(t + 1) * P], 4)
            pe.wait_ge(s_te, 20)
            for i in range(4 * NC4):
                f, c = divmod(i, NC4)
                if i >= 4:
                    pe.wait_ge(s_ga, i - 3)
                nc.tensor.matmul(banks[i % 4][:, :], w1m[:, f * P:(f + 1) * P], xsT[:, c * CH:(c + 1) * CH],
                                 start=True, stop=True).then_inc(s_ml, 1)
            pe.wait_ge(s_ga, 4 * NC4)
            for c in range(NC4):
                for i in range(4):
                    t = 4 * c + i
                    for f in range(4):
                        last = nc.tensor.matmul(banks[4 + c][:, i * P:(i + 1) * P], hidT[:, f, t * P:(t + 1) * P],
                                                w2m[:, f, :], start=(f == 0), stop=(f == 3))
                last.then_inc(s_m2, 1)

        @block.vector
        def _(dve):
            dve.wait_ge(s_x, 16)
            for t in range(NT):
                nc.vector.bn_stats(stats[:, t, :], xn[:, t, :]).then_inc(s_rs, 1)
            for t in range(NT):
                dve.wait_ge(s_rs, t + 1)
                nc.vector.bn_aggr(mv[:, t, :], stats[:, t, :]).then_inc(s_mv, 1)
            dve.wait_ge(s_mv, NT)
            nc.vector.tensor_scalar(sd.rearrange("p (t o) -> p t o", o=1), mv[:, :, 1:2], EPS, None, ALU.add).then_inc(s_mv, 1)
            dve.wait_ge(s_sd, 1)
            nc.vector.reciprocal(rstd, sd).then_inc(s_rs, 1)
            dve.wait_ge(s_rs, NT + 1)
            for t in range(NT):
                nc.vector.tensor_scalar(xn[:, t, :], xn[:, t, :], mv[:, t, 0:1], rstd[:, t:t + 1],
                                        ALU.subtract, ALU.mult).then_inc(s_xn, 1)
            dve.wait_ge(s_b, 48)
            nc.vector.tensor_scalar(bqn, bqk[:, 0:NP], -0.125, None, ALU.mult).then_inc(s_bq, 1)
            dve.wait_ge(s_wp, 48)
            nc.vector.tensor_scalar(wneg, wsT, 0.0, None, ALU.is_lt).then_inc(s_bq, 1)
            dve.wait_ge(s_bq, 2)
            nc.vector.scalar_tensor_tensor(out=wsT, in0=wsT, scalar=0.0, in1=wneg, op0=ALU.is_gt, op1=ALU.subtract).then_inc(s_ws, 1)
            for i, n in enumerate(by_dve):
                kind, t, c = prods[n]
                dve.wait_ge(s_proj, n + 1)
                cols = slice(c * CH, (c + 1) * CH)
                if kind == "v":
                    nc.vector.tensor_tensor(values[:, t, cols], banks[n % 8][:, :], bv_all[:, cols], ALU.add).then_inc(s_pv_ev, 1)
                else:
                    nc.vector.scalar_tensor_tensor(out=resT[:, cols], in0=resT[:, cols], scalar=bp, in1=banks[n % 8][:, :],
                                                   op0=ALU.add, op1=ALU.add).then_inc(s_pv_ev, 1)
            dve.wait_ge(s_pv_ev, len(by_dve))
            nc.vector.memset(mins[:, 0:4], 0.0).then_inc(s_stageA, 1)
            dve.wait_ge(s_pa, len(by_act))
            nc.vector.memset(mins[:, 4:8], 0.0).then_inc(s_stageA, 1)
            for i in range(2):
                dve.wait_ge(s_qd[i], 16 * (NP * NC4 // 2))

            srch = [0]

            def step(ins, base=0):
                srch[0] += 1
                ins.then_inc(s_srch, 1)
                dve.wait_ge(s_srch, base + srch[0])

            def mask_relu(t):
                for c, (a, b) in enumerate(chunks(t)):
                    dve.wait_ge(s_fqk, first_mask_chunk(t) + c + 1)
                    if c == 0 and t >= 2:
                        dve.wait_ge(s_ttr, first_unit(t - 1))
                        dve.wait_ge(s_row, 16 * (t - 1))
                        if searched(t - 2):
                            dve.wait_ge(s_dg, t - 2 - first_searched + 1)
                    nc.vector.tensor_scalar(penalty[t % 2][:, a:b], banks[c][:, 0:b - a], -1.0, 0.0,
                                            ALU.mult, ALU.max).then_inc(s_relu, 1)

            def mask_copy(t):
                for c, (a, b) in enumerate(chunks(t)):
                    dve.wait_ge(s_fmm, first_mask_chunk(t) + c + 1)
                    nc.vector.tensor_copy(penalty[t % 2][:, a:b], banks[4 + c % 2][:, 0:b - a]).then_inc(s_fcp, 1)

            def logits(t, h, par):
                k = len(units(t))
                base = first_unit(t) + k * h
                if not (t == 0 and isinstance(h, int) and h < 2):
                    g = len(chunks(t))
                    at = first_chunk(t) + g * (h - 1) if not (isinstance(h, int) and h < 2) else \
                        (first_chunk(t) - len(chunks(t - 1)) if h == 0 else first_chunk(t))
                    dve.wait_ge(s_tr, at)
                    dve.wait_ge(s_exp, H * t + h - 1)
                for c, (a, b) in enumerate(units(t)):
                    dve.wait_ge(s_qk, base + c + 1)
                    nc.vector.memset(mins[:, 4 * par + 2 + c:4 * par + 3 + c], 0.0)
                    nc.vector.tensor_tensor_reduce(logit[par][:, a:b], wide[:, a:b], penalty[t % 2][:, a:b],
                                                   1.0, 3e38, ALU.add, ALU.min,
                                                   mins[:, 4 * par + c:4 * par + c + 1]).then_inc(s_ttr, 1)
                dve.wait_ge(s_ttr, base + k)
                nc.vector.tensor_reduce(bias[:, par:par + 1], mins[:, 4 * par:4 * par + k], AX_X, ALU.min).then_inc(s_mb, 1)

            def recip(t, h, par):
                dve.wait_ge(s_exp, H * t + h + 1)
                if not (t == 0 and isinstance(h, int) and h < 2):
                    dve.wait_ge(s_y, H * t + h - 1)
                nc.vector.reciprocal(rsum[:, par:par + 1], sums[:, par:par + 1]).then_inc(s_rec, 1)

            PER = 4

            def search(t, i, base):
                n = P * (t + 1)
                pen = penalty[t % 2][:, 0:n]
                keep = keep3[:, 0:1] if t == first_searched else keep3[:, 1:2]
                at = base + PER * i
                nc.vector.tensor_tensor(cand.bitcast(I32), low.bitcast(I32), bits[:, ds(i, 1)], ALU.bitwise_or).then_inc(s_srch, 1)
                dve.wait_ge(s_srch, at + 1)
                nc.vector.tensor_scalar(equal[:, 0:n], pen, cand, None, ALU.is_lt, ALU.add, accum_out=count).then_inc(s_srch, 1)
                dve.wait_ge(s_srch, at + 2)
                nc.vector.scalar_tensor_tensor(out=taken, in0=count, scalar=keep, in1=cand, op0=ALU.is_lt, op1=ALU.mult).then_inc(s_srch, 1)
                dve.wait_ge(s_srch, at + 3)
                nc.vector.tensor_tensor(low, low, taken, ALU.max).then_inc(s_srch, 1)
                dve.wait_ge(s_srch, at + 4)

            FIN = 6

            def prune(t, base):
                n = P * (t + 1)
                pen = penalty[t % 2][:, 0:n]
                keep = keep3[:, 0:1] if t == first_searched else keep3[:, 1:2]
                e, r = equal[:, 0:n], rank[:, 0:n]
                nc.vector.tensor_scalar(e, pen, low, None, ALU.is_lt, ALU.add, accum_out=count).then_inc(s_srch, 1)
                dve.wait_ge(s_srch, base + 1)
                nc.vector.tensor_scalar(need, count, -1.0, keep, ALU.mult, ALU.add).then_inc(s_srch, 1)
                nc.vector.tensor_scalar(e, pen, low, None, ALU.is_equal).then_inc(s_srch, 1)
                dve.wait_ge(s_srch, base + 3)
                nc.vector.tensor_tensor_scan(r, e, e, 0.0, ALU.add, ALU.max).then_inc(s_srch, 1)
                dve.wait_ge(s_srch, base + 4)
                nc.vector.scalar_tensor_tensor(out=r, in0=r, scalar=need, in1=e, op0=ALU.is_gt, op1=ALU.mult).then_inc(s_srch, 1)
                dve.wait_ge(s_srch, base + 5)
                nc.vector.scalar_tensor_tensor(out=e, in0=pen, scalar=low, in1=r, op0=ALU.is_gt, op1=ALU.add).then_inc(s_srch, 1)
                dve.wait_ge(s_srch, base + 6)
                dve.wait_ge(s_row, 16 * (t + 1)) if t + 1 < NT else None
                nc.vector.scalar_tensor_tensor(out=pen, in0=e, scalar=BIG, in1=pen, op0=ALU.mult, op1=ALU.add).then_inc(s_fin, 1)

            first_searched = min(t for t in range(NT) if searched(t))

            def per_tile(t):
                return 1 + PER * BITS + FIN if searched(t) else 0

            mask_relu(0)
            mask_copy(0)
            for t in range(NT):
                look = t + 1 < NT and searched(t + 1)
                base = sum(per_tile(u) for u in range(t + 1))
                if t + 1 < NT:
                    mask_relu(t + 1)
                dve.wait_ge(s_big, t + 1)
                if searched(t):
                    dve.wait_ge(s_dg, t - first_searched + 1)
                logits(t, 0, 0)
                if t + 1 < NT:
                    mask_copy(t + 1)
                if look:
                    dve.wait_ge(s_big, t + 2)
                    nc.vector.memset(low, 0.0).then_inc(s_srch, 1)
                    dve.wait_ge(s_srch, base + 1)

                def two_heads(p, t=t, look=look, base=base):
                    for par in range(2):
                        if look:
                            for i in range(STEPS):
                                search(t + 1, 2 * STEPS * p + STEPS * par + i, base + 1)
                        logits(t, 2 * p + 1 + par, 1 - par)
                        recip(t, 2 * p + par, par)

                all_pairs(dve, t, two_heads)
                if look:
                    for i in range(STEPS):
                        search(t + 1, BITS - 2 * STEPS + i, base + 1)
                logits(t, H - 1, 1)
                recip(t, H - 2, 0)
                if look:
                    for i in range(STEPS):
                        search(t + 1, BITS - STEPS + i, base + 1)
                    prune(t + 1, base + 1 + PER * BITS)
                elif t + 1 < NT:
                    nc.vector.memset(taken, 0.0).then_inc(s_fin, 1)
                if t == 0:
                    pass
                recip(t, H - 1, 1)
                dve.wait_ge(s_pr, t + 1)
                cols = slice(t * P, (t + 1) * P)
                nc.vector.tensor_tensor(resT[:, cols], resT[:, cols], banks[0][:, 0:P], ALU.add).then_inc(s_res, 1)


            def layer_norm(n, src, dst):
                at = STAT * n
                for t in range(NT):
                    nc.vector.bn_stats(st2[:, t, :], src(t)).then_inc(s_stat, 1)
                for t in range(NT):
                    dve.wait_ge(s_stat, at + t + 1)
                    nc.vector.bn_aggr(mv2[:, t, :], st2[:, t, :]).then_inc(s_stat, 1)
                dve.wait_ge(s_stat, at + 2 * NT)
                nc.vector.tensor_scalar(sd2.rearrange("p (t o) -> p t o", o=1), mv2[:, :, 1:2], EPS, None, ALU.add).then_inc(s_stat, 1)
                dve.wait_ge(s_sq, n + 1)
                nc.vector.reciprocal(rs2, sd2).then_inc(s_stat, 1)
                dve.wait_ge(s_stat, at + STAT)
                for t in range(NT):
                    nc.vector.tensor_scalar(dst(t), src(t), mv2[:, t, 0:1], rs2[:, t:t + 1],
                                            ALU.subtract, ALU.mult).then_inc(s_ln, 1)

            dve.wait_ge(s_te, 4)
            layer_norm(0, lambda t: x1[:, t, :], lambda t: x1n[:, t, :])
            dve.wait_ge(s_ln, NT)
            layer_norm(1, lambda t: x1n[:, t, :], lambda t: xaT[:, t * P:(t + 1) * P])
            nc.vector.tensor_tensor(acc, x1, b2all.rearrange("p (o c) -> p o c", o=1).to_broadcast([P, NT, C]), ALU.add).then_inc(s_ac0, 1)

            dve.wait_ge(s_lg, 1)
            gates = [0]

            def gstep(ins):
                gates[0] += 1
                ins.then_inc(s_gt, 1)
                dve.wait_ge(s_gt, gates[0])

            logits8 = banks[4][:, 0:NT * NE].rearrange("p (t e) -> p t e", t=NT)
            gstep(nc.vector.tensor_copy(prob, logits8))
            nc.vector.tensor_reduce(top, prob, AX_X, ALU.max).then_inc(s_gm, 1)
            dve.wait_ge(s_gm, 1)
            gstep(nc.vector.tensor_tensor(prob, prob, top.to_broadcast([P, NT, NE]), ALU.subtract))
            dve.wait_ge(s_ge, 1)
            gstep(nc.vector.tensor_reduce(top, prob, AX_X, ALU.add))
            gstep(nc.vector.reciprocal(top, top))
            gstep(nc.vector.tensor_tensor(prob, prob, top.to_broadcast([P, NT, NE]), ALU.mult))
            for e in range(NE):
                mine = prob[:, :, e:e + 1]
                gstep(nc.vector.tensor_tensor(cmp[:, :, e:NE], prob[:, :, e:NE], mine.to_broadcast([P, NT, NE - e]), ALU.is_gt))
                if e:
                    gstep(nc.vector.tensor_tensor(cmp[:, :, 0:e], prob[:, :, 0:e], mine.to_broadcast([P, NT, e]), ALU.is_ge))
                gstep(nc.vector.tensor_reduce(rnk[:, :, e:e + 1], cmp, AX_X, ALU.add))
            gstep(nc.vector.tensor_scalar(keptw, rnk, 2.0, 0.5, ALU.is_lt, ALU.mult))
            gstep(nc.vector.memset(gate, 0.5 / 8))
            gstep(nc.vector.tensor_tensor(gate[:, :, 0:NE], keptw, prob, ALU.mult))

            dve.wait_ge(s_sp, 4)
            nc.vector.scalar_tensor_tensor(out=delta, in0=delta, scalar=0.0, in1=absz, op0=ALU.max, op1=ALU.add).then_inc(s_dx, 1)
            dve.wait_ge(s_dx, 1)
            nc.vector.tensor_tensor(dxT, delta, xsT, ALU.mult).then_inc(s_dx, 1)
            nc.vector.scalar_tensor_tensor(out=ssmT, in0=xsT, scalar=dskip, in1=x1T, op0=ALU.mult, op1=ALU.add).then_inc(s_yi, 1)
            nc.vector.tensor_scalar(rate, rate, -1.0, None, ALU.mult).then_inc(s_dx, 1)
            dve.wait_ge(s_yi, 1)

            def scan(n, j, k):
                if k == 0:
                    dve.wait_ge(s_an, n + 1)
                    dve.wait_ge(s_bx, n + 1)
                    nc.vector.tensor_tensor_scan(state[j], decay[j], state[j], 0.0, ALU.mult, ALU.add).then_inc(s_sc, 1)
                elif k == 1:
                    dve.wait_ge(s_sc, n + 1)
                    dve.wait_ge(s_cb[j], 16 * (n // 2 + 1) if isinstance(n, int) else 8 * (n - j) + 16)
                    nc.vector.tensor_tensor(state[j], state[j], rowC[j], ALU.mult).then_inc(s_hc, 1)
                else:
                    dve.wait_ge(s_hc, n + 1)
                    dve.wait_ge(s_ya, n)
                    nc.vector.tensor_tensor(ssmT, ssmT, state[j], ALU.add).then_inc(s_ya, 1)

            def gated(e, c):
                if not (isinstance(e, int) and e == 0 and c < 2):
                    dve.wait_ge(s_eo, NC4 * e + c - 1)
                for f in range(4):
                    m = 4 * c + f
                    dve.wait_ge(s_si, 4 * NC4 * e + m + 1)
                    nc.vector.tensor_tensor(guT[c % 2][:, f, :], silu[m % 2], banks[2 * (m % 2) + 1][:, :], ALU.mult).then_inc(s_gu, 1)

            def add_up(e, c):
                dve.wait_ge(s_eo, NC4 * e + c + 1)
                if not (isinstance(e, int) and e == 0):
                    dve.wait_ge(s_ac, NC4 * (e - 1) + c + 1)
                for i in range(4):
                    t = 4 * c + i
                    last = nc.vector.scalar_tensor_tensor(
                        out=acc[:, t, :], in0=banks[4 + c % 2][:, i * P:(i + 1) * P],
                        scalar=gate[:, t, ds(e, 1)], in1=acc[:, t, :], op0=ALU.mult, op1=ALU.add)
                last.then_inc(s_ac, 1)

            def expert(e, scans):
                for c in range(NC4):
                    gated(e, c)
                    if c > 0:
                        add_up(e, c - 1)
                    for n, j, k in scans[c]:
                        scan(n, j, k)
                add_up(e, NC4 - 1)

            def steps(n):
                return [[(n, 0, 0), (n, 0, 1)], [(n + 1, 1, 0)], [(n, 0, 2), (n + 1, 1, 1)], [(n + 1, 1, 2)]]

            dve.wait_ge(s_ac0, 1)
            for e in range(2):
                expert(e, steps(2 * e))
            with dve.Fori(1, NE // 2) as p:
                expert(2 * p, steps(4 * p))
                expert(2 * p + 1, steps(4 * p + 2))
            expert(NE, [[]] * NC4)

            dve.wait_ge(s_ya, NS)
            nc.vector.memset(sd2, 0.0).then_inc(s_dx, 1)
            dve.wait_ge(s_dx, 4)
            dve.wait_ge(s_te, 16)
            layer_norm(2, lambda t: x1n[:, t, :], lambda t: dxT[:, t * P:(t + 1) * P])
            dve.wait_ge(s_ac, NC4 * (NE + 1))
            nc.vector.tensor_tensor(acc, acc, x1n, ALU.add).then_inc(s_ac0, 1)
            dve.wait_ge(s_ac0, 2)
            for c in range(NC4):
                dve.wait_ge(s_m2, c + 1)
                part4 = acc[:, 4 * c:4 * c + 4, :]
                nc.vector.tensor_tensor(part4, part4, banks[4 + c][:, :].rearrange("p (t c) -> p t c", t=4), ALU.add).then_inc(s_o, 1)


def constants():
    bits = np.zeros((P, BITS), np.int32)
    bits[:, :31] = 1 << np.arange(30, -1, -1, dtype=np.int32)
    keep = np.full((P, 2), BUDGET, np.float32)
    t3 = BUDGET // P
    keep[:, 0] = np.minimum(BUDGET, t3 * P + np.arange(P) + 1)
    return {"c_ident": np.eye(P, dtype=np.float32), "c_until": np.triu(np.ones((P, P), np.float32)),
            "c_ones": np.ones((P, P), np.float32), "c_bits": bits, "c_keep": keep}


def layout(x):
    c = np.ascontiguousarray
    g = lambda n: np.asarray(x[n])
    X = g("L0_attn_x")[0]
    a = {"x": X, "xT": X.T, "W_attnT": g("L0_attn_W_attn").T, "b_qkT": g("L0_attn_b_attn")[:2 * H * HD].reshape(-1, P).T,
         "b_v": g("L0_attn_b_attn")[None, 2 * H * HD:], "W_projT": g("L0_attn_W_proj").T, "b_proj": g("L0_attn_b_proj")[:, None],
         "W_signT": g("L0_ffn_weight").T}
    col = lambda n: g(n)[:, None]
    a.update({"W1T": g("L1_attn_W1").T, "W2T": g("L1_attn_W2").T, "WdT": g("L1_attn_Wd").T, "WbcT": g("L1_attn_Wbc").T,
              "gate_WT": g("L1_ffn_gate_W").T, "b2": g("L1_attn_b2")[None], "ln1_g": col("L1_attn_ln1_g"),
              "ln1_b": col("L1_attn_ln1_b"), "bd": col("L1_attn_bd"), "D": col("L1_attn_D"), "ln2_g": col("L1_attn_ln2_g"),
              "ln2_b": col("L1_attn_ln2_b"), "b1T": g("L1_attn_b1").reshape(4, P).T, "bbc": col("L1_attn_bbc"),
              "A_log": g("L1_attn_A_log")})
    ns, d, fs = g("L1_ffn_w1_s").shape
    beside = lambda w: w.transpose(1, 0, 2).reshape(1, d, ns * fs)
    a["w1"] = np.concatenate([g("L1_ffn_w1_e"), beside(g("L1_ffn_w1_s"))])
    a["w3"] = np.concatenate([g("L1_ffn_w3_e"), beside(g("L1_ffn_w3_s"))])
    a["w2"] = np.concatenate([g("L1_ffn_w2_e"), g("L1_ffn_w2_s").reshape(1, ns * fs, d)])
    a.update(constants())
    return {k: c(v) for k, v in a.items()}


def kernel(**inputs):
    import concourse.bacc as bacc
    from concourse.bass_utils import run_bass_kernel_spmd

    arrays = layout(inputs)
    nc = bacc.Bacc("TRN2", target_bir_lowering=False, num_devices=1)
    aps = {n: nc.dram_tensor(n, a.shape, mybir.dt.from_np(a.dtype), kind="ExternalInput").ap() for n, a in arrays.items()}
    out = nc.dram_tensor("out", (1, T, C), F32, kind="ExternalOutput").ap()
    build(nc, aps, out)
    return run_bass_kernel_spmd(nc, [arrays], core_ids=[0]).results[0]["out"]
```

```python
from contextlib import ExitStack

import numpy as np

import concourse.bass as bass
from concourse import mybir

F32 = mybir.dt.float32
U16 = mybir.dt.uint16
F16 = mybir.dt.float16
I32 = mybir.dt.int32
ALU = mybir.AluOpType
ACT = mybir.ActivationFunctionType
AX_X = mybir.AxisListType.X
ds = bass.ds

P = 128
T = 2048
C = 128
H = 16
HD = 64
NP = H // 2
NT = T // P
CH = 512
NC4 = T // CH
BUDGET = int(T * 0.2) - 1
BIG = 1e30
EPS = 1e-5
HI_BITS = 15
LO_BITS = 16
BITS = HI_BITS + LO_BITS
STEPS = 3
SPLIT = 2
NS = 16
NE = 8
F = 512


def chunks(t):
    n = P * (t + 1)
    return [(c, min(c + CH, n)) for c in range(0, n, CH)]


def units(t):
    n = P * (t + 1)
    return [(c, min(c + 2 * CH, n)) for c in range(0, n, 2 * CH)]


def first_unit(t):
    return sum(H * len(units(u)) for u in range(t))


def first_chunk(t):
    return sum(H * len(chunks(u)) for u in range(t))


def first_mask_chunk(t):
    return sum(len(chunks(u)) for u in range(t))


def mask_steps(t):
    return 2 + 3 * t


def searched(t):
    return P * (t + 1) > BUDGET


def build(nc, A, out):
    with ExitStack() as ctx:
        def sb(name, shape, dt=F32):
            return ctx.enter_context(nc.sbuf_tensor(name, shape, dt))

        def sem(name):
            return ctx.enter_context(nc.semaphore(name))

        wide = ctx.enter_context(nc.psum_tensor("wide", [P, 8 * CH], F32))
        banks = [wide[:, i * CH:(i + 1) * CH] for i in range(8)]

        q_dram = nc.dram_tensor("q_dram", [NP, P, T], F32).ap()
        q0_dram = nc.dram_tensor("q0_dram", [HD, T + 1], F32).ap()
        bc_dram = nc.dram_tensor("bc_dram", [2 * NS, T], F32).ap()
        row_dram = nc.dram_tensor("row_dram", [NT, T], F32).ap()

        keysT = sb("keysT", [P, NP, T])
        values = sb("values", [P, NT, H * HD])
        resT = sb("resT", [P, T])
        wpT = sb("wpT", [P, NP, C])
        ident = sb("ident", [P, P])
        until = sb("until", [P, P])
        ones = sb("ones", [P, P])
        bits = sb("bits", [P, BITS])
        keep3 = sb("keep3", [P, 2 + NT])
        small = sb("small", [P, 256])
        region = sb("region", [P, 14848])

        def part(at, n):
            return region[:, at:at + n]

        waT = part(0, 3 * H * HD)
        xn = part(3072, T).rearrange("p (t c) -> p t c", t=NT)
        xnT = part(5120, T)
        q_stage = [part(7168 + CH * i, CH) for i in range(2)]
        bv_all = part(8192, H * HD)
        wsT = part(9216, C)
        wneg = part(9344, C)
        logit = [part(T * i, T) for i in range(2)]
        probsT = part(2 * T, T)
        penalty = [part(3 * T + T * i, T) for i in range(2)]
        half = part(5 * T, T // 2).bitcast(U16)
        flags = part(5 * T + T // 2, T // 2).bitcast(U16)
        side = part(5 * T, T // 2).bitcast(F16)
        rank = part(5 * T + T // 2, T // 2).bitcast(F16)
        carry = part(5 * T, T)
        zq = [part(6 * T + P * i, P) for i in range(2)]
        zf = part(6 * T + 2 * P, P)
        y = part(6 * T + 3 * P, H * HD)
        yT = part(6 * T + 3 * P + H * HD, H * HD)
        yP = part(6 * T + 3 * P + 2 * H * HD, P)

        stats = small[:, 0:96].rearrange("p (t s) -> p t s", t=NT)
        mv = small[:, 96:128].rearrange("p (t s) -> p t s", t=NT)
        rstd = small[:, 128:144]
        bqk = small[:, 144:160]
        bqn = small[:, 160:168]
        bp = small[:, 168:169]
        mins = small[:, 170:178]
        bias = small[:, 178:180]
        sums = small[:, 180:182]
        rsum = small[:, 182:184]
        low = small[:, 184:185]
        cand = small[:, 185:186]
        count = small[:, 186:187]
        turn_up = small[:, 187:188]
        need = small[:, 188:189]
        upper = small[:, 189:190]
        balance = small[:, 190:191]
        sd = small[:, 192:208]
        zero = small[:, 208:209]

        L = sem
        s_cst, s_x, s_wa, s_b, s_wp = L("s_cst"), L("s_x"), L("s_wa"), L("s_b"), L("s_wp")
        s_zero, s_mv, s_sd, s_rs, s_xn, s_xt = L("s_zero"), L("s_mv"), L("s_sd"), L("s_rs"), L("s_xn"), L("s_xt")
        s_xnT, s_bq, s_ws, s_proj, s_pa, s_pv_ev = L("s_xnT"), L("s_bq"), L("s_ws"), L("s_proj"), L("s_pa"), L("s_pv_ev")
        s_qd = [L("s_qd0"), L("s_qd1")]
        s_q0 = [L("s_q00"), L("s_q01")]
        s_q0z = L("s_q0z")
        s_stageA = L("s_stageA")

        def halves(t):
            both = penalty[t % 2][:, 0:P * (t + 1)].bitcast(U16).rearrange("p (n two) -> p n two", two=2)
            return both[:, :, 0:1].rearrange("p n a -> p (n a)"), both[:, :, 1:2].rearrange("p n a -> p (n a)")

        first_searched = min(t for t in range(NT) if searched(t))
        block = ctx.enter_context(nc.Block())

        prods = ([("q", 0, c) for c in range(NC4)] + [("k", 0, c) for c in range(NC4)]
                 + [("q", p, c) for p in range(1, NP) for c in range(NC4)]
                 + [("k", p, c) for p in range(1, NP) for c in range(NC4)]
                 + [("v", t, c) for t in range(NT) for c in range(2)]
                 + [("s", 0, c) for c in range(NC4)])
        by_act = [n for n, x in enumerate(prods) if x[0] in "qk"]
        by_dve = [n for n, x in enumerate(prods) if x[0] in "vs"]

        def evacuated(eng, n):
            if n in by_act:
                eng.wait_ge(s_pa, by_act.index(n) + 1)
            else:
                eng.wait_ge(s_pv_ev, by_dve.index(n) + 1)

        s_zq = [L("s_zq0"), L("s_zq1")]
        s_zpad = L("s_zpad")
        s_qk = L("s_qk")
        s_ttr = L("s_ttr")
        s_mb = L("s_mb")
        s_exp = L("s_exp")
        s_tr = L("s_tr")
        s_cp = L("s_cp")
        s_pvc = L("s_pvc")
        s_rec = L("s_rec")
        s_y = L("s_y")
        s_zf = L("s_zf")
        s_fqk = L("s_fqk")
        s_relu = L("s_relu")
        s_msk = L("s_msk")
        s_fmm = L("s_fmm")
        s_fcp = L("s_fcp")
        s_big = L("s_big")
        s_row = L("s_row")
        s_carry = L("s_carry")
        s_srch = L("s_srch")
        s_fin = L("s_fin")
        s_half = L("s_half")
        s_low = L("s_low")
        s_side = L("s_side")
        s_dg = L("s_dg")
        s_yt = L("s_yt")
        s_yc = L("s_yc")
        s_pr = L("s_pr")
        s_yp = L("s_yp")
        s_res = L("s_res")

        kv = keysT[:, :, :].rearrange("p a n -> p (a n)")
        vv = values[:, :, :].rearrange("p a n -> p (a n)")

        def tiles(x):
            return x.rearrange("p (t c) -> p t c", t=NT)

        x1n, x1T = tiles(kv[:, 0:T]), kv[:, T:2 * T]
        xsT = kv[:, 2 * T:3 * T]
        delta, dxT = kv[:, 3 * T:4 * T], kv[:, 4 * T:5 * T]
        decay = [kv[:, (5 + i) * T:(6 + i) * T] for i in range(2)]
        acc = tiles(kv[:, 7 * T:8 * T])
        rowB = [vv[:, i * T:(i + 1) * T] for i in range(2)]
        rowC = [vv[:, (2 + i) * T:(3 + i) * T] for i in range(2)]
        state = [vv[:, (4 + i) * T:(5 + i) * T] for i in range(2)]
        ssmT = vv[:, 6 * T:7 * T]
        bcT = vv[:, 7 * T:8 * T]
        xaT = vv[:, 0:T]
        absz = vv[:, 2 * T:3 * T]
        hidT = vv[:, 0:4 * T].rearrange("p (f n) -> p f n", f=4)
        guT = [part(4 * CH * i, 4 * CH).rearrange("p (f n) -> p f n", f=4) for i in range(2)]
        w1b = [part(4096 + 1536 * i, F) for i in range(2)]
        w3b = [part(4608 + 1536 * i, F) for i in range(2)]
        w2b = [part(5120 + 1536 * i, F).rearrange("p (f c) -> p f c", f=4) for i in range(2)]
        silu = [part(7168 + CH * i, CH) for i in range(2)]
        w1m = part(8192, F)
        w2m = part(8704, F).rearrange("p (f c) -> p f c", f=4)
        wd, wbc, wg = part(9216, C), part(9344, 2 * NS), part(9376, NE)
        b2all = part(9384, C)
        x1 = tiles(part(9512, T))
        scr = part(11560, 8 * P)
        prob, keptw, cmp = (scr[:, P * i:P * (i + 1)].rearrange("p (t e) -> p t e", t=NT) for i in range(3))
        gate = scr[:, 3 * P:3 * P + NT * (NE + 1)].rearrange("p (t e) -> p t e", t=NT)
        top = scr[:, 640:640 + NT].rearrange("p (t o) -> p t o", o=1)
        rnk = scr[:, 656:656 + P].rearrange("p (t e) -> p t e", t=NT)
        vecs = part(12600, 64)
        ln1g, ln1b, bd, dskip, ln2g, ln2b, b1 = (vecs[:, a:b] for a, b in
                                                 ((0, 1), (1, 2), (2, 3), (3, 4), (4, 5), (5, 6), (6, 10)))
        bbc = vecs[:, 10:11]
        rate = vecs[:, 16:32]
        st2 = part(12700, 96).rearrange("p (t s) -> p t s", t=NT)
        mv2 = part(12800, 32).rearrange("p (t s) -> p t s", t=NT)
        sd2, rs2 = part(12832, NT), part(12848, NT)

        s_cw = L("s_cw")
        s_stat = L("s_stat")
        s_sq = L("s_sq")
        s_ln = L("s_ln")
        s_tp = L("s_tp")
        s_te = L("s_te")
        s_lg = L("s_lg")
        s_gt = L("s_gt")
        s_ge = L("s_ge")
        s_dl = L("s_dl")
        s_z = L("s_z")
        s_sp = L("s_sp")
        s_dx = L("s_dx")
        s_bcd = L("s_bcd")
        s_w = [L("s_w0"), L("s_w1")]
        s_bb = [L("s_bb0"), L("s_bb1")]
        s_cb = [L("s_cb0"), L("s_cb1")]
        s_an = L("s_an")
        s_bx = L("s_bx")
        s_sc = L("s_sc")
        s_hc = L("s_hc")
        s_ya = L("s_ya")
        s_h = L("s_h")
        s_si = L("s_si")
        s_gu = L("s_gu")
        s_eo = L("s_eo")
        s_ac = L("s_ac")
        s_ml = L("s_ml")
        s_ga = L("s_ga")
        s_m2 = L("s_m2")
        s_o = L("s_o")
        s_out = L("s_out")

        s_ac0 = L("s_ac0")
        s_gm = L("s_gm")
        s_yi = L("s_yi")
        STAT = 2 * NT + 2
        NW = 15

        @block.sync
        def _(sp):
            for dst, src in ((ident[:, :], A["c_ident"]), (until[:, :], A["c_until"]),
                             (ones[:, :], A["c_ones"]),
                             (bits[:, :], A["c_bits"]), (keep3[:, :], A["c_keep"])):
                sp.dma_start(dst, src).then_inc(s_cst, 16)
            sp.dma_start(xn, A["x"].rearrange("(t p) c -> p t c", p=P)).then_inc(s_x, 16)
            sp.dma_start(waT, A["W_attnT"]).then_inc(s_wa, 16)
            sp.dma_start(bqk, A["b_qkT"]).then_inc(s_b, 16)
            sp.dma_start(bp, A["b_proj"]).then_inc(s_b, 16)
            sp.dma_start(bv_all, A["b_v"].to_broadcast([P, H * HD])).then_inc(s_b, 16)
            sp.dma_start(wsT, A["W_signT"]).then_inc(s_wp, 16)
            sp.dma_start(resT[:, :], A["xT"]).then_inc(s_wp, 16)
            sp.dma_start(wpT[:, :, :], A["W_projT"].rearrange("(k p) c -> p k c", p=P)).then_inc(s_wp, 16)
            sp.wait_ge(s_zero, 1)
            with nc.allow_non_contiguous_dma(reason="one column"):
                sp.dma_start(q0_dram[:, 0:1], zero[0:HD, :]).then_inc(s_q0z, 16)
            for i in range(NP * NC4):
                p, c = divmod(i, NC4)
                n = prods.index(("q", p, c))
                evacuated(sp, n)
                sp.dma_start(q_dram[p, :, c * CH:(c + 1) * CH], q_stage[i % 2]).then_inc(s_qd[i % 2], 16)
                if p == 0:
                    sp.dma_start(q0_dram[:, 1 + c * CH:1 + (c + 1) * CH], q_stage[i % 2][0:HD, :]).then_inc(s_q0[i % 2], 16)

            def load_zf(t):
                if t > 0:
                    sp.wait_ge(s_fqk, first_mask_chunk(t))
                sp.dma_start(zf[0:HD, :], q0_dram[:, t * P:(t + 1) * P]).then_inc(s_zf, 16)

            def load_zq(t, h, par):
                if not (t == 0 and isinstance(h, int) and h < 2):
                    prev = first_unit(t) + len(units(t)) * (h - 1)
                    if isinstance(h, int) and h < 2:
                        prev = first_unit(t) - len(units(t - 1)) * (1 - h)
                    sp.wait_ge(s_qk, prev)
                pair = h // 2 if isinstance(h, int) else (h - par) // 2
                dst = zq[par][HD * par:HD * par + HD, :]
                src = q_dram[ds(pair, 1), HD * par:HD * par + HD, t * P:(t + 1) * P]
                sp.dma_start(dst, src.rearrange("a p n -> (a p) n")).then_inc(s_zq[par], 16)

            sp.wait_ge(s_q0z, 16)
            for i in range(2):
                sp.wait_ge(s_q0[i], 16 * (NC4 // 2))
                sp.wait_ge(s_qd[i], 16 * (NP * NC4 // 2))
            sp.wait_ge(s_stageA, 2)
            sp.wait_ge(s_zpad, 2)
            load_zf(0)
            load_zq(0, 0, 0)
            load_zq(0, 1, 1)
            for t in range(NT):
                if t + 1 < NT:
                    load_zf(t + 1)
                    sp.wait_ge(s_big, t + 1)
                    n = P * (t + 1)
                    sp.dma_start(row_dram[t:t + 1, 0:n], penalty[t % 2][P - 1:P, 0:n]).then_inc(s_row, 16)
                    sp.wait_ge(s_row, 16 * (t + 1))
                    if searched(t):
                        sp.wait_ge(s_fin, t)
                    if t > 0:
                        sp.wait_ge(s_msk, mask_steps(t))
                    sp.dma_start(carry[0:1, 0:n], row_dram[t:t + 1, 0:n]).then_inc(s_carry, 16)
                with sp.Fori(1, NP) as p:
                    load_zq(t, 2 * p, 0)
                    load_zq(t, 2 * p + 1, 1)
                if t + 1 < NT:
                    load_zq(t + 1, 0, 0)
                    load_zq(t + 1, 1, 1)
            sp.wait_ge(s_res, NT)
            sp.wait_ge(s_pvc, first_chunk(NT))
            for dst, src in ((w1m, A["W1T"]), (w2m, A["W2T"].rearrange("(f p) c -> p f c", p=P)), (wd, A["WdT"]),
                             (wbc, A["WbcT"]), (wg, A["gate_WT"]), (b2all, A["b2"].to_broadcast([P, C])),
                             (ln1g, A["ln1_g"]), (ln1b, A["ln1_b"]), (bd, A["bd"]), (dskip, A["D"]),
                             (ln2g, A["ln2_g"]), (ln2b, A["ln2_b"]), (b1, A["b1T"]),
                             (bbc[0:2 * NS, :], A["bbc"]), (rate, A["A_log"])):
                sp.dma_start(dst, src).then_inc(s_cw, 16)

            def weights(e, par):
                if not (isinstance(e, int) and e < 2):
                    sp.wait_ge(s_eo, NC4 * (e - 1))
                for dst, name in ((w1b[par], "w1"), (w3b[par], "w3")):
                    sp.dma_start(dst, A[name][ds(e, 1), :, :].rearrange("a p f -> (a p) f")).then_inc(s_w[par], 16)
                sp.dma_start(w2b[par], A["w2"][ds(e, 1), :, :].rearrange("a (f p) c -> (a p) f c", p=P)).then_inc(s_w[par], 16)

            def rows(n, j):
                if not (isinstance(n, int) and n < 2):
                    sp.wait_ge(s_bx, n - 1)
                sp.dma_start(rowB[j], bc_dram[ds(n, 1), :].to_broadcast([P, T])).then_inc(s_bb[j], 16)
                if not (isinstance(n, int) and n < 2):
                    sp.wait_ge(s_hc, n - 1)
                sp.dma_start(rowC[j], bc_dram[ds(NS + n, 1), :].to_broadcast([P, T])).then_inc(s_cb[j], 16)

            weights(0, 0)
            weights(1, 1)
            sp.wait_ge(s_z, 2 * NC4)
            sp.dma_start(bc_dram, bcT[0:2 * NS, :]).then_inc(s_bcd, 16)
            sp.wait_ge(s_bcd, 16)
            sp.wait_ge(s_dx, 1)
            for j in range(2):
                rows(j, j)
            rows(2, 0)
            rows(3, 1)
            with sp.Fori(1, NE // 2) as p:
                rows(4 * p, 0)
                rows(4 * p + 1, 1)
                weights(2 * p, 0)
                rows(4 * p + 2, 0)
                rows(4 * p + 3, 1)
                weights(2 * p + 1, 1)
            weights(NE, 0)
            for c in range(NC4):
                sp.wait_ge(s_o, c + 1)
                sp.dma_start(out[0].rearrange("(t p) c -> p t c", p=P)[:, 4 * c:4 * c + 4, :],
                             acc[:, 4 * c:4 * c + 4, :]).then_inc(s_out, 16)
            sp.wait_ge(s_out, 16 * NC4)

        @block.gpsimd
        def _(pool):
            nc.gpsimd.memset(zero, 0.0).then_inc(s_zero, 1)
            pool.wait_ge(s_stageA, 2)
            nc.gpsimd.memset(zq[0], 0.0).then_inc(s_zpad, 1)
            nc.gpsimd.memset(zq[1], 0.0).then_inc(s_zpad, 1)
            for t in range(NT):
                pen = penalty[t % 2]
                pool.wait_ge(s_relu, first_mask_chunk(t + 1))
                nc.gpsimd.memset(pen[:, 0:1], 0.0).then_inc(s_msk, 1)
                pool.wait_ge(s_msk, mask_steps(t - 1) + 1 if t > 0 else 1)
                lo = max(0, P * (t - 1))
                w = P * (t + 1) - lo
                nc.gpsimd.affine_select(out=pen[:, lo:lo + w], in_=pen[:, lo:lo + w], compare_op=ALU.is_ge, fill=0.0,
                                        base=P * t - 2 - lo, pattern=[[-1, w]], channel_multiplier=1).then_inc(s_msk, 1)
                if t > 0:
                    pool.wait_ge(s_msk, mask_steps(t - 1) + 2)
                    pool.wait_ge(s_carry, 16 * t)
                    nc.gpsimd.tensor_tensor(pen[0:1, 0:P * t], pen[0:1, 0:P * t], carry[0:1, 0:P * t], ALU.add).then_inc(s_msk, 1)
                pool.wait_ge(s_fcp, first_mask_chunk(t + 1))
                dg = pen[:, P * t:P * (t + 1)]
                nc.gpsimd.affine_select(out=dg, in_=dg, compare_op=ALU.is_ge, fill=BIG,
                                        base=0, pattern=[[-1, P]], channel_multiplier=1).then_inc(s_big, 1)
                if searched(t):
                    pool.wait_ge(s_fin, t)
                    nc.gpsimd.affine_select(out=dg, in_=dg, compare_op=ALU.not_equal, fill=0.0,
                                            base=0, pattern=[[-1, P]], channel_multiplier=1).then_inc(s_dg, 1)

            def inputs(n, j):
                pool.wait_ge(s_bb[j], 16 * (n // 2 + 1) if isinstance(n, int) else 8 * (n - j) + 16)
                if not (isinstance(n, int) and n < 2):
                    pool.wait_ge(s_ya, n - 1)
                nc.gpsimd.tensor_tensor(state[j], dxT, rowB[j], ALU.mult).then_inc(s_bx, 1)

            pool.wait_ge(s_dx, 2)
            for n in range(4):
                inputs(n, n % 2)
            with pool.Fori(1, NE // 2) as p:
                for n in range(4):
                    inputs(4 * p + n, n % 2)

        @block.scalar
        def _(act):
            act.wait_ge(s_mv, NT + 1)
            nc.scalar.activation(sd, sd, ACT.Sqrt).then_inc(s_sd, 1)
            for b in range(4):
                act.wait_ge(s_xt, b + 1)
                nc.scalar.activation(xnT[:, b * CH:(b + 1) * CH], banks[b][:, :], ACT.Copy).then_inc(s_xnT, 1)
            act.wait_ge(s_bq, 1)
            nq = 0
            for n in by_act:
                kind, p, c = prods[n]
                act.wait_ge(s_proj, n + 1)
                if kind == "q":
                    if nq >= 2:
                        act.wait_ge(s_qd[nq % 2], 16 * (nq // 2))
                        if nq < NC4 + 2:
                            act.wait_ge(s_q0[nq % 2], 16 * (nq // 2))
                    nc.scalar.activation(q_stage[nq % 2], banks[n % 8][:, :], ACT.Identity,
                                         bias=bqn[:, p:p + 1], scale=-0.125).then_inc(s_pa, 1)
                    nq += 1
                else:
                    nc.scalar.activation(keysT[:, p, c * CH:(c + 1) * CH], banks[n % 8][:, :], ACT.Identity,
                                         bias=bqk[:, NP + p:NP + p + 1]).then_inc(s_pa, 1)

            def exps(t, h, par):
                n = P * (t + 1)
                act.wait_ge(s_mb, H * t + h + 1)
                if t > 0 or not isinstance(h, int) or h >= 2:
                    act.wait_ge(s_rec, H * t + h - 1)
                x = logit[par][:, 0:n]
                nc.scalar.activation(x, x, ACT.Exp, bias=bias[:, par:par + 1], scale=-1.0,
                                     accum_out=sums[:, par:par + 1]).then_inc(s_exp, 1)

            def copies(t, h):
                k = len(chunks(t))
                for c, (a, b) in enumerate(chunks(t)):
                    i = first_chunk(t) + k * h + c
                    act.wait_ge(s_tr, i + 1)
                    if t > 0 and c == 0:
                        act.wait_ge(s_pvc, first_chunk(t))
                    if not (t == 0 and isinstance(h, int) and h == 0):
                        act.wait_ge(s_pvc, i - k + 1)
                    nc.scalar.activation(probsT[:, a:b], banks[4 + c % 2][:, 0:b - a], ACT.Copy).then_inc(s_cp, 1)

            def outs(t, h, par):
                act.wait_ge(s_pvc, first_chunk(t) + len(chunks(t)) * (h + 1))
                act.wait_ge(s_rec, H * t + h + 1)
                if t > 0:
                    act.wait_ge(s_yt, 2 * t)
                nc.scalar.activation(y[:, ds(h * HD, HD)], banks[6 + par][:, 0:HD], ACT.Copy,
                                     scale=rsum[:, par:par + 1]).then_inc(s_y, 1)

            def sides(t):
                n = P * (t + 1)
                act.wait_ge(s_low, t - first_searched + 1)
                nc.scalar.activation(side[:, 0:n], penalty[t % 2][:, 0:n], ACT.Sign, bias=low, scale=-1.0,
                                     accum_out=balance).then_inc(s_side, 1)

            def mask_relu(t):
                for c, (a, b) in enumerate(chunks(t)):
                    act.wait_ge(s_fqk, first_mask_chunk(t) + c + 1)
                    if c == 0 and t >= 2:
                        act.wait_ge(s_ttr, first_unit(t - 1))
                        act.wait_ge(s_row, 16 * (t - 1))
                        if searched(t - 2):
                            act.wait_ge(s_dg, t - 2 - first_searched + 1)
                    nc.scalar.activation(penalty[t % 2][:, a:b], banks[c][:, 0:b - a], ACT.Relu, scale=-1.0).then_inc(s_relu, 1)

            def mask_copy(t):
                for c, (a, b) in enumerate(chunks(t)):
                    act.wait_ge(s_fmm, first_mask_chunk(t) + c + 1)
                    nc.scalar.activation(penalty[t % 2][:, a:b], banks[c][:, 0:b - a], ACT.Copy).then_inc(s_fcp, 1)

            def upper_halves(t):
                n = P * (t + 1)
                act.wait_ge(s_big, t + 1)
                nc.scalar.activation(half[:, 0:n], halves(t)[1], ACT.Copy).then_inc(s_half, 1)

            mask_relu(0)
            mask_copy(0)
            exps(0, 0, 0)
            for t in range(NT):
                def head(h, par, t=t):
                    if t < 4:
                        exps(t, h + 1, 1 - par)
                        copies(t, h)
                    else:
                        copies(t, h)
                        exps(t, h + 1, 1 - par)
                    outs(t, h, par)

                def two_heads(p):
                    head(2 * p, 0)
                    head(2 * p + 1, 1)

                exps(t, 1, 1)
                if t + 1 < NT:
                    mask_relu(t + 1)
                copies(t, 0)
                outs(t, 0, 0)
                if t + 1 < NT:
                    mask_copy(t + 1)
                copies(t, 1)
                exps(t, 2, 0)
                outs(t, 1, 1)
                if t + 1 < NT and searched(t + 1):
                    upper_halves(t + 1)
                with act.Fori(1, NP - 1) as p:
                    two_heads(p)
                copies(t, H - 2)
                if t + 1 < NT and searched(t + 1):
                    sides(t + 1)
                exps(t, H - 1, 1)
                outs(t, H - 2, 0)
                copies(t, H - 1)
                outs(t, H - 1, 1)
                if t + 1 < NT:
                    exps(t + 1, 0, 0)
                for b in range(2):
                    act.wait_ge(s_yt, 2 * t + b + 1)
                    nc.scalar.activation(yT[:, b * CH:(b + 1) * CH], banks[4 + b][:, :], ACT.Copy).then_inc(s_yc, 1)
                act.wait_ge(s_pr, t + 1)
                if t > 0:
                    act.wait_ge(s_res, t)
                nc.scalar.activation(yP, banks[4][:, 0:P], ACT.Copy).then_inc(s_yp, 1)

            def from_banks(done, dst, first_bank, **affine):
                for b in range(NC4):
                    act.wait_ge(s_tp, done + b + 1)
                    nc.scalar.activation(dst[:, b * CH:(b + 1) * CH], banks[first_bank + b][:, :],
                                         ACT.Identity if affine else ACT.Copy, **affine).then_inc(s_te, 1)

            def root(n):
                act.wait_ge(s_stat, STAT * n + 2 * NT + 1)
                nc.scalar.activation(sd2, sd2, ACT.Sqrt).then_inc(s_sq, 1)

            act.wait_ge(s_cw, 16 * NW)
            from_banks(0, x1.rearrange("p t c -> p (t c)"), 0)
            root(0)
            root(1)
            from_banks(4, x1T, 4)
            from_banks(8, xsT, 0, bias=ln1b, scale=ln1g)
            act.wait_ge(s_gt, 2)
            nc.scalar.activation(prob, prob, ACT.Exp).then_inc(s_ge, 1)
            nc.scalar.activation(rate, rate, ACT.Exp).then_inc(s_sp, 1)
            for c in range(NC4):
                cols = slice(c * CH, (c + 1) * CH)
                act.wait_ge(s_dl, c + 1)
                nc.scalar.activation(delta[:, cols], banks[c][:, :], ACT.Identity, bias=bd).then_inc(s_z, 1)
            for c in range(NC4):
                cols = slice(c * CH, (c + 1) * CH)
                act.wait_ge(s_dl, NC4 + c + 1)
                nc.scalar.activation(bcT[0:2 * NS, cols], banks[4 + c][0:2 * NS, :], ACT.Identity,
                                     bias=bbc[0:2 * NS, :]).then_inc(s_z, 1)
            act.wait_ge(s_z, NC4)
            nc.scalar.activation(absz, delta, ACT.Abs).then_inc(s_sp, 1)
            act.wait_ge(s_sp, 2)
            nc.scalar.activation(absz, absz, ACT.Exp, scale=-1.0).then_inc(s_sp, 1)
            act.wait_ge(s_sp, 3)
            nc.scalar.activation(absz, absz, ACT.Ln, bias=ones[:, 0:1]).then_inc(s_sp, 1)

            def decays(n, j):
                if not (isinstance(n, int) and n < 2):
                    act.wait_ge(s_sc, n - 1)
                nc.scalar.activation(decay[j], delta, ACT.Exp, scale=rate[:, ds(n, 1)]).then_inc(s_an, 1)

            def silus(e):
                for m in range(4 * NC4):
                    i = 4 * NC4 * e + m
                    act.wait_ge(s_h, i + 1)
                    if not (isinstance(e, int) and e == 0 and m < 2):
                        act.wait_ge(s_gu, i - 1)
                    nc.scalar.activation(silu[m % 2], banks[2 * (m % 2)][:, :], ACT.Silu).then_inc(s_si, 1)

            act.wait_ge(s_dx, 3)
            for e in range(2):
                for j in range(2):
                    decays(2 * e + j, j)
                silus(e)
            with act.Fori(1, NE // 2) as p:
                for par in range(2):
                    for j in range(2):
                        decays(4 * p + 2 * par + j, j)
                    silus(2 * p + par)
            silus(NE)

            from_banks(12, x1n.rearrange("p t c -> p (t c)"), 0)
            root(2)
            from_banks(16, xsT, 4, bias=ln2b, scale=ln2g)
            for i in range(4 * NC4):
                f, c = divmod(i, NC4)
                act.wait_ge(s_ml, i + 1)
                nc.scalar.activation(hidT[:, f, c * CH:(c + 1) * CH], banks[i % 4][:, :], ACT.Gelu,
                                     bias=b1[:, f:f + 1]).then_inc(s_ga, 1)

        @block.tensor
        def _(pe):
            pe.wait_ge(s_cst, 16 * 5)
            for b in range(4):
                for i in range(4):
                    t = 4 * b + i
                    pe.wait_ge(s_xn, t + 1)
                    last = nc.tensor.transpose(banks[b][:, i * P:(i + 1) * P], xn[:, t, :], ident[:, :])
                last.then_inc(s_xt, 1)
            pe.wait_ge(s_wa, 16)
            pe.wait_ge(s_xnT, 4)
            pe.wait_ge(s_ws, 1)
            for n, (kind, p, c) in enumerate(prods):
                if n >= 8:
                    evacuated(pe, n - 8)
                cols = slice(c * CH, (c + 1) * CH)
                if kind == "q":
                    w, x = waT[:, p * P:(p + 1) * P], xnT[:, cols]
                elif kind == "k":
                    w, x = waT[:, (NP + p) * P:(NP + p + 1) * P], xnT[:, cols]
                elif kind == "v":
                    w, x = xnT[:, p * P:(p + 1) * P], waT[:, 2 * H * HD + c * CH:2 * H * HD + (c + 1) * CH]
                else:
                    w, x = wsT, xnT[:, cols]
                nc.tensor.matmul(banks[n % 8][:, :], w, x, start=True, stop=True).then_inc(s_proj, 1)

            pe.wait_ge(s_stageA, 2)
            pe.wait_ge(s_zpad, 2)

            def mask_scores(t):
                pe.wait_ge(s_zf, 16 * (t + 1))
                k = len(units(t - 1)) if t > 0 else 0
                for c, (a, b) in enumerate(chunks(t)):
                    if t > 0 and c % 2 == 0:
                        pe.wait_ge(s_ttr, first_unit(t - 1) + k + min(c // 2 + 1, k))
                    nc.tensor.matmul(banks[c][:, 0:b - a], zf[0:HD, :], keysT[0:HD, 0, a:b],
                                     start=True, stop=True).then_inc(s_fqk, 1)

            def mask_sums(t):
                pe.wait_ge(s_msk, mask_steps(t))
                k = len(units(t - 1)) if t > 0 else 0
                for c, (a, b) in enumerate(chunks(t)):
                    if t > 0 and c % 2 == 0:
                        pe.wait_ge(s_ttr, first_unit(t - 1) + 2 * k + min(c // 2 + 1, k))
                    nc.tensor.matmul(banks[c][:, 0:b - a], until[:, :], penalty[t % 2][:, a:b],
                                     start=True, stop=True).then_inc(s_fmm, 1)

            def scores(t, h, par, c):
                a, b = chunks(t)[c]
                k = len(units(t))
                pair = h // 2 if isinstance(h, int) else (h - par) // 2
                if c == 0:
                    pe.wait_ge(s_zq[par], 16 * (NP * t + pair + 1))
                if isinstance(h, int) and h == 0:
                    if t == 0:
                        pe.wait_ge(s_fcp, 1)
                    elif c % 2 == 0:
                        before = len(units(t - 1))
                        pe.wait_ge(s_ttr, first_unit(t) - before + min(c // 2 + 1, before))
                elif isinstance(h, int) and h == 2 and t + 1 < NT:
                    pe.wait_ge(s_relu, first_mask_chunk(t + 1) + c + 1)
                elif isinstance(h, int) and h == 3 and t + 1 < NT:
                    pe.wait_ge(s_fcp, first_mask_chunk(t + 1) + c + 1)
                elif c % 2 == 0:
                    pe.wait_ge(s_ttr, first_unit(t) + k * (h - 1) + c // 2 + 1)
                last = nc.tensor.matmul(banks[c][:, 0:b - a], zq[par], keysT[:, ds(pair, 1), a:b].rearrange("p a n -> p (a n)"),
                                        start=True, stop=True)
                if c % 2 or c == len(chunks(t)) - 1:
                    last.then_inc(s_qk, 1)

            def weigh(t, h, par, ahead=None):
                k = len(chunks(t))
                base = first_chunk(t) + k * h
                pe.wait_ge(s_exp, H * t + h + 1)

                def turn(c):
                    a, b = chunks(t)[c]
                    if c == 0 and t > 0:
                        pe.wait_ge(s_yp, t)
                    pe.wait_ge(s_cp, base + c if c == 0 and k % 2 else base + c - 1) if k > 1 or t > 0 or not isinstance(h, int) or h > 0 else None
                    for i in range((b - a) // P):
                        last = nc.tensor.transpose(banks[4 + c % 2][:, i * P:(i + 1) * P],
                                                   logit[par][:, a + i * P:a + (i + 1) * P], ident[:, :])
                    last.then_inc(s_tr, 1)

                def sum_values(c):
                    a, b = chunks(t)[c]
                    pe.wait_ge(s_cp, base + c + 1)
                    if c == 0 and not (t == 0 and isinstance(h, int) and h < 2):
                        pe.wait_ge(s_y, H * t + h - 1)
                    for i in range((b - a) // P):
                        j = a // P + i
                        last = nc.tensor.matmul(banks[6 + par][:, 0:HD], probsT[:, j * P:(j + 1) * P],
                                                values[:, j, ds(h * HD, HD)], start=(j == 0), stop=(j == t))
                    last.then_inc(s_pvc, 1)

                k_ahead = len(chunks(ahead[0])) if ahead else 0
                for c in range(k):
                    turn(c)
                    if c < k_ahead:
                        scores(*ahead, c)
                    if c > 0:
                        sum_values(c - 1)
                for c in range(k, k_ahead):
                    scores(*ahead, c)
                sum_values(k - 1)

            def turn_outputs(t):
                pe.wait_ge(s_y, H * (t + 1))
                pe.wait_ge(s_cp, first_chunk(t + 1))
                for b in range(2):
                    for i in range(4):
                        k = 4 * b + i
                        last = nc.tensor.transpose(banks[4 + b][:, i * P:(i + 1) * P], y[:, k * P:(k + 1) * P], ident[:, :])
                    last.then_inc(s_yt, 1)

            def project(t):
                pe.wait_ge(s_yc, 2 * (t + 1))
                for k in range(NP):
                    last = nc.tensor.matmul(banks[4][:, 0:P], wpT[:, k, :], yT[:, k * P:(k + 1) * P],
                                            start=(k == 0), stop=(k == NP - 1))
                last.then_inc(s_pr, 1)

            mask_scores(0)
            mask_sums(0)
            for h in range(2):
                scores(0, h, h, 0)
            for t in range(NT):
                if t > 0:
                    project(t - 1)
                if t + 1 < NT:
                    mask_scores(t + 1)
                weigh(t, 0, 0, (t, 2, 0))
                if t + 1 < NT:
                    mask_sums(t + 1)
                weigh(t, 1, 1, (t, 3, 1))
                with pe.Fori(1, NP - 1) as p:
                    weigh(t, 2 * p, 0, (t, 2 * p + 2, 0))
                    weigh(t, 2 * p + 1, 1, (t, 2 * p + 3, 1))
                weigh(t, H - 2, 0, (t + 1, 0, 0) if t + 1 < NT else None)
                weigh(t, H - 1, 1)
                turn_outputs(t)
                if t + 1 < NT:
                    for c in range(len(chunks(t + 1))):
                        scores(t + 1, 1, 1, c)
            project(NT - 1)

            def turn_tiles(src, first_bank):
                for b in range(NC4):
                    for i in range(4):
                        last = nc.tensor.transpose(banks[first_bank + b][:, i * P:(i + 1) * P], src(4 * b + i), ident[:, :])
                    last.then_inc(s_tp, 1)

            pe.wait_ge(s_res, NT)
            turn_tiles(lambda t: resT[:, t * P:(t + 1) * P], 0)
            pe.wait_ge(s_ln, NT)
            turn_tiles(lambda t: x1n[:, t, :], 4)
            pe.wait_ge(s_ln, 2 * NT)
            pe.wait_ge(s_te, 4)
            turn_tiles(lambda t: xaT[:, t * P:(t + 1) * P], 0)
            pe.wait_ge(s_cw, 16 * NW)
            pe.wait_ge(s_te, 8)
            for t in range(NT):
                last = nc.tensor.matmul(banks[4][:, t * NE:(t + 1) * NE], x1T[:, t * P:(t + 1) * P], wg, start=True, stop=True)
            last.then_inc(s_lg, 1)
            pe.wait_ge(s_te, 12)
            for c in range(NC4):
                nc.tensor.matmul(banks[c][:, :], wd, xsT[:, c * CH:(c + 1) * CH], start=True, stop=True).then_inc(s_dl, 1)
            pe.wait_ge(s_gt, 1)
            for c in range(NC4):
                nc.tensor.matmul(banks[4 + c][0:2 * NS, :], wbc, xsT[:, c * CH:(c + 1) * CH],
                                 start=True, stop=True).then_inc(s_dl, 1)

            pe.wait_ge(s_z, 2 * NC4)

            def hidden(e, par, c):
                x = x1T[:, c * CH:(c + 1) * CH]
                for f in range(4):
                    m = 4 * c + f
                    if not (isinstance(e, int) and e == 0 and m < 2):
                        pe.wait_ge(s_gu, 4 * NC4 * e + m - 1)
                    cols = slice(f * P, (f + 1) * P)
                    nc.tensor.matmul(banks[2 * (m % 2)][:, :], w1b[par][:, cols], x, start=True, stop=True)
                    nc.tensor.matmul(banks[2 * (m % 2) + 1][:, :], w3b[par][:, cols], x, start=True, stop=True).then_inc(s_h, 1)

            def outputs(e, par, c):
                pe.wait_ge(s_gu, 4 * NC4 * e + 4 * (c + 1))
                if not (isinstance(e, int) and e == 0 and c < 2):
                    pe.wait_ge(s_ac, NC4 * e + c - 1)
                for i in range(4):
                    for f in range(4):
                        last = nc.tensor.matmul(banks[4 + c % 2][:, i * P:(i + 1) * P], guT[c % 2][:, f, i * P:(i + 1) * P],
                                                w2b[par][:, f, :], start=(f == 0), stop=(f == 3))
                last.then_inc(s_eo, 1)

            def expert(e, par):
                pe.wait_ge(s_w[par], 48 * (e // 2 + 1) if isinstance(e, int) else 24 * (e - par) + 48)
                for c in range(NC4):
                    hidden(e, par, c)
                    if c > 0:
                        outputs(e, par, c - 1)
                outputs(e, par, NC4 - 1)

            expert(0, 0)
            expert(1, 1)
            with pe.Fori(1, NE // 2) as p:
                expert(2 * p, 0)
                expert(2 * p + 1, 1)
            expert(NE, 0)

            pe.wait_ge(s_dx, 4)
            pe.wait_ge(s_gu, 4 * NC4 * (NE + 1))
            turn_tiles(lambda t: ssmT[:, t * P:(t + 1) * P], 0)
            pe.wait_ge(s_ln, 3 * NT)
            pe.wait_ge(s_ac, NC4 * (NE + 1))
            turn_tiles(lambda t: dxT[:, t * P:(t + 1) * P], 4)
            pe.wait_ge(s_te, 20)
            for i in range(4 * NC4):
                f, c = divmod(i, NC4)
                if i >= 4:
                    pe.wait_ge(s_ga, i - 3)
                nc.tensor.matmul(banks[i % 4][:, :], w1m[:, f * P:(f + 1) * P], xsT[:, c * CH:(c + 1) * CH],
                                 start=True, stop=True).then_inc(s_ml, 1)
            pe.wait_ge(s_ga, 4 * NC4)
            for c in range(NC4):
                for i in range(4):
                    t = 4 * c + i
                    for f in range(4):
                        last = nc.tensor.matmul(banks[4 + c][:, i * P:(i + 1) * P], hidT[:, f, t * P:(t + 1) * P],
                                                w2m[:, f, :], start=(f == 0), stop=(f == 3))
                last.then_inc(s_m2, 1)

        @block.vector
        def _(dve):
            dve.wait_ge(s_x, 16)
            for t in range(NT):
                nc.vector.bn_stats(stats[:, t, :], xn[:, t, :]).then_inc(s_rs, 1)
            for t in range(NT):
                dve.wait_ge(s_rs, t + 1)
                nc.vector.bn_aggr(mv[:, t, :], stats[:, t, :]).then_inc(s_mv, 1)
            dve.wait_ge(s_mv, NT)
            nc.vector.tensor_scalar(sd.rearrange("p (t o) -> p t o", o=1), mv[:, :, 1:2], EPS, None, ALU.add).then_inc(s_mv, 1)
            dve.wait_ge(s_sd, 1)
            nc.vector.reciprocal(rstd, sd).then_inc(s_rs, 1)
            dve.wait_ge(s_rs, NT + 1)
            for t in range(NT):
                nc.vector.tensor_scalar(xn[:, t, :], xn[:, t, :], mv[:, t, 0:1], rstd[:, t:t + 1],
                                        ALU.subtract, ALU.mult).then_inc(s_xn, 1)
            dve.wait_ge(s_b, 48)
            nc.vector.tensor_scalar(bqn, bqk[:, 0:NP], -0.125, None, ALU.mult).then_inc(s_bq, 1)
            dve.wait_ge(s_wp, 48)
            nc.vector.tensor_scalar(wneg, wsT, 0.0, None, ALU.is_lt).then_inc(s_bq, 1)
            dve.wait_ge(s_bq, 2)
            nc.vector.scalar_tensor_tensor(out=wsT, in0=wsT, scalar=0.0, in1=wneg, op0=ALU.is_gt, op1=ALU.subtract).then_inc(s_ws, 1)
            for i, n in enumerate(by_dve):
                kind, t, c = prods[n]
                dve.wait_ge(s_proj, n + 1)
                cols = slice(c * CH, (c + 1) * CH)
                if kind == "v":
                    nc.vector.tensor_tensor(values[:, t, cols], banks[n % 8][:, :], bv_all[:, cols], ALU.add).then_inc(s_pv_ev, 1)
                else:
                    nc.vector.scalar_tensor_tensor(out=resT[:, cols], in0=resT[:, cols], scalar=bp, in1=banks[n % 8][:, :],
                                                   op0=ALU.add, op1=ALU.add).then_inc(s_pv_ev, 1)
            dve.wait_ge(s_pv_ev, len(by_dve))
            nc.vector.memset(mins[:, 0:4], 0.0).then_inc(s_stageA, 1)
            dve.wait_ge(s_pa, len(by_act))
            nc.vector.memset(mins[:, 4:8], 0.0).then_inc(s_stageA, 1)
            for i in range(2):
                dve.wait_ge(s_qd[i], 16 * (NP * NC4 // 2))

            def logits(t, h, par, steps=()):
                k = len(units(t))
                steps = list(steps)
                base = first_unit(t) + k * h
                for c, (a, b) in enumerate(units(t)):
                    now = len(steps) if c == k - 1 else SPLIT
                    for i in steps[:now]:
                        search(t + 1, i)
                    steps = steps[now:]
                    g = len(chunks(t))
                    if not (isinstance(h, int) and h < 2):
                        dve.wait_ge(s_tr, first_chunk(t) + g * (h - 2) + min(2 * c + 2, g))
                    elif t > 0:
                        g = len(chunks(t - 1))
                        dve.wait_ge(s_tr, first_chunk(t) - g * (2 - h) + min(2 * c + 2, g))
                    dve.wait_ge(s_qk, base + c + 1)
                    nc.vector.memset(mins[:, 4 * par + 2 + c:4 * par + 3 + c], 0.0)
                    nc.vector.tensor_tensor_reduce(logit[par][:, a:b], wide[:, a:b], penalty[t % 2][:, a:b],
                                                   1.0, 3e38, ALU.add, ALU.min,
                                                   mins[:, 4 * par + c:4 * par + c + 1]).then_inc(s_ttr, 1)
                dve.wait_ge(s_ttr, base + k)
                nc.vector.tensor_reduce(bias[:, par:par + 1], mins[:, 4 * par:4 * par + k], AX_X, ALU.min).then_inc(s_mb, 1)

            def recip(t, h, par):
                dve.wait_ge(s_exp, H * t + h + 1)
                if not (t == 0 and isinstance(h, int) and h < 2):
                    dve.wait_ge(s_y, H * t + h - 1)
                nc.vector.reciprocal(rsum[:, par:par + 1], sums[:, par:par + 1]).then_inc(s_rec, 1)

            PER = 3
            AT_FIRST = 1
            AT_HALF = 6
            AT_LAST = 2
            FIN = 5
            STEP_SUM = AT_FIRST + PER * BITS + AT_HALF + AT_LAST + FIN

            def search_base(t):
                return STEP_SUM * sum(searched(u) for u in range(t))

            def keep(t):
                return keep3[:, 0:1] if t == first_searched else keep3[:, 1:2]

            def search_first(t):
                nc.vector.memset(cand, float(1 << (HI_BITS - 1))).then_inc(s_srch, 1)
                dve.wait_ge(s_srch, search_base(t) + AT_FIRST)
                dve.wait_ge(s_half, t - first_searched + 1)

            def search(t, i):
                n = P * (t + 1)
                at = search_base(t) + AT_FIRST + PER * i
                if not isinstance(i, int) or i >= HI_BITS:
                    at = at + (AT_HALF if i_in_lower(i) else 0)
                nc.vector.tensor_scalar(flags[:, 0:n], half[:, 0:n], cand, None, ALU.is_lt, ALU.add, accum_out=count).then_inc(s_srch, 1)
                dve.wait_ge(s_srch, at + 1)
                nc.vector.tensor_scalar(turn_up, count, keep(t), -0.5, ALU.is_lt, ALU.add).then_inc(s_srch, 1)
                dve.wait_ge(s_srch, at + 2)
                nc.vector.scalar_tensor_tensor(out=cand, in0=turn_up, scalar=bits[:, ds(i, 1)], in1=cand, op0=ALU.mult, op1=ALU.add).then_inc(s_srch, 1)
                dve.wait_ge(s_srch, at + 3)

            lower_half = [False]

            def i_in_lower(i):
                return i >= HI_BITS if isinstance(i, int) else lower_half[0]

            def search_half(t):
                n = P * (t + 1)
                at = search_base(t) + AT_FIRST + PER * HI_BITS
                nc.vector.tensor_scalar(upper, cand, -0.5, None, ALU.add).then_inc(s_srch, 1)
                dve.wait_ge(s_srch, at + 1)
                nc.vector.tensor_copy(low.bitcast(U16)[:, 1:2], upper).then_inc(s_srch, 1)
                nc.vector.tensor_scalar(flags[:, 0:n], half[:, 0:n], upper, 65535.0, ALU.is_gt, ALU.mult).then_inc(s_srch, 1)
                dve.wait_ge(s_srch, at + 3)
                nc.vector.scalar_tensor_tensor(out=half[:, 0:n], in0=half[:, 0:n], scalar=upper, in1=halves(t)[0],
                                               op0=ALU.is_equal, op1=ALU.mult).then_inc(s_srch, 1)
                dve.wait_ge(s_srch, at + 4)
                nc.vector.tensor_tensor(half[:, 0:n], half[:, 0:n], flags[:, 0:n], ALU.max).then_inc(s_srch, 1)
                nc.vector.memset(cand, float(1 << (LO_BITS - 1))).then_inc(s_srch, 1)
                dve.wait_ge(s_srch, at + 6)

            def search_last(t):
                at = search_base(t) + AT_FIRST + PER * BITS + AT_HALF
                nc.vector.tensor_scalar(upper, cand, -0.5, None, ALU.add).then_inc(s_srch, 1)
                dve.wait_ge(s_srch, at + 1)
                nc.vector.tensor_copy(low.bitcast(U16)[:, 0:1], upper).then_inc(s_srch, 1)
                dve.wait_ge(s_srch, at + 2)
                nc.vector.memset(need, 0.0).then_inc(s_low, 1)

            def rank_equals(t):
                n = P * (t + 1)
                at = search_base(t + 1) - FIN
                dve.wait_ge(s_side, t - first_searched + 1)
                nc.vector.tensor_scalar(rank[:, 0:n], side[:, 0:n], 0.0, None, ALU.is_equal).then_inc(s_srch, 1)
                dve.wait_ge(s_srch, at + 1)
                nc.vector.tensor_tensor_scan(rank[:, 0:n], rank[:, 0:n], rank[:, 0:n], 0.0, ALU.add, ALU.max).then_inc(s_srch, 1)
                dve.wait_ge(s_srch, at + 2)

            def prune(t):
                n = P * (t + 1)
                at = search_base(t + 1) - FIN + 2
                nc.vector.tensor_tensor(need, rank[:, n - 1:n], balance, ALU.subtract).then_inc(s_srch, 1)
                dve.wait_ge(s_srch, at + 1)
                nc.vector.tensor_scalar(need, need, 0.5, keep3[:, 2 + t:3 + t], ALU.mult, ALU.add).then_inc(s_srch, 1)
                dve.wait_ge(s_srch, at + 2)
                nc.vector.scalar_tensor_tensor(out=rank[:, 0:n], in0=rank[:, 0:n], scalar=need, in1=side[:, 0:n],
                                               op0=ALU.is_gt, op1=ALU.subtract).then_inc(s_srch, 1)
                dve.wait_ge(s_srch, at + 3)
                pen = penalty[t % 2][:, 0:n]
                if t + 1 < NT:
                    dve.wait_ge(s_row, 16 * (t + 1))
                nc.vector.scalar_tensor_tensor(out=pen, in0=rank[:, 0:n], scalar=BIG, in1=pen, op0=ALU.mult, op1=ALU.max).then_inc(s_fin, 1)

            for t in range(NT):
                ahead = t + 1 < NT
                look = ahead and searched(t + 1)
                dve.wait_ge(s_big, t + 1)
                if searched(t):
                    dve.wait_ge(s_dg, t - first_searched + 1)

                def slot(h, par, first_step=None, t=t):
                    logits(t, h, par, () if first_step is None else [first_step + i for i in range(STEPS)])
                    recip(t, h - 1, 1 - par)

                logits(t, 0, 0)
                slot(1, 1)
                if t > 0:
                    dve.wait_ge(s_yp, t)
                    cols = slice((t - 1) * P, t * P)
                    nc.vector.tensor_tensor(resT[:, cols], resT[:, cols], yP, ALU.add).then_inc(s_res, 1)
                slot(2, 0)
                slot(3, 1)
                if look:
                    search_first(t + 1)
                lower_half[0] = False
                with dve.Fori(2, 4) as p:
                    slot(2 * p, 0, 2 * STEPS * p - 4 * STEPS if look else None)
                    slot(2 * p + 1, 1, 2 * STEPS * p - 3 * STEPS if look else None)
                slot(8, 0, 4 * STEPS if look else None)
                if look:
                    search_half(t + 1)
                slot(9, 1)
                lower_half[0] = True
                with dve.Fori(5, 7) as p:
                    slot(2 * p, 0, 2 * STEPS * p - 5 * STEPS if look else None)
                    slot(2 * p + 1, 1, 2 * STEPS * p - 4 * STEPS if look else None)
                slot(14, 0, 9 * STEPS if look else None)
                if look:
                    search(t + 1, BITS - 1)
                    search_last(t + 1)
                slot(15, 1)
                if look:
                    rank_equals(t + 1)
                    prune(t + 1)
                elif ahead:
                    nc.vector.memset(need, 0.0).then_inc(s_fin, 1)
                recip(t, H - 1, 1)
            dve.wait_ge(s_yp, NT)
            cols = slice((NT - 1) * P, NT * P)
            nc.vector.tensor_tensor(resT[:, cols], resT[:, cols], yP, ALU.add).then_inc(s_res, 1)

            def layer_norm(n, src, dst):
                at = STAT * n
                for t in range(NT):
                    nc.vector.bn_stats(st2[:, t, :], src(t)).then_inc(s_stat, 1)
                for t in range(NT):
                    dve.wait_ge(s_stat, at + t + 1)
                    nc.vector.bn_aggr(mv2[:, t, :], st2[:, t, :]).then_inc(s_stat, 1)
                dve.wait_ge(s_stat, at + 2 * NT)
                nc.vector.tensor_scalar(sd2.rearrange("p (t o) -> p t o", o=1), mv2[:, :, 1:2], EPS, None, ALU.add).then_inc(s_stat, 1)
                dve.wait_ge(s_sq, n + 1)
                nc.vector.reciprocal(rs2, sd2).then_inc(s_stat, 1)
                dve.wait_ge(s_stat, at + STAT)
                for t in range(NT):
                    nc.vector.tensor_scalar(dst(t), src(t), mv2[:, t, 0:1], rs2[:, t:t + 1],
                                            ALU.subtract, ALU.mult).then_inc(s_ln, 1)

            dve.wait_ge(s_te, 4)
            layer_norm(0, lambda t: x1[:, t, :], lambda t: x1n[:, t, :])
            dve.wait_ge(s_ln, NT)
            layer_norm(1, lambda t: x1n[:, t, :], lambda t: xaT[:, t * P:(t + 1) * P])
            nc.vector.tensor_tensor(acc, x1, b2all.rearrange("p (o c) -> p o c", o=1).to_broadcast([P, NT, C]), ALU.add).then_inc(s_ac0, 1)

            dve.wait_ge(s_lg, 1)
            gates = [0]

            def gstep(ins):
                gates[0] += 1
                ins.then_inc(s_gt, 1)
                dve.wait_ge(s_gt, gates[0])

            logits8 = banks[4][:, 0:NT * NE].rearrange("p (t e) -> p t e", t=NT)
            gstep(nc.vector.tensor_copy(prob, logits8))
            nc.vector.tensor_reduce(top, prob, AX_X, ALU.max).then_inc(s_gm, 1)
            dve.wait_ge(s_gm, 1)
            gstep(nc.vector.tensor_tensor(prob, prob, top.to_broadcast([P, NT, NE]), ALU.subtract))
            dve.wait_ge(s_ge, 1)
            gstep(nc.vector.tensor_reduce(top, prob, AX_X, ALU.add))
            gstep(nc.vector.reciprocal(top, top))
            gstep(nc.vector.tensor_tensor(prob, prob, top.to_broadcast([P, NT, NE]), ALU.mult))
            for e in range(NE):
                mine = prob[:, :, e:e + 1]
                gstep(nc.vector.tensor_tensor(cmp[:, :, e:NE], prob[:, :, e:NE], mine.to_broadcast([P, NT, NE - e]), ALU.is_gt))
                if e:
                    gstep(nc.vector.tensor_tensor(cmp[:, :, 0:e], prob[:, :, 0:e], mine.to_broadcast([P, NT, e]), ALU.is_ge))
                gstep(nc.vector.tensor_reduce(rnk[:, :, e:e + 1], cmp, AX_X, ALU.add))
            gstep(nc.vector.tensor_scalar(keptw, rnk, 2.0, 0.5, ALU.is_lt, ALU.mult))
            gstep(nc.vector.memset(gate, 0.5 / 8))
            gstep(nc.vector.tensor_tensor(gate[:, :, 0:NE], keptw, prob, ALU.mult))

            dve.wait_ge(s_sp, 4)
            nc.vector.scalar_tensor_tensor(out=delta, in0=delta, scalar=0.0, in1=absz, op0=ALU.max, op1=ALU.add).then_inc(s_dx, 1)
            dve.wait_ge(s_dx, 1)
            nc.vector.tensor_tensor(dxT, delta, xsT, ALU.mult).then_inc(s_dx, 1)
            nc.vector.scalar_tensor_tensor(out=ssmT, in0=xsT, scalar=dskip, in1=x1T, op0=ALU.mult, op1=ALU.add).then_inc(s_yi, 1)
            nc.vector.tensor_scalar(rate, rate, -1.0, None, ALU.mult).then_inc(s_dx, 1)
            dve.wait_ge(s_yi, 1)

            def scan(n, j, k):
                if k == 0:
                    dve.wait_ge(s_an, n + 1)
                    dve.wait_ge(s_bx, n + 1)
                    nc.vector.tensor_tensor_scan(state[j], decay[j], state[j], 0.0, ALU.mult, ALU.add).then_inc(s_sc, 1)
                elif k == 1:
                    dve.wait_ge(s_sc, n + 1)
                    dve.wait_ge(s_cb[j], 16 * (n // 2 + 1) if isinstance(n, int) else 8 * (n - j) + 16)
                    nc.vector.tensor_tensor(state[j], state[j], rowC[j], ALU.mult).then_inc(s_hc, 1)
                else:
                    dve.wait_ge(s_hc, n + 1)
                    dve.wait_ge(s_ya, n)
                    nc.vector.tensor_tensor(ssmT, ssmT, state[j], ALU.add).then_inc(s_ya, 1)

            def gated(e, c):
                if not (isinstance(e, int) and e == 0 and c < 2):
                    dve.wait_ge(s_eo, NC4 * e + c - 1)
                for f in range(4):
                    m = 4 * c + f
                    dve.wait_ge(s_si, 4 * NC4 * e + m + 1)
                    nc.vector.tensor_tensor(guT[c % 2][:, f, :], silu[m % 2], banks[2 * (m % 2) + 1][:, :], ALU.mult).then_inc(s_gu, 1)

            def add_up(e, c):
                dve.wait_ge(s_eo, NC4 * e + c + 1)
                if not (isinstance(e, int) and e == 0):
                    dve.wait_ge(s_ac, NC4 * (e - 1) + c + 1)
                for i in range(4):
                    t = 4 * c + i
                    last = nc.vector.scalar_tensor_tensor(
                        out=acc[:, t, :], in0=banks[4 + c % 2][:, i * P:(i + 1) * P],
                        scalar=gate[:, t, ds(e, 1)], in1=acc[:, t, :], op0=ALU.mult, op1=ALU.add)
                last.then_inc(s_ac, 1)

            def expert(e, scans):
                for c in range(NC4):
                    gated(e, c)
                    if c > 0:
                        add_up(e, c - 1)
                    for n, j, k in scans[c]:
                        scan(n, j, k)
                add_up(e, NC4 - 1)

            def steps(n):
                return [[(n, 0, 0), (n, 0, 1)], [(n + 1, 1, 0)], [(n, 0, 2), (n + 1, 1, 1)], [(n + 1, 1, 2)]]

            dve.wait_ge(s_ac0, 1)
            for e in range(2):
                expert(e, steps(2 * e))
            with dve.Fori(1, NE // 2) as p:
                expert(2 * p, steps(4 * p))
                expert(2 * p + 1, steps(4 * p + 2))
            expert(NE, [[]] * NC4)

            dve.wait_ge(s_ya, NS)
            nc.vector.memset(sd2, 0.0).then_inc(s_dx, 1)
            dve.wait_ge(s_dx, 4)
            dve.wait_ge(s_te, 16)
            layer_norm(2, lambda t: x1n[:, t, :], lambda t: dxT[:, t * P:(t + 1) * P])
            dve.wait_ge(s_ac, NC4 * (NE + 1))
            nc.vector.tensor_tensor(acc, acc, x1n, ALU.add).then_inc(s_ac0, 1)
            dve.wait_ge(s_ac0, 2)
            for c in range(NC4):
                dve.wait_ge(s_m2, c + 1)
                part4 = acc[:, 4 * c:4 * c + 4, :]
                nc.vector.tensor_tensor(part4, part4, banks[4 + c][:, :].rearrange("p (t c) -> p t c", t=4), ALU.add).then_inc(s_o, 1)


def constants():
    bits = np.concatenate([2.0 ** np.arange(n - 1, -1, -1) for n in (HI_BITS, LO_BITS)])
    bits = np.broadcast_to(bits.astype(np.float32), (P, BITS))
    keep = np.full((P, 2 + NT), BUDGET, np.float32)
    t3 = BUDGET // P
    keep[:, 0] = np.minimum(BUDGET, t3 * P + np.arange(P) + 1)
    for t in range(NT):
        keep[:, 2 + t] = keep[:, 0 if t == t3 else 1] - P * (t + 1) / 2
    return {"c_ident": np.eye(P, dtype=np.float32), "c_until": np.triu(np.ones((P, P), np.float32)),
            "c_ones": np.ones((P, P), np.float32), "c_bits": bits, "c_keep": keep}


def layout(x):
    c = np.ascontiguousarray
    g = lambda n: np.asarray(x[n])
    X = g("L0_attn_x")[0]
    a = {"x": X, "xT": X.T, "W_attnT": g("L0_attn_W_attn").T, "b_qkT": g("L0_attn_b_attn")[:2 * H * HD].reshape(-1, P).T,
         "b_v": g("L0_attn_b_attn")[None, 2 * H * HD:], "W_projT": g("L0_attn_W_proj").T, "b_proj": g("L0_attn_b_proj")[:, None],
         "W_signT": g("L0_ffn_weight").T}
    col = lambda n: g(n)[:, None]
    a.update({"W1T": g("L1_attn_W1").T, "W2T": g("L1_attn_W2").T, "WdT": g("L1_attn_Wd").T, "WbcT": g("L1_attn_Wbc").T,
              "gate_WT": g("L1_ffn_gate_W").T, "b2": g("L1_attn_b2")[None], "ln1_g": col("L1_attn_ln1_g"),
              "ln1_b": col("L1_attn_ln1_b"), "bd": col("L1_attn_bd"), "D": col("L1_attn_D"), "ln2_g": col("L1_attn_ln2_g"),
              "ln2_b": col("L1_attn_ln2_b"), "b1T": g("L1_attn_b1").reshape(4, P).T, "bbc": col("L1_attn_bbc"),
              "A_log": g("L1_attn_A_log")})
    ns, d, fs = g("L1_ffn_w1_s").shape
    beside = lambda w: w.transpose(1, 0, 2).reshape(1, d, ns * fs)
    a["w1"] = np.concatenate([g("L1_ffn_w1_e"), beside(g("L1_ffn_w1_s"))])
    a["w3"] = np.concatenate([g("L1_ffn_w3_e"), beside(g("L1_ffn_w3_s"))])
    a["w2"] = np.concatenate([g("L1_ffn_w2_e"), g("L1_ffn_w2_s").reshape(1, ns * fs, d)])
    a.update(constants())
    return {k: c(v) for k, v in a.items()}


def kernel(**inputs):
    import concourse.bacc as bacc
    from concourse.bass_utils import run_bass_kernel_spmd

    arrays = layout(inputs)
    nc = bacc.Bacc("TRN2", target_bir_lowering=False, num_devices=1)
    aps = {n: nc.dram_tensor(n, a.shape, mybir.dt.from_np(a.dtype), kind="ExternalInput").ap() for n, a in arrays.items()}
    out = nc.dram_tensor("out", (1, T, C), F32, kind="ExternalOutput").ap()
    build(nc, aps, out)
    return run_bass_kernel_spmd(nc, [arrays], core_ids=[0]).results[0]["out"]
```

```python
from contextlib import ExitStack

import numpy as np

import concourse.bass as bass
from concourse import mybir

F32 = mybir.dt.float32
U16 = mybir.dt.uint16
F16 = mybir.dt.float16
ALU = mybir.AluOpType
ACT = mybir.ActivationFunctionType
AX_X = mybir.AxisListType.X
ds = bass.ds

P = 128
T = 2048
C = 128
H = 16
HD = 64
NP = H // 2
NT = T // P
CH = 512
NC4 = T // CH
BUDGET = int(T * 0.2) - 1
BIG = 1e30
EPS = 1e-5
HI_BITS = 15
LO_BITS = 16
BITS = HI_BITS + LO_BITS
NS = 16
NE = 8
F = 512


def chunks(t):
    n = P * (t + 1)
    return [(c, min(c + CH, n)) for c in range(0, n, CH)]


def units(t):
    n = P * (t + 1)
    return [(c, min(c + 2 * CH, n)) for c in range(0, n, 2 * CH)]


def first_unit(t):
    return sum(H * len(units(u)) for u in range(t))


def first_chunk(t):
    return sum(H * len(chunks(u)) for u in range(t))


def first_mask_chunk(t):
    return sum(len(chunks(u)) for u in range(t))


def mask_steps(t):
    return 2 * (t + 1)


def searched(t):
    return P * (t + 1) > BUDGET


def build(nc, A, out):
    with ExitStack() as ctx:
        def sb(name, shape, dt=F32):
            return ctx.enter_context(nc.sbuf_tensor(name, shape, dt))

        def sem(name):
            return ctx.enter_context(nc.semaphore(name))

        wide = ctx.enter_context(nc.psum_tensor("wide", [P, 8 * CH], F32))
        banks = [wide[:, i * CH:(i + 1) * CH] for i in range(8)]

        q_dram = nc.dram_tensor("q_dram", [NP, P, T], F32).ap()
        q0_dram = nc.dram_tensor("q0_dram", [HD, T + 1], F32).ap()
        bc_dram = nc.dram_tensor("bc_dram", [2 * NS, T], F32).ap()

        keysT = sb("keysT", [P, NP, T])
        values = sb("values", [P, NT, H * HD])
        resT = sb("resT", [P, T])
        wpT = sb("wpT", [P, NP, C])
        ident = sb("ident", [P, P])
        until = sb("until", [P, P])
        from_last = sb("from_last", [P, P])
        keep3 = sb("keep3", [P, 1 + NT])
        small = sb("small", [P, 256])
        region = sb("region", [P, 15872])

        def part(at, n):
            return region[:, at:at + n]

        waT = part(0, 3 * H * HD)
        xn = part(3072, T).rearrange("p (t c) -> p t c", t=NT)
        xnT = part(5120, T)
        q_stage = [part(7168 + CH * i, CH) for i in range(2)]
        bv_all = part(8192, H * HD)
        wsT = part(9216, C)
        wneg = part(9344, C)
        logit = [part(T * i, T) for i in range(2)]
        penalty = [part(2 * T + T * i, T) for i in range(3)]
        half = part(5 * T, T // 2).bitcast(U16)
        flags = part(5 * T + T // 2, T // 2).bitcast(U16)
        side = part(5 * T, T // 2).bitcast(F16)
        rank = part(5 * T + T // 2, T // 2).bitcast(F16)
        at = 6 * T
        probsT = [part(at + CH * i, CH) for i in range(2)]
        y = part(at + 2 * CH, H * HD)
        yT = part(at + 2 * CH + H * HD, H * HD)
        at += 2 * CH + 2 * H * HD
        zq = [part(at + P * i, P) for i in range(2)]
        zf = part(at + 2 * P, P)
        yP = part(at + 3 * P, P)

        stats = small[:, 0:96].rearrange("p (t s) -> p t s", t=NT)
        mv = small[:, 96:128].rearrange("p (t s) -> p t s", t=NT)
        rstd = small[:, 128:144]
        bqk = small[:, 144:160]
        bqn = small[:, 160:168]
        bp = small[:, 168:169]
        mins = small[:, 170:178]
        bias = small[:, 178:180]
        part_sums = small[:, 180:184]
        sums = small[:, 209:211]
        rsum = small[:, 211:213]
        low = small[:, 184:185]
        cand = small[:, 185:186]
        count = small[:, 186:187]
        turn_up = small[:, 187:188]
        need = small[:, 188:189]
        upper = small[:, 189:190]
        balance = small[:, 190:191]
        sd = small[:, 192:208]
        zero = small[:, 208:209]

        L = sem
        s_cst, s_x, s_wa, s_b, s_wp = L("s_cst"), L("s_x"), L("s_wa"), L("s_b"), L("s_wp")
        s_zero, s_mv, s_sd, s_rs, s_xn, s_xt = L("s_zero"), L("s_mv"), L("s_sd"), L("s_rs"), L("s_xn"), L("s_xt")
        s_xnT, s_bq, s_ws, s_proj, s_pa, s_pv_ev = L("s_xnT"), L("s_bq"), L("s_ws"), L("s_proj"), L("s_pa"), L("s_pv_ev")
        s_qd = [L("s_qd0"), L("s_qd1")]
        s_q0 = [L("s_q00"), L("s_q01")]
        s_q0z = L("s_q0z")
        s_stageA = L("s_stageA")

        def halves(t):
            both = penalty[t % 3][:, 0:P * (t + 1)].bitcast(U16).rearrange("p (n two) -> p n two", two=2)
            return both[:, :, 0:1].rearrange("p n a -> p (n a)"), both[:, :, 1:2].rearrange("p n a -> p (n a)")

        first_searched = min(t for t in range(NT) if searched(t))
        block = ctx.enter_context(nc.Block())

        others = [("k", p, c) for p in range(NP) for c in range(NC4)]
        others = [x for pair in zip(others, [("v", t, c) for t in range(NT) for c in range(2)]) for x in pair]
        prods = []
        for i in range(NP * NC4):
            prods.append(("q", *divmod(i, NC4)))
            for _ in range(1 + i % 2):
                prods.append(others.pop(0))
        prods += others + [("s", 0, c) for c in range(NC4)]
        by_act = [n for n, x in enumerate(prods) if x[0] in "qk"]
        by_dve = [n for n, x in enumerate(prods) if x[0] in "vs"]

        def evacuated(eng, n):
            if n in by_act:
                eng.wait_ge(s_pa, by_act.index(n) + 1)
            else:
                eng.wait_ge(s_pv_ev, by_dve.index(n) + 1)

        s_zq = [L("s_zq0"), L("s_zq1")]
        s_zpad = L("s_zpad")
        s_qk = L("s_qk")
        s_ttr = L("s_ttr")
        s_mb = L("s_mb")
        s_exp = L("s_exp")
        s_tr = L("s_tr")
        s_cp = L("s_cp")
        s_pvc = L("s_pvc")
        s_sum = L("s_sum")
        s_rec = L("s_rec")
        s_y = L("s_y")
        s_zf = L("s_zf")
        s_fqk = L("s_fqk")
        s_relu = L("s_relu")
        s_msk = L("s_msk")
        s_fmm = L("s_fmm")
        s_fcp = L("s_fcp")
        s_big = L("s_big")
        s_srch = L("s_srch")
        s_fin = L("s_fin")
        s_half = L("s_half")
        s_low = L("s_low")
        s_side = L("s_side")
        s_dg = L("s_dg")
        s_yt = L("s_yt")
        s_yc = L("s_yc")
        s_pr = L("s_pr")
        s_yp = L("s_yp")
        s_res = L("s_res")

        kv = keysT[:, :, :].rearrange("p a n -> p (a n)")
        vv = values[:, :, :].rearrange("p a n -> p (a n)")

        def tiles(x):
            return x.rearrange("p (t c) -> p t c", t=NT)

        x1n, x1T = tiles(kv[:, 0:T]), kv[:, T:2 * T]
        xsT = kv[:, 2 * T:3 * T]
        delta, dxT = kv[:, 3 * T:4 * T], kv[:, 4 * T:5 * T]
        decay = [kv[:, (5 + i) * T:(6 + i) * T] for i in range(2)]
        acc = tiles(kv[:, 7 * T:8 * T])
        rowB = [vv[:, i * T:(i + 1) * T] for i in range(2)]
        rowC = [vv[:, (2 + i) * T:(3 + i) * T] for i in range(2)]
        state = [vv[:, (4 + i) * T:(5 + i) * T] for i in range(2)]
        ssmT = vv[:, 6 * T:7 * T]
        bcT = vv[:, 7 * T:8 * T]
        xaT = vv[:, 0:T]
        absz = vv[:, 2 * T:3 * T]
        hidT = vv[:, 0:4 * T].rearrange("p (f n) -> p f n", f=4)
        guT = [part(4 * CH * i, 4 * CH).rearrange("p (f n) -> p f n", f=4) for i in range(2)]
        w1b = [part(4096 + 1536 * i, F) for i in range(2)]
        w3b = [part(4608 + 1536 * i, F) for i in range(2)]
        w2b = [part(5120 + 1536 * i, F).rearrange("p (f c) -> p f c", f=4) for i in range(2)]
        silu = [part(at, CH) for at in (7168, 7168 + CH, 13000)]
        w1m = part(8192, F)
        w2m = part(8704, F).rearrange("p (f c) -> p f c", f=4)
        wd, wbc, wg = part(9216, C), part(9344, 2 * NS), part(9376, NE)
        b2all = part(9384, C)
        x1 = tiles(part(9512, T))
        scr = part(11560, 8 * P)
        prob, keptw, cmp = (scr[:, P * i:P * (i + 1)].rearrange("p (t e) -> p t e", t=NT) for i in range(3))
        gate = scr[:, 3 * P:3 * P + NT * (NE + 1)].rearrange("p (t e) -> p t e", t=NT)
        top = scr[:, 640:640 + NT].rearrange("p (t o) -> p t o", o=1)
        rnk = scr[:, 656:656 + P].rearrange("p (t e) -> p t e", t=NT)
        vecs = part(12600, 64)
        ln1g, ln1b, bd, dskip, ln2g, ln2b, b1 = (vecs[:, a:b] for a, b in
                                                 ((0, 1), (1, 2), (2, 3), (3, 4), (4, 5), (5, 6), (6, 10)))
        bbc = vecs[:, 10:11]
        rate = vecs[:, 16:32]
        st2 = part(12700, 96).rearrange("p (t s) -> p t s", t=NT)
        mv2 = part(12800, 32).rearrange("p (t s) -> p t s", t=NT)
        sd2, rs2 = part(12832, NT), part(12848, NT)

        s_cw = L("s_cw")
        s_stat = L("s_stat")
        s_sq = L("s_sq")
        s_ln = L("s_ln")
        s_tp = L("s_tp")
        s_te = L("s_te")
        s_lg = L("s_lg")
        s_gt = L("s_gt")
        s_ge = L("s_ge")
        s_dl = L("s_dl")
        s_z = L("s_z")
        s_sp = L("s_sp")
        s_dx = L("s_dx")
        s_bcd = L("s_bcd")
        s_w = [L("s_w0"), L("s_w1")]
        s_bb = [L("s_bb0"), L("s_bb1")]
        s_cb = [L("s_cb0"), L("s_cb1")]
        s_an = L("s_an")
        s_bx = L("s_bx")
        s_sc = L("s_sc")
        s_hc = L("s_hc")
        s_ya = L("s_ya")
        s_h = L("s_h")
        s_si = L("s_si")
        s_gu = L("s_gu")
        s_eo = L("s_eo")
        s_ac = L("s_ac")
        s_ml = L("s_ml")
        s_ga = L("s_ga")
        s_m2 = L("s_m2")
        s_o = L("s_o")
        s_out = L("s_out")

        s_ac0 = L("s_ac0")
        s_gm = L("s_gm")
        s_yi = L("s_yi")
        STAT = 2 * NT + 2
        NW = 15

        @block.sync
        def _(sp):
            sp.dma_start(xn, A["x"].rearrange("(t p) c -> p t c", p=P)).then_inc(s_x, 16)
            sp.dma_start(waT, A["W_attnT"]).then_inc(s_wa, 16)
            for dst, src in ((ident[:, :], A["c_ident"]), (until[:, :], A["c_until"]),
                             (from_last[:, :], A["c_last"]),
                             (keep3[:, :], A["c_keep"])):
                sp.dma_start(dst, src).then_inc(s_cst, 16)
            sp.dma_start(bqk, A["b_qkT"]).then_inc(s_b, 16)
            sp.dma_start(bp, A["b_proj"]).then_inc(s_b, 16)
            sp.dma_start(bv_all, A["b_v"].to_broadcast([P, H * HD])).then_inc(s_b, 16)
            sp.dma_start(wsT, A["W_signT"]).then_inc(s_wp, 16)
            sp.dma_start(resT[:, :], A["xT"]).then_inc(s_wp, 16)
            sp.dma_start(wpT[:, :, :], A["W_projT"].rearrange("(k p) c -> p k c", p=P)).then_inc(s_wp, 16)
            sp.wait_ge(s_zero, 1)
            with nc.allow_non_contiguous_dma(reason="one column"):
                sp.dma_start(q0_dram[:, 0:1], zero[0:HD, :]).then_inc(s_q0z, 16)
            for i in range(NP * NC4):
                p, c = divmod(i, NC4)
                n = prods.index(("q", p, c))
                evacuated(sp, n)
                sp.dma_start(q_dram[p, :, c * CH:(c + 1) * CH], q_stage[i % 2]).then_inc(s_qd[i % 2], 16)
                if p == 0:
                    sp.dma_start(q0_dram[:, 1 + c * CH:1 + (c + 1) * CH], q_stage[i % 2][0:HD, :]).then_inc(s_q0[i % 2], 16)

            def load_zf(t):
                if t > 0:
                    sp.wait_ge(s_fqk, first_mask_chunk(t))
                sp.dma_start(zf[0:HD, :], q0_dram[:, t * P:(t + 1) * P]).then_inc(s_zf, 16)

            def load_zq(t, h, par):
                if not (t == 0 and isinstance(h, int) and h < 2):
                    prev = first_unit(t) + len(units(t)) * (h - 1)
                    if isinstance(h, int) and h < 2:
                        prev = first_unit(t) - len(units(t - 1)) * (1 - h)
                    sp.wait_ge(s_qk, prev)
                pair = h // 2 if isinstance(h, int) else (h - par) // 2
                dst = zq[par][HD * par:HD * par + HD, :]
                src = q_dram[ds(pair, 1), HD * par:HD * par + HD, t * P:(t + 1) * P]
                sp.dma_start(dst, src.rearrange("a p n -> (a p) n")).then_inc(s_zq[par], 16)

            sp.wait_ge(s_q0z, 16)
            for i in range(2):
                sp.wait_ge(s_q0[i], 16 * (NC4 // 2))
                sp.wait_ge(s_qd[i], 16 * (NP * NC4 // 2))
            sp.wait_ge(s_zpad, 2)
            load_zf(0)
            load_zq(0, 0, 0)
            load_zq(0, 1, 1)
            load_zf(1)
            for t in range(NT):
                if t + 2 < NT:
                    load_zf(t + 2)
                with sp.Fori(1, NP) as p:
                    load_zq(t, 2 * p, 0)
                    load_zq(t, 2 * p + 1, 1)
                if t + 1 < NT:
                    load_zq(t + 1, 0, 0)
                    load_zq(t + 1, 1, 1)
            sp.wait_ge(s_res, NT)
            sp.wait_ge(s_pvc, first_chunk(NT))
            for dst, src in ((w1m, A["W1T"]), (w2m, A["W2T"].rearrange("(f p) c -> p f c", p=P)), (wd, A["WdT"]),
                             (wbc, A["WbcT"]), (wg, A["gate_WT"]), (b2all, A["b2"].to_broadcast([P, C])),
                             (ln1g, A["ln1_g"]), (ln1b, A["ln1_b"]), (bd, A["bd"]), (dskip, A["D"]),
                             (ln2g, A["ln2_g"]), (ln2b, A["ln2_b"]), (b1, A["b1T"]),
                             (bbc[0:2 * NS, :], A["bbc"]), (rate, A["A_log"])):
                sp.dma_start(dst, src).then_inc(s_cw, 16)

            def weights(e, par):
                if not (isinstance(e, int) and e < 2):
                    sp.wait_ge(s_eo, NC4 * (e - 1))
                for dst, name in ((w1b[par], "w1"), (w3b[par], "w3")):
                    sp.dma_start(dst, A[name][ds(e, 1), :, :].rearrange("a p f -> (a p) f")).then_inc(s_w[par], 16)
                sp.dma_start(w2b[par], A["w2"][ds(e, 1), :, :].rearrange("a (f p) c -> (a p) f c", p=P)).then_inc(s_w[par], 16)

            def rows(n, j):
                if not (isinstance(n, int) and n < 2):
                    sp.wait_ge(s_bx, n - 1)
                sp.dma_start(rowB[j], bc_dram[ds(n, 1), :].to_broadcast([P, T])).then_inc(s_bb[j], 16)
                if not (isinstance(n, int) and n < 2):
                    sp.wait_ge(s_hc, n - 1)
                sp.dma_start(rowC[j], bc_dram[ds(NS + n, 1), :].to_broadcast([P, T])).then_inc(s_cb[j], 16)

            weights(0, 0)
            weights(1, 1)
            sp.wait_ge(s_z, 2 * NC4)
            sp.dma_start(bc_dram, bcT[0:2 * NS, :]).then_inc(s_bcd, 16)
            sp.wait_ge(s_bcd, 16)
            sp.wait_ge(s_dx, 1)
            for j in range(2):
                rows(j, j)
            rows(2, 0)
            rows(3, 1)
            with sp.Fori(1, NE // 2) as p:
                rows(4 * p, 0)
                rows(4 * p + 1, 1)
                weights(2 * p, 0)
                rows(4 * p + 2, 0)
                rows(4 * p + 3, 1)
                weights(2 * p + 1, 1)
            weights(NE, 0)
            for c in range(NC4):
                sp.wait_ge(s_o, c + 1)
                sp.dma_start(out[0].rearrange("(t p) c -> p t c", p=P)[:, 4 * c:4 * c + 4, :],
                             acc[:, 4 * c:4 * c + 4, :]).then_inc(s_out, 16)
            sp.wait_ge(s_out, 16 * NC4)

        @block.gpsimd
        def _(pool):
            nc.gpsimd.memset(zero, 0.0).then_inc(s_zero, 1)
            nc.gpsimd.memset(zq[0], 0.0).then_inc(s_zpad, 1)
            nc.gpsimd.memset(zq[1], 0.0).then_inc(s_zpad, 1)
            def mask(t):
                pen = penalty[t % 3]
                pool.wait_ge(s_relu, first_mask_chunk(t + 1))
                done = mask_steps(t - 1) if t > 0 else 0
                nc.gpsimd.memset(pen[:, 0:1], 0.0).then_inc(s_msk, 1)
                pool.wait_ge(s_msk, done + 1)
                lo = max(0, P * (t - 1))
                w = P * (t + 1) - lo
                nc.gpsimd.affine_select(out=pen[:, lo:lo + w], in_=pen[:, lo:lo + w], compare_op=ALU.is_ge, fill=0.0,
                                        base=P * t - 2 - lo, pattern=[[-1, w]], channel_multiplier=1).then_inc(s_msk, 1)
                pool.wait_ge(s_fcp, first_mask_chunk(t + 1))
                dg = pen[:, P * t:P * (t + 1)]
                nc.gpsimd.affine_select(out=dg, in_=dg, compare_op=ALU.is_ge, fill=BIG,
                                        base=0, pattern=[[-1, P]], channel_multiplier=1).then_inc(s_big, 1)

            def exempt(t):
                pool.wait_ge(s_fin, t - first_searched + 1)
                dg = penalty[t % 3][:, P * t:P * (t + 1)]
                nc.gpsimd.affine_select(out=dg, in_=dg, compare_op=ALU.not_equal, fill=0.0,
                                        base=0, pattern=[[-1, P]], channel_multiplier=1).then_inc(s_dg, 1)

            mask(0)
            mask(1)
            for t in range(NT):
                if t + 2 < NT:
                    mask(t + 2)
                if t + 1 < NT and searched(t + 1):
                    exempt(t + 1)

            def inputs(n, j):
                pool.wait_ge(s_bb[j], 16 * (n // 2 + 1) if isinstance(n, int) else 8 * (n - j) + 16)
                if not (isinstance(n, int) and n < 2):
                    pool.wait_ge(s_ya, n - 1)
                nc.gpsimd.tensor_tensor(state[j], dxT, rowB[j], ALU.mult).then_inc(s_bx, 1)

            pool.wait_ge(s_dx, 2)
            for n in range(4):
                inputs(n, n % 2)
            with pool.Fori(1, NE // 2) as p:
                for n in range(4):
                    inputs(4 * p + n, n % 2)

        @block.scalar
        def _(act):
            act.wait_ge(s_mv, NT + 1)
            nc.scalar.activation(sd, sd, ACT.Sqrt).then_inc(s_sd, 1)
            for b in range(4):
                act.wait_ge(s_xt, b + 1)
                nc.scalar.activation(xnT[:, b * CH:(b + 1) * CH], banks[b][:, :], ACT.Copy).then_inc(s_xnT, 1)
            act.wait_ge(s_bq, 1)
            nq = 0
            for n in by_act:
                kind, p, c = prods[n]
                act.wait_ge(s_proj, n + 1)
                if kind == "q":
                    if nq >= 2:
                        act.wait_ge(s_qd[nq % 2], 16 * (nq // 2))
                        if nq < NC4 + 2:
                            act.wait_ge(s_q0[nq % 2], 16 * (nq // 2))
                    nc.scalar.activation(q_stage[nq % 2], banks[n % 8][:, :], ACT.Identity,
                                         bias=bqn[:, p:p + 1], scale=-0.125).then_inc(s_pa, 1)
                    nq += 1
                else:
                    nc.scalar.activation(keysT[:, p, c * CH:(c + 1) * CH], banks[n % 8][:, :], ACT.Identity,
                                         bias=bqk[:, NP + p:NP + p + 1]).then_inc(s_pa, 1)

            def exps(t, h, par, u):
                a, b = units(t)[u]
                if u == 0:
                    act.wait_ge(s_mb, H * t + h + 1)
                    if t > 0 or not isinstance(h, int) or h >= 2:
                        act.wait_ge(s_rec, H * t + h - 1)
                x = logit[par][:, a:b]
                nc.scalar.activation(x, x, ACT.Exp, bias=bias[:, par:par + 1], scale=-1.0,
                                     accum_out=part_sums[:, 2 * par + u:2 * par + u + 1]).then_inc(s_exp, 1)

            def all_exps(t, h, par):
                for u in range(len(units(t))):
                    exps(t, h, par, u)

            def copy(t, h, c):
                k = len(chunks(t))
                a, b = chunks(t)[c]
                i = first_chunk(t) + k * h + c
                act.wait_ge(s_tr, i + 1)
                if c >= 2 or not (t == 0 and isinstance(h, int) and h == 0):
                    act.wait_ge(s_pvc, i - 1 if c >= 2 else i - c)
                nc.scalar.activation(probsT[c % 2][:, 0:b - a], banks[4 + c % 2][:, 0:b - a], ACT.Copy).then_inc(s_cp, 1)

            def copies(t, h):
                for c in range(len(chunks(t))):
                    copy(t, h, c)

            def outs(t, h, par):
                act.wait_ge(s_pvc, first_chunk(t) + len(chunks(t)) * (h + 1))
                act.wait_ge(s_rec, H * t + h + 1)
                if t > 0:
                    act.wait_ge(s_yt, 2 * t)
                nc.scalar.activation(y[:, ds(h * HD, HD)], banks[6 + par][:, 0:HD], ACT.Copy,
                                     scale=rsum[:, par:par + 1]).then_inc(s_y, 1)

            def sides(t):
                n = P * (t + 1)
                act.wait_ge(s_low, t - first_searched + 1)
                nc.scalar.activation(side[:, 0:n], penalty[t % 3][:, 0:n], ACT.Sign, bias=low, scale=-1.0,
                                     accum_out=balance).then_inc(s_side, 1)

            def mask_relu(t):
                for c, (a, b) in enumerate(chunks(t)):
                    act.wait_ge(s_fqk, first_mask_chunk(t) + c + 1)
                    if c == 0 and t >= 3:
                        act.wait_ge(s_ttr, first_unit(t - 2))
                        if searched(t - 3):
                            act.wait_ge(s_dg, t - 3 - first_searched + 1)
                    nc.scalar.activation(penalty[t % 3][:, a:b], banks[c][:, 0:b - a], ACT.Relu, scale=-1.0).then_inc(s_relu, 1)

            def mask_copy(t):
                for c, (a, b) in enumerate(chunks(t)):
                    act.wait_ge(s_fmm, first_mask_chunk(t) + c + 1)
                    nc.scalar.activation(penalty[t % 3][:, a:b], banks[c][:, 0:b - a], ACT.Copy).then_inc(s_fcp, 1)

            def upper_halves(t):
                n = P * (t + 1)
                act.wait_ge(s_big, t + 1)
                if searched(t - 1):
                    act.wait_ge(s_fin, t - first_searched)
                nc.scalar.activation(half[:, 0:n], halves(t)[1], ACT.Copy).then_inc(s_half, 1)

            for t in range(2):
                mask_relu(t)
                mask_copy(t)
            all_exps(0, 0, 0)
            for t in range(NT):
                def head(h, par, t=t):
                    for c in range(len(chunks(t))):
                        copy(t, h, c)
                        if c % 2 == 1 or c == len(chunks(t)) - 1:
                            exps(t, h + 1, 1 - par, c // 2)
                    outs(t, h, par)

                def two_heads(p):
                    head(2 * p, 0)
                    head(2 * p + 1, 1)

                all_exps(t, 1, 1)
                if t + 2 < NT:
                    mask_relu(t + 2)
                copies(t, 0)
                if t + 1 < NT and searched(t + 1):
                    sides(t + 1)
                outs(t, 0, 0)
                if t + 2 < NT:
                    mask_copy(t + 2)
                copies(t, 1)
                all_exps(t, 2, 0)
                outs(t, 1, 1)
                if t + 2 < NT and searched(t + 2):
                    upper_halves(t + 2)
                with act.Fori(1, NP - 1) as p:
                    two_heads(p)
                head(H - 2, 0)
                copies(t, H - 1)
                outs(t, H - 1, 1)
                if t + 1 < NT:
                    all_exps(t + 1, 0, 0)
                for b in range(2):
                    act.wait_ge(s_yt, 2 * t + b + 1)
                    nc.scalar.activation(yT[:, b * CH:(b + 1) * CH], banks[4 + b][:, :], ACT.Copy).then_inc(s_yc, 1)
                act.wait_ge(s_pr, t + 1)
                if t > 0:
                    act.wait_ge(s_res, t)
                nc.scalar.activation(yP, banks[4][:, 0:P], ACT.Copy).then_inc(s_yp, 1)

            def from_banks(done, dst, first_bank, **affine):
                for b in range(NC4):
                    act.wait_ge(s_tp, done + b + 1)
                    nc.scalar.activation(dst[:, b * CH:(b + 1) * CH], banks[first_bank + b][:, :],
                                         ACT.Identity if affine else ACT.Copy, **affine).then_inc(s_te, 1)

            def silus(e, chunks_of=range(NC4)):
                for c in chunks_of:
                    for f in range(4):
                        m = 4 * c + f
                        i = 4 * NC4 * e + m
                        act.wait_ge(s_h, i + 1)
                        if m >= 3:
                            act.wait_ge(s_gu, i - 2)
                        elif not (isinstance(e, int) and e == 0):
                            act.wait_ge(s_gu, 4 * NC4 * e)
                        nc.scalar.activation(silu[m % 3], banks[2 * (m % 3)][:, :], ACT.Silu).then_inc(s_si, 1)

            def root(n):
                act.wait_ge(s_stat, STAT * n + 2 * NT + 1)
                nc.scalar.activation(sd2, sd2, ACT.Sqrt).then_inc(s_sq, 1)

            from_banks(0, x1.rearrange("p t c -> p (t c)"), 0)
            root(0)
            root(1)
            from_banks(4, x1T, 4)
            act.wait_ge(s_cw, 16 * NW)
            from_banks(8, xsT, 0, bias=ln1b, scale=ln1g)
            act.wait_ge(s_gt, 2)
            nc.scalar.activation(prob, prob, ACT.Exp).then_inc(s_ge, 1)
            nc.scalar.activation(rate, rate, ACT.Exp).then_inc(s_sp, 1)
            for c in range(NC4):
                cols = slice(c * CH, (c + 1) * CH)
                act.wait_ge(s_dl, c + 1)
                nc.scalar.activation(delta[:, cols], banks[c][:, :], ACT.Identity, bias=bd).then_inc(s_z, 1)
            for c in range(NC4):
                cols = slice(c * CH, (c + 1) * CH)
                act.wait_ge(s_dl, NC4 + c + 1)
                nc.scalar.activation(bcT[0:2 * NS, cols], banks[4 + c][0:2 * NS, :], ACT.Identity,
                                     bias=bbc[0:2 * NS, :]).then_inc(s_z, 1)
            silus(0, range(1))
            act.wait_ge(s_z, NC4)
            nc.scalar.activation(absz, delta, ACT.Abs).then_inc(s_sp, 1)
            act.wait_ge(s_sp, 2)
            nc.scalar.activation(absz, absz, ACT.Exp, scale=-1.0).then_inc(s_sp, 1)
            act.wait_ge(s_sp, 3)
            nc.scalar.activation(absz, absz, ACT.Ln, bias=until[:, P - 1:P]).then_inc(s_sp, 1)

            def decays(n, j):
                if not (isinstance(n, int) and n < 2):
                    act.wait_ge(s_sc, n - 1)
                nc.scalar.activation(decay[j], delta, ACT.Exp, scale=rate[:, ds(n, 1)]).then_inc(s_an, 1)

            silus(0, range(1, 2))
            act.wait_ge(s_dx, 3)
            for e in range(2):
                for j in range(2):
                    decays(2 * e + j, j)
                silus(e, range(2 if e == 0 else 0, NC4))
            with act.Fori(1, NE // 2) as p:
                for par in range(2):
                    for j in range(2):
                        decays(4 * p + 2 * par + j, j)
                    silus(2 * p + par)
            from_banks(12, x1n.rearrange("p t c -> p (t c)"), 0)
            silus(NE, range(2))
            root(2)
            silus(NE, range(2, NC4))

            from_banks(16, xsT, 4, bias=ln2b, scale=ln2g)
            for i in range(4 * NC4):
                f, c = divmod(i, NC4)
                act.wait_ge(s_ml, i + 1)
                nc.scalar.activation(hidT[:, f, c * CH:(c + 1) * CH], banks[i % 4][:, :], ACT.Gelu,
                                     bias=b1[:, f:f + 1]).then_inc(s_ga, 1)

        @block.tensor
        def _(pe):
            pe.wait_ge(s_cst, 16 * 4)
            for b in range(4):
                for i in range(4):
                    t = 4 * b + i
                    pe.wait_ge(s_xn, t + 1)
                    last = nc.tensor.transpose(banks[b][:, i * P:(i + 1) * P], xn[:, t, :], ident[:, :])
                last.then_inc(s_xt, 1)
            pe.wait_ge(s_wa, 16)
            pe.wait_ge(s_xnT, 4)
            pe.wait_ge(s_ws, 1)
            for n, (kind, p, c) in enumerate(prods):
                if n >= 8:
                    evacuated(pe, n - 8)
                cols = slice(c * CH, (c + 1) * CH)
                if kind == "q":
                    w, x = waT[:, p * P:(p + 1) * P], xnT[:, cols]
                elif kind == "k":
                    w, x = waT[:, (NP + p) * P:(NP + p + 1) * P], xnT[:, cols]
                elif kind == "v":
                    w, x = xnT[:, p * P:(p + 1) * P], waT[:, 2 * H * HD + c * CH:2 * H * HD + (c + 1) * CH]
                else:
                    w, x = wsT, xnT[:, cols]
                nc.tensor.matmul(banks[n % 8][:, :], w, x, start=True, stop=True).then_inc(s_proj, 1)

            pe.wait_ge(s_stageA, 2)
            pe.wait_ge(s_zpad, 2)

            def mask_scores(t):
                pe.wait_ge(s_zf, 16 * (t + 1))
                if t == 1:
                    pe.wait_ge(s_fcp, 1)
                k = len(units(t - 2)) if t > 1 else 0
                for c, (a, b) in enumerate(chunks(t)):
                    if t > 1 and c % 2 == 0:
                        pe.wait_ge(s_ttr, first_unit(t - 2) + k + min(c // 2 + 1, k))
                    nc.tensor.matmul(banks[c][:, 0:b - a], zf[0:HD, :], keysT[0:HD, 0, a:b],
                                     start=True, stop=True).then_inc(s_fqk, 1)

            def mask_sums(t):
                k = len(units(t - 2)) if t > 1 else 0
                for c, (a, b) in enumerate(chunks(t)):
                    carried = min(b, P * t)
                    if carried > a:
                        if t > 1 and c % 2 == 0:
                            pe.wait_ge(s_ttr, first_unit(t - 2) + 2 * k + min(c // 2 + 1, k))
                        pe.wait_ge(s_relu, first_mask_chunk(t) + c + 1)
                        pe.wait_ge(s_big, t)
                        nc.tensor.matmul(banks[c][:, 0:carried - a], from_last[:, :], penalty[(t - 1) % 3][:, a:carried],
                                         start=True, stop=False)
                pe.wait_ge(s_msk, mask_steps(t))
                for c, (a, b) in enumerate(chunks(t)):
                    carried = min(b, P * t)
                    if carried > a:
                        last = nc.tensor.matmul(banks[c][:, 0:carried - a], until[:, :], penalty[t % 3][:, a:carried],
                                                start=False, stop=True)
                    if b > carried:
                        if carried <= a and t > 1:
                            pe.wait_ge(s_ttr, first_unit(t - 2) + 3 * k)
                        last = nc.tensor.matmul(banks[c][:, max(carried - a, 0):b - a], until[:, :], penalty[t % 3][:, max(a, carried):b],
                                                start=True, stop=True)
                    last.then_inc(s_fmm, 1)

            def scores(t, h, par, c):
                a, b = chunks(t)[c]
                k = len(units(t))
                pair = h // 2 if isinstance(h, int) else (h - par) // 2
                if c == 0:
                    pe.wait_ge(s_zq[par], 16 * (NP * t + pair + 1))
                if isinstance(h, int) and h == 0:
                    if t == 0:
                        pe.wait_ge(s_fcp, 2)
                    elif c % 2 == 0:
                        before = len(units(t - 1))
                        pe.wait_ge(s_ttr, first_unit(t) - before + min(c // 2 + 1, before))
                elif isinstance(h, int) and h == 2 and t + 2 < NT:
                    pe.wait_ge(s_relu, first_mask_chunk(t + 2) + c + 1)
                elif isinstance(h, int) and h == 3 and t + 2 < NT:
                    pe.wait_ge(s_fcp, first_mask_chunk(t + 2) + c + 1)
                elif c % 2 == 0:
                    pe.wait_ge(s_ttr, first_unit(t) + k * (h - 1) + c // 2 + 1)
                last = nc.tensor.matmul(banks[c][:, 0:b - a], zq[par], keysT[:, ds(pair, 1), a:b].rearrange("p a n -> p (a n)"),
                                        start=True, stop=True)
                if c % 2 or c == len(chunks(t)) - 1:
                    last.then_inc(s_qk, 1)

            def weigh(t, h, par, ahead=None):
                k = len(chunks(t))
                base = first_chunk(t) + k * h

                def turn(c):
                    a, b = chunks(t)[c]
                    if c == 0 and t > 0:
                        pe.wait_ge(s_yp, t)
                    pe.wait_ge(s_cp, base + c if c == 0 and k % 2 else base + c - 1) if k > 1 or t > 0 or not isinstance(h, int) or h > 0 else None
                    if c % 2 == 0:
                        pe.wait_ge(s_exp, first_unit(t) + len(units(t)) * h + c // 2 + 1)
                    for i in range((b - a) // P):
                        last = nc.tensor.transpose(banks[4 + c % 2][:, i * P:(i + 1) * P],
                                                   logit[par][:, a + i * P:a + (i + 1) * P], ident[:, :])
                    last.then_inc(s_tr, 1)

                def sum_values(c):
                    a, b = chunks(t)[c]
                    pe.wait_ge(s_cp, base + c + 1)
                    if c == 0 and not (t == 0 and isinstance(h, int) and h < 2):
                        pe.wait_ge(s_y, H * t + h - 1)
                    for i in range((b - a) // P):
                        j = a // P + i
                        last = nc.tensor.matmul(banks[6 + par][:, 0:HD], probsT[c % 2][:, i * P:(i + 1) * P],
                                                values[:, j, ds(h * HD, HD)], start=(j == 0), stop=(j == t))
                    last.then_inc(s_pvc, 1)

                k_ahead = len(chunks(ahead[0])) if ahead else 0
                for c in range(k):
                    turn(c)
                    if c < k_ahead:
                        scores(*ahead, c)
                    if c > 0:
                        sum_values(c - 1)
                for c in range(k, k_ahead):
                    scores(*ahead, c)
                sum_values(k - 1)

            def turn_outputs(t):
                pe.wait_ge(s_y, H * (t + 1))
                pe.wait_ge(s_cp, first_chunk(t + 1))
                for b in range(2):
                    for i in range(4):
                        k = 4 * b + i
                        last = nc.tensor.transpose(banks[4 + b][:, i * P:(i + 1) * P], y[:, k * P:(k + 1) * P], ident[:, :])
                    last.then_inc(s_yt, 1)

            def project(t):
                pe.wait_ge(s_yc, 2 * (t + 1))
                for k in range(NP):
                    last = nc.tensor.matmul(banks[4][:, 0:P], wpT[:, k, :], yT[:, k * P:(k + 1) * P],
                                            start=(k == 0), stop=(k == NP - 1))
                last.then_inc(s_pr, 1)

            for t in range(2):
                mask_scores(t)
                mask_sums(t)
            for h in range(2):
                scores(0, h, h, 0)
            for t in range(NT):
                if t > 0:
                    project(t - 1)
                if t + 2 < NT:
                    mask_scores(t + 2)
                weigh(t, 0, 0, (t, 2, 0))
                if t + 2 < NT:
                    mask_sums(t + 2)
                weigh(t, 1, 1, (t, 3, 1))
                with pe.Fori(1, NP - 1) as p:
                    weigh(t, 2 * p, 0, (t, 2 * p + 2, 0))
                    weigh(t, 2 * p + 1, 1, (t, 2 * p + 3, 1))
                weigh(t, H - 2, 0, (t + 1, 0, 0) if t + 1 < NT else None)
                weigh(t, H - 1, 1)
                if t + 1 < NT:
                    for c in range(len(chunks(t + 1))):
                        scores(t + 1, 1, 1, c)
                turn_outputs(t)
            project(NT - 1)

            def turn_tiles(src, first_bank, normed=None):
                for b in range(NC4):
                    if normed is not None:
                        pe.wait_ge(s_ln, normed + 4 * (b + 1))
                    for i in range(4):
                        last = nc.tensor.transpose(banks[first_bank + b][:, i * P:(i + 1) * P], src(4 * b + i), ident[:, :])
                    last.then_inc(s_tp, 1)

            pe.wait_ge(s_res, NT)
            turn_tiles(lambda t: resT[:, t * P:(t + 1) * P], 0)
            turn_tiles(lambda t: x1n[:, t, :], 4, normed=0)
            pe.wait_ge(s_te, 4)
            turn_tiles(lambda t: xaT[:, t * P:(t + 1) * P], 0, normed=NT)
            pe.wait_ge(s_cw, 16 * NW)
            pe.wait_ge(s_te, 8)
            for t in range(NT):
                last = nc.tensor.matmul(banks[4][:, t * NE:(t + 1) * NE], x1T[:, t * P:(t + 1) * P], wg, start=True, stop=True)
            last.then_inc(s_lg, 1)
            pe.wait_ge(s_te, 12)
            for c in range(NC4):
                nc.tensor.matmul(banks[c][:, :], wd, xsT[:, c * CH:(c + 1) * CH], start=True, stop=True).then_inc(s_dl, 1)
            pe.wait_ge(s_gt, 1)
            for c in range(NC4):
                nc.tensor.matmul(banks[4 + c][0:2 * NS, :], wbc, xsT[:, c * CH:(c + 1) * CH],
                                 start=True, stop=True).then_inc(s_dl, 1)

            pe.wait_ge(s_z, 2 * NC4)

            def hidden(e, par, c):
                x = x1T[:, c * CH:(c + 1) * CH]
                for f in range(4):
                    m = 4 * c + f
                    if m >= 3:
                        pe.wait_ge(s_gu, 4 * NC4 * e + m - 2)
                    elif not (isinstance(e, int) and e == 0):
                        pe.wait_ge(s_gu, 4 * NC4 * e)
                    cols = slice(f * P, (f + 1) * P)
                    nc.tensor.matmul(banks[2 * (m % 3)][:, :], w1b[par][:, cols], x, start=True, stop=True)
                    nc.tensor.matmul(banks[2 * (m % 3) + 1][:, :], w3b[par][:, cols], x, start=True, stop=True).then_inc(s_h, 1)

            def outputs(e, par, c):
                pe.wait_ge(s_gu, 4 * NC4 * e + 4 * (c + 1))
                if not (isinstance(e, int) and e == 0 and c < 2):
                    pe.wait_ge(s_ac, NC4 * e + c - 1)
                for i in range(4):
                    for f in range(4):
                        last = nc.tensor.matmul(banks[6 + c % 2][:, i * P:(i + 1) * P], guT[c % 2][:, f, i * P:(i + 1) * P],
                                                w2b[par][:, f, :], start=(f == 0), stop=(f == 3))
                last.then_inc(s_eo, 1)

            def expert(e, par):
                pe.wait_ge(s_w[par], 48 * (e // 2 + 1) if isinstance(e, int) else 24 * (e - par) + 48)
                for c in range(NC4):
                    hidden(e, par, c)
                    if c > 0:
                        outputs(e, par, c - 1)
                outputs(e, par, NC4 - 1)

            expert(0, 0)
            expert(1, 1)
            with pe.Fori(1, NE // 2) as p:
                expert(2 * p, 0)
                expert(2 * p + 1, 1)
            pe.wait_ge(s_ya, NS)
            pe.wait_ge(s_gu, 4 * NC4 * NE)
            turn_tiles(lambda t: ssmT[:, t * P:(t + 1) * P], 0)
            pe.wait_ge(s_te, 16)
            expert(NE, 0)

            pe.wait_ge(s_ac, NC4 * (NE + 1))
            turn_tiles(lambda t: dxT[:, t * P:(t + 1) * P], 4, normed=2 * NT)
            for i in range(4 * NC4):
                f, c = divmod(i, NC4)
                if i >= 4:
                    pe.wait_ge(s_ga, i - 3)
                else:
                    pe.wait_ge(s_te, 16 + c + 1)
                nc.tensor.matmul(banks[i % 4][:, :], w1m[:, f * P:(f + 1) * P], xsT[:, c * CH:(c + 1) * CH],
                                 start=True, stop=True).then_inc(s_ml, 1)
            pe.wait_ge(s_ga, 4 * NC4)
            for c in range(NC4):
                for i in range(4):
                    t = 4 * c + i
                    for f in range(4):
                        last = nc.tensor.matmul(banks[4 + c][:, i * P:(i + 1) * P], hidT[:, f, t * P:(t + 1) * P],
                                                w2m[:, f, :], start=(f == 0), stop=(f == 3))
                last.then_inc(s_m2, 1)

        @block.vector
        def _(dve):
            dve.wait_ge(s_x, 16)
            for t in range(NT):
                nc.vector.bn_stats(stats[:, t, :], xn[:, t, :]).then_inc(s_rs, 1)
            for t in range(NT):
                dve.wait_ge(s_rs, t + 1)
                nc.vector.bn_aggr(mv[:, t, :], stats[:, t, :]).then_inc(s_mv, 1)
            dve.wait_ge(s_mv, NT)
            nc.vector.tensor_scalar(sd.rearrange("p (t o) -> p t o", o=1), mv[:, :, 1:2], EPS, None, ALU.add).then_inc(s_mv, 1)
            dve.wait_ge(s_sd, 1)
            nc.vector.reciprocal(rstd, sd).then_inc(s_rs, 1)
            dve.wait_ge(s_rs, NT + 1)
            for t in range(NT):
                nc.vector.tensor_scalar(xn[:, t, :], xn[:, t, :], mv[:, t, 0:1], rstd[:, t:t + 1],
                                        ALU.subtract, ALU.mult).then_inc(s_xn, 1)
            dve.wait_ge(s_b, 48)
            nc.vector.tensor_scalar(bqn, bqk[:, 0:NP], -0.125, None, ALU.mult).then_inc(s_bq, 1)
            dve.wait_ge(s_wp, 48)
            nc.vector.tensor_scalar(wneg, wsT, 0.0, None, ALU.is_lt).then_inc(s_bq, 1)
            dve.wait_ge(s_bq, 2)
            nc.vector.scalar_tensor_tensor(out=wsT, in0=wsT, scalar=0.0, in1=wneg, op0=ALU.is_gt, op1=ALU.subtract).then_inc(s_ws, 1)
            for i, n in enumerate(by_dve):
                kind, t, c = prods[n]
                dve.wait_ge(s_proj, n + 1)
                cols = slice(c * CH, (c + 1) * CH)
                if kind == "v":
                    nc.vector.tensor_tensor(values[:, t, cols], banks[n % 8][:, :], bv_all[:, cols], ALU.add).then_inc(s_pv_ev, 1)
                else:
                    nc.vector.scalar_tensor_tensor(out=resT[:, cols], in0=resT[:, cols], scalar=bp, in1=banks[n % 8][:, :],
                                                   op0=ALU.add, op1=ALU.add).then_inc(s_pv_ev, 1)
            dve.wait_ge(s_pv_ev, len(by_dve))
            nc.vector.memset(mins[:, 0:4], 0.0).then_inc(s_stageA, 1)
            dve.wait_ge(s_pa, len(by_act))
            nc.vector.memset(mins[:, 4:8], 0.0).then_inc(s_stageA, 1)
            for i in range(2):
                dve.wait_ge(s_qd[i], 16 * (NP * NC4 // 2))

            def logits(t, h, par, u):
                k = len(units(t))
                a, b = units(t)[u]
                g = len(chunks(t))
                if not (isinstance(h, int) and h < 2):
                    dve.wait_ge(s_tr, first_chunk(t) + g * (h - 2) + min(2 * u + 2, g))
                elif t > 0:
                    g = len(chunks(t - 1))
                    dve.wait_ge(s_tr, first_chunk(t) - g * (2 - h) + min(2 * u + 2, g))
                dve.wait_ge(s_qk, first_unit(t) + k * h + u + 1)
                nc.vector.tensor_tensor_reduce(logit[par][:, a:b], wide[:, a:b], penalty[t % 3][:, a:b],
                                               1.0, 3e38, ALU.add, ALU.min,
                                               mins[:, 4 * par + u:4 * par + u + 1]).then_inc(s_ttr, 1)

            def least(t, h, par):
                k = len(units(t))
                dve.wait_ge(s_ttr, first_unit(t) + k * (h + 1))
                nc.vector.tensor_reduce(bias[:, par:par + 1], mins[:, 4 * par:4 * par + k], AX_X, ALU.min).then_inc(s_mb, 1)

            def total(t, h, par):
                k = len(units(t))
                dve.wait_ge(s_exp, first_unit(t) + k * (h + 1))
                nc.vector.tensor_reduce(sums[:, par:par + 1], part_sums[:, 2 * par:2 * par + k], AX_X, ALU.add).then_inc(s_sum, 1)

            def recip(t, h, par):
                dve.wait_ge(s_sum, H * t + h + 1)
                if not (t == 0 and isinstance(h, int) and h < 2):
                    dve.wait_ge(s_y, H * t + h - 1)
                nc.vector.reciprocal(rsum[:, par:par + 1], sums[:, par:par + 1]).then_inc(s_rec, 1)

            PER = 3
            AT_FIRST = 1
            AT_HALF = 6
            AT_LAST = 2
            FIN = 5
            STEP_SUM = AT_FIRST + PER * BITS + AT_HALF + AT_LAST + FIN

            def search_base(t):
                return STEP_SUM * sum(searched(u) for u in range(t))

            def keep(t):
                return keep3[:, 0:1] if t == first_searched else float(BUDGET)

            def search_first(t):
                nc.vector.memset(cand, float(1 << (HI_BITS - 1))).then_inc(s_srch, 1)
                dve.wait_ge(s_srch, search_base(t) + AT_FIRST)
                dve.wait_ge(s_half, t - first_searched + 1)

            def bit(i):
                return float(1 << ((HI_BITS if i < HI_BITS else BITS) - 1 - i))

            def step_base(t, i):
                return search_base(t) + AT_FIRST + PER * i + (AT_HALF if i >= HI_BITS else 0)

            def step_count(t, i):
                n = P * (t + 1)
                dve.wait_ge(s_srch, step_base(t, i))
                nc.vector.tensor_scalar(flags[:, 0:n], half[:, 0:n], cand, None, ALU.is_lt, ALU.add, accum_out=count).then_inc(s_srch, 1)

            def step_compare(t, i):
                dve.wait_ge(s_srch, step_base(t, i) + 1)
                nc.vector.tensor_scalar(turn_up, count, keep(t), -0.5, ALU.is_lt, ALU.add).then_inc(s_srch, 1)

            def step_move(t, i):
                dve.wait_ge(s_srch, step_base(t, i) + 2)
                nc.vector.scalar_tensor_tensor(out=cand, in0=turn_up, scalar=bit(i), in1=cand, op0=ALU.mult, op1=ALU.add).then_inc(s_srch, 1)

            def search_half(t):
                n = P * (t + 1)
                at = search_base(t) + AT_FIRST + PER * HI_BITS
                dve.wait_ge(s_srch, at)
                nc.vector.tensor_scalar(upper, cand, -0.5, None, ALU.add).then_inc(s_srch, 1)
                dve.wait_ge(s_srch, at + 1)
                nc.vector.tensor_copy(low.bitcast(U16)[:, 1:2], upper).then_inc(s_srch, 1)
                nc.vector.tensor_scalar(flags[:, 0:n], half[:, 0:n], upper, 65535.0, ALU.is_gt, ALU.mult).then_inc(s_srch, 1)
                dve.wait_ge(s_srch, at + 3)
                nc.vector.scalar_tensor_tensor(out=half[:, 0:n], in0=half[:, 0:n], scalar=upper, in1=halves(t)[0],
                                               op0=ALU.is_equal, op1=ALU.mult).then_inc(s_srch, 1)
                dve.wait_ge(s_srch, at + 4)
                nc.vector.tensor_tensor(half[:, 0:n], half[:, 0:n], flags[:, 0:n], ALU.max).then_inc(s_srch, 1)
                nc.vector.memset(cand, float(1 << (LO_BITS - 1))).then_inc(s_srch, 1)
                dve.wait_ge(s_srch, at + 6)

            def search_last(t):
                at = search_base(t) + AT_FIRST + PER * BITS + AT_HALF
                dve.wait_ge(s_srch, at)
                nc.vector.tensor_scalar(upper, cand, -0.5, None, ALU.add).then_inc(s_srch, 1)
                dve.wait_ge(s_srch, at + 1)
                nc.vector.tensor_copy(low.bitcast(U16)[:, 0:1], upper).then_inc(s_srch, 1)
                dve.wait_ge(s_srch, at + 2)
                nc.vector.memset(need, 0.0).then_inc(s_low, 1)

            def rank_equals(t):
                n = P * (t + 1)
                at = search_base(t + 1) - FIN
                dve.wait_ge(s_side, t - first_searched + 1)
                nc.vector.tensor_scalar(rank[:, 0:n], side[:, 0:n], 0.0, None, ALU.is_equal).then_inc(s_srch, 1)
                dve.wait_ge(s_srch, at + 1)
                nc.vector.tensor_tensor_scan(rank[:, 0:n], rank[:, 0:n], rank[:, 0:n], 0.0, ALU.add, ALU.max).then_inc(s_srch, 1)
                dve.wait_ge(s_srch, at + 2)

            def prune(t):
                n = P * (t + 1)
                at = search_base(t + 1) - FIN + 2
                nc.vector.tensor_tensor(need, rank[:, n - 1:n], balance, ALU.subtract).then_inc(s_srch, 1)
                dve.wait_ge(s_srch, at + 1)
                nc.vector.tensor_scalar(need, need, 0.5, keep3[:, 1 + t:2 + t], ALU.mult, ALU.add).then_inc(s_srch, 1)
                dve.wait_ge(s_srch, at + 2)
                nc.vector.scalar_tensor_tensor(out=rank[:, 0:n], in0=rank[:, 0:n], scalar=need, in1=side[:, 0:n],
                                               op0=ALU.is_gt, op1=ALU.subtract).then_inc(s_srch, 1)
                dve.wait_ge(s_srch, at + 3)
                pen = penalty[t % 3][:, 0:n]
                if t + 1 < NT:
                    dve.wait_ge(s_fmm, first_mask_chunk(t + 2))
                nc.vector.scalar_tensor_tensor(out=pen, in0=rank[:, 0:n], scalar=BIG, in1=pen, op0=ALU.mult, op1=ALU.max).then_inc(s_fin, 1)

            for t in range(NT):
                ends = t + 1 < NT and searched(t + 1)
                begins = t + 2 < NT and searched(t + 2)

                def slot(h, par, steps=(), t=t):
                    before = (t, h - 2) if h >= 2 else (t - 1, H + h - 2)
                    first, second, third = list(steps) + [None] * (3 - len(steps))
                    if first:
                        step_count(*first)
                    if before[0] >= 0:
                        total(*before, par)
                    if first:
                        step_compare(*first)
                    if before[0] >= 0:
                        recip(*before, par)
                    if first:
                        step_move(*first)
                    logits(t, h, par, 0)
                    if third:
                        step_count(*second)
                        step_compare(*second)
                        step_move(*second)
                    if third or second:
                        step_count(*(third or second))
                    if len(units(t)) > 1:
                        logits(t, h, par, 1)
                    if third or second:
                        step_compare(*(third or second))
                    least(t, h, par)
                    if third or second:
                        step_move(*(third or second))

                dve.wait_ge(s_big, t + 1)
                if searched(t):
                    dve.wait_ge(s_dg, t - first_searched + 1)
                slot(0, 0, [(t + 1, i) for i in range(BITS - 6, BITS - 3)] if ends else ())
                slot(1, 1, [(t + 1, i) for i in range(BITS - 3, BITS)] if ends else ())
                if ends:
                    search_last(t + 1)
                if t > 0:
                    dve.wait_ge(s_yp, t)
                    cols = slice((t - 1) * P, t * P)
                    nc.vector.tensor_tensor(resT[:, cols], resT[:, cols], yP, ALU.add).then_inc(s_res, 1)
                slot(2, 0)
                if ends:
                    rank_equals(t + 1)
                    prune(t + 1)
                slot(3, 1)
                if begins:
                    search_first(t + 2)
                step = 0
                for h in range(4, H):
                    if h == 10:
                        if begins:
                            search_half(t + 2)
                        slot(h, 0)
                        continue
                    n = 3 if h % 2 == 0 and h < 10 else 2
                    slot(h, h % 2, [(t + 2, step + i) for i in range(n)] if begins else ())
                    step += n
            for h in (H - 2, H - 1):
                total(NT - 1, h, h % 2)
                recip(NT - 1, h, h % 2)
            dve.wait_ge(s_yp, NT)
            cols = slice((NT - 1) * P, NT * P)
            nc.vector.tensor_tensor(resT[:, cols], resT[:, cols], yP, ALU.add).then_inc(s_res, 1)

            def norm_stats(n, src, taken=None):
                for t in range(NT):
                    if taken is not None and t % 4 == 0:
                        dve.wait_ge(s_te, taken + t // 4 + 1)
                    nc.vector.bn_stats(st2[:, t, :], src(t)).then_inc(s_stat, 1)

            def norm_variance(n):
                at = STAT * n
                for t in range(NT):
                    dve.wait_ge(s_stat, at + t + 1)
                    nc.vector.bn_aggr(mv2[:, t, :], st2[:, t, :]).then_inc(s_stat, 1)
                dve.wait_ge(s_stat, at + 2 * NT)
                nc.vector.tensor_scalar(sd2.rearrange("p (t o) -> p t o", o=1), mv2[:, :, 1:2], EPS, None, ALU.add).then_inc(s_stat, 1)

            def norm_apply(n, src, dst):
                dve.wait_ge(s_sq, n + 1)
                nc.vector.reciprocal(rs2, sd2).then_inc(s_stat, 1)
                dve.wait_ge(s_stat, STAT * (n + 1))
                for t in range(NT):
                    nc.vector.tensor_scalar(dst(t), src(t), mv2[:, t, 0:1], rs2[:, t:t + 1],
                                            ALU.subtract, ALU.mult).then_inc(s_ln, 1)

            def layer_norm(n, src, dst, taken=None):
                norm_stats(n, src, taken)
                norm_variance(n)
                norm_apply(n, src, dst)

            layer_norm(0, lambda t: x1[:, t, :], lambda t: x1n[:, t, :], taken=0)
            dve.wait_ge(s_ln, NT)
            layer_norm(1, lambda t: x1n[:, t, :], lambda t: xaT[:, t * P:(t + 1) * P])
            dve.wait_ge(s_cw, 16 * NW)
            nc.vector.tensor_tensor(acc, x1, b2all.rearrange("p (o c) -> p o c", o=1).to_broadcast([P, NT, C]), ALU.add).then_inc(s_ac0, 1)

            dve.wait_ge(s_lg, 1)
            gates = [0]

            def gstep(ins):
                gates[0] += 1
                ins.then_inc(s_gt, 1)
                dve.wait_ge(s_gt, gates[0])

            logits8 = banks[4][:, 0:NT * NE].rearrange("p (t e) -> p t e", t=NT)
            gstep(nc.vector.tensor_copy(prob, logits8))
            nc.vector.tensor_reduce(top, prob, AX_X, ALU.max).then_inc(s_gm, 1)
            dve.wait_ge(s_gm, 1)
            gstep(nc.vector.tensor_tensor(prob, prob, top.to_broadcast([P, NT, NE]), ALU.subtract))
            dve.wait_ge(s_ge, 1)
            gstep(nc.vector.tensor_reduce(top, prob, AX_X, ALU.add))
            gstep(nc.vector.reciprocal(top, top))
            gstep(nc.vector.tensor_tensor(prob, prob, top.to_broadcast([P, NT, NE]), ALU.mult))
            for e in range(NE):
                mine = prob[:, :, e:e + 1]
                gstep(nc.vector.tensor_tensor(cmp[:, :, e:NE], prob[:, :, e:NE], mine.to_broadcast([P, NT, NE - e]), ALU.is_gt))
                if e:
                    gstep(nc.vector.tensor_tensor(cmp[:, :, 0:e], prob[:, :, 0:e], mine.to_broadcast([P, NT, e]), ALU.is_ge))
                gstep(nc.vector.tensor_reduce(rnk[:, :, e:e + 1], cmp, AX_X, ALU.add))
            gstep(nc.vector.tensor_scalar(keptw, rnk, 2.0, 0.5, ALU.is_lt, ALU.mult))
            gstep(nc.vector.memset(gate, 0.5 / 8))
            gstep(nc.vector.tensor_tensor(gate[:, :, 0:NE], keptw, prob, ALU.mult))

            def gated(e, c):
                if not (isinstance(e, int) and e == 0 and c < 2):
                    dve.wait_ge(s_eo, NC4 * e + c - 1)
                for f in range(4):
                    m = 4 * c + f
                    dve.wait_ge(s_si, 4 * NC4 * e + m + 1)
                    nc.vector.tensor_tensor(guT[c % 2][:, f, :], silu[m % 3], banks[2 * (m % 3) + 1][:, :], ALU.mult).then_inc(s_gu, 1)

            gated(0, 0)
            dve.wait_ge(s_sp, 4)
            nc.vector.scalar_tensor_tensor(out=delta, in0=delta, scalar=0.0, in1=absz, op0=ALU.max, op1=ALU.add).then_inc(s_dx, 1)
            dve.wait_ge(s_dx, 1)
            nc.vector.tensor_tensor(dxT, delta, xsT, ALU.mult).then_inc(s_dx, 1)
            nc.vector.tensor_scalar(rate, rate, -1.0, None, ALU.mult).then_inc(s_dx, 1)
            gated(0, 1)
            nc.vector.scalar_tensor_tensor(out=ssmT, in0=xsT, scalar=dskip, in1=x1T, op0=ALU.mult, op1=ALU.add).then_inc(s_yi, 1)
            dve.wait_ge(s_yi, 1)

            def scan(n, j, k):
                if k == 0:
                    dve.wait_ge(s_an, n + 1)
                    dve.wait_ge(s_bx, n + 1)
                    nc.vector.tensor_tensor_scan(state[j], decay[j], state[j], 0.0, ALU.mult, ALU.add).then_inc(s_sc, 1)
                elif k == 1:
                    dve.wait_ge(s_sc, n + 1)
                    dve.wait_ge(s_cb[j], 16 * (n // 2 + 1) if isinstance(n, int) else 8 * (n - j) + 16)
                    nc.vector.tensor_tensor(state[j], state[j], rowC[j], ALU.mult).then_inc(s_hc, 1)
                else:
                    dve.wait_ge(s_hc, n + 1)
                    dve.wait_ge(s_ya, n)
                    nc.vector.tensor_tensor(ssmT, ssmT, state[j], ALU.add).then_inc(s_ya, 1)

            def add_up(e, c):
                dve.wait_ge(s_eo, NC4 * e + c + 1)
                if not (isinstance(e, int) and e == 0):
                    dve.wait_ge(s_ac, NC4 * (e - 1) + c + 1)
                for i in range(4):
                    t = 4 * c + i
                    last = nc.vector.scalar_tensor_tensor(
                        out=acc[:, t, :], in0=banks[6 + c % 2][:, i * P:(i + 1) * P],
                        scalar=gate[:, t, ds(e, 1)], in1=acc[:, t, :], op0=ALU.mult, op1=ALU.add)
                last.then_inc(s_ac, 1)

            def expert(e, scans):
                for c in range(NC4):
                    if not (isinstance(e, int) and e == 0 and c < 2):
                        gated(e, c)
                    if c > 0:
                        add_up(e, c - 1)
                    for n, j, k in scans[c]:
                        scan(n, j, k)
                add_up(e, NC4 - 1)

            def steps(n):
                return [[(n, 0, 0), (n, 0, 1)], [(n + 1, 1, 0)], [(n, 0, 2), (n + 1, 1, 1)], [(n + 1, 1, 2)]]

            dve.wait_ge(s_ac0, 1)
            expert(0, [[], [(0, 0, 0), (0, 0, 1)], [(1, 1, 0), (0, 0, 2)], [(1, 1, 1), (1, 1, 2)]])
            expert(1, steps(2))
            with dve.Fori(1, NE // 2) as p:
                expert(2 * p, steps(4 * p))
                expert(2 * p + 1, steps(4 * p + 2))
            dve.wait_ge(s_te, 16)
            gated(NE, 0)
            norm_stats(2, lambda t: x1n[:, t, :])
            gated(NE, 1)
            add_up(NE, 0)
            norm_variance(2)
            gated(NE, 2)
            add_up(NE, 1)
            norm_apply(2, lambda t: x1n[:, t, :], lambda t: dxT[:, t * P:(t + 1) * P])
            gated(NE, 3)
            add_up(NE, 2)
            add_up(NE, 3)

            dve.wait_ge(s_ac, NC4 * (NE + 1))
            nc.vector.tensor_tensor(acc, acc, x1n, ALU.add).then_inc(s_ac0, 1)
            dve.wait_ge(s_ac0, 2)
            for c in range(NC4):
                dve.wait_ge(s_m2, c + 1)
                part4 = acc[:, 4 * c:4 * c + 4, :]
                nc.vector.tensor_tensor(part4, part4, banks[4 + c][:, :].rearrange("p (t c) -> p t c", t=4), ALU.add).then_inc(s_o, 1)


def constants():
    keep = np.full((P, 1 + NT), BUDGET, np.float32)
    t3 = BUDGET // P
    keep[:, 0] = np.minimum(BUDGET, t3 * P + np.arange(P) + 1)
    for t in range(NT):
        keep[:, 1 + t] = (keep[:, 0] if t == t3 else BUDGET) - P * (t + 1) / 2
    return {"c_ident": np.eye(P, dtype=np.float32), "c_until": np.triu(np.ones((P, P), np.float32)),
            "c_last": np.eye(P, dtype=np.float32)[:, P - 1:] * np.ones((1, P), np.float32), "c_keep": keep}


def layout(x):
    c = np.ascontiguousarray
    g = lambda n: np.asarray(x[n])
    X = g("L0_attn_x")[0]
    a = {"x": X, "xT": X.T, "W_attnT": g("L0_attn_W_attn").T, "b_qkT": g("L0_attn_b_attn")[:2 * H * HD].reshape(-1, P).T,
         "b_v": g("L0_attn_b_attn")[None, 2 * H * HD:], "W_projT": g("L0_attn_W_proj").T, "b_proj": g("L0_attn_b_proj")[:, None],
         "W_signT": g("L0_ffn_weight").T}
    col = lambda n: g(n)[:, None]
    a.update({"W1T": g("L1_attn_W1").T, "W2T": g("L1_attn_W2").T, "WdT": g("L1_attn_Wd").T, "WbcT": g("L1_attn_Wbc").T,
              "gate_WT": g("L1_ffn_gate_W").T, "b2": g("L1_attn_b2")[None], "ln1_g": col("L1_attn_ln1_g"),
              "ln1_b": col("L1_attn_ln1_b"), "bd": col("L1_attn_bd"), "D": col("L1_attn_D"), "ln2_g": col("L1_attn_ln2_g"),
              "ln2_b": col("L1_attn_ln2_b"), "b1T": g("L1_attn_b1").reshape(4, P).T, "bbc": col("L1_attn_bbc"),
              "A_log": g("L1_attn_A_log")})
    ns, d, fs = g("L1_ffn_w1_s").shape
    beside = lambda w: w.transpose(1, 0, 2).reshape(1, d, ns * fs)
    a["w1"] = np.concatenate([g("L1_ffn_w1_e"), beside(g("L1_ffn_w1_s"))])
    a["w3"] = np.concatenate([g("L1_ffn_w3_e"), beside(g("L1_ffn_w3_s"))])
    a["w2"] = np.concatenate([g("L1_ffn_w2_e"), g("L1_ffn_w2_s").reshape(1, ns * fs, d)])
    a.update(constants())
    return {k: c(v) for k, v in a.items()}


def kernel(**inputs):
    import concourse.bacc as bacc
    from concourse.bass_utils import run_bass_kernel_spmd

    arrays = layout(inputs)
    nc = bacc.Bacc("TRN2", target_bir_lowering=False, num_devices=1)
    aps = {n: nc.dram_tensor(n, a.shape, mybir.dt.from_np(a.dtype), kind="ExternalInput").ap() for n, a in arrays.items()}
    out = nc.dram_tensor("out", (1, T, C), F32, kind="ExternalOutput").ap()
    build(nc, aps, out)
    return run_bass_kernel_spmd(nc, [arrays], core_ids=[0]).results[0]["out"]
```
